# Optimizing a Trainium2 kernel written in Bass

```python
import numpy as np
import jax
import jax.numpy as jnp

def _softmax(x, axis=-1):
    return jax.nn.softmax(x, axis=axis)

def _gelu(x):
    return jax.nn.gelu(x, approximate=True)

def _silu(x):
    return jax.nn.silu(x)

def _sigmoid(x):
    return jax.nn.sigmoid(x)

def _layernorm(x, axis=-1, eps=1e-05):
    m = jnp.mean(x, axis=axis, keepdims=True)
    v = jnp.var(x, axis=axis, keepdims=True)
    return (x - m) / jnp.sqrt(v + eps)

def _scatter_add(tgt, idx, src, axis=0):
    return tgt.at[idx].add(src)

def _segment_sum(src, seg, n):
    return jax.ops.segment_sum(src, seg, n)
kernel_name = 'mk_early_fusion_d1_tok_img1024_r4_9099bf'

def setup_inputs(seed: int=0):
    np.random.seed(seed)
    _w = jnp.asarray

    def _rec_inputs():
        import jax
        import jax.numpy as jnp
        _rk = jax.random.key(seed)
        x = 7.22013e-05 + 1.00017 * jax.random.normal(jax.random.fold_in(_rk, 1), (16, 64, 256, 4), jnp.float32)
        txt = -1.32754e-10 + 0.999995 * jax.random.normal(jax.random.fold_in(_rk, 2), (16, 32, 256), jnp.float32)
        return (x, txt)
    x, txt = _rec_inputs()

    def _L0_tok_setup():
        import jax, jax.numpy as jnp
        import numpy as np
        B, F, L, H, D = (8, 64, 256, 4, 64)
        MODEL = H * F
        WIN = 128

        def _local_mask():
            m = np.ones((L, L), dtype=bool)
            m = np.tril(m, WIN - 1)
            m = np.triu(m, -(WIN - 1))
            return jnp.asarray(m)

        def _flatten(y):
            n = y.shape[0]
            return y.transpose(0, 2, 3, 1).reshape(n, L, -1)
        key = jax.random.key(seed)
        ks = jax.random.split(key, 12)
        s = lambda n: 1.0 / np.sqrt(n)
        xav = np.sqrt(6.0 / (L + L))
        return {'x': jax.random.normal(ks[0], (B, F, L, H), jnp.float32), 'Wq_w': jax.random.normal(ks[1], (D, F), jnp.float32) * s(F), 'Wq_b': jnp.zeros((D,), jnp.float32), 'Wk_w': jax.random.normal(ks[2], (D, F), jnp.float32) * s(F), 'Wk_b': jnp.zeros((D,), jnp.float32), 'Wv_w': jax.random.normal(ks[3], (D, F), jnp.float32) * s(F), 'Wv_b': jnp.zeros((D,), jnp.float32), 'w_bias': jax.random.uniform(ks[4], (L, L), jnp.float32, -xav, xav), 'out_w': jax.random.normal(ks[5], (H * D, MODEL), jnp.float32) * s(H * D), 'out_b': jnp.zeros((MODEL,), jnp.float32), 'ln_g': jnp.ones((MODEL,), jnp.float32), 'ln_b': jnp.zeros((MODEL,), jnp.float32), 'local_mask': _local_mask()}
    _L0_tok_all = _L0_tok_setup()
    _L0_tok_in = {k: v for k, v in _L0_tok_all.items() if k in ('Wq_w', 'Wq_b', 'Wk_w', 'Wk_b', 'Wv_w', 'Wv_b', 'w_bias', 'out_w', 'out_b', 'ln_g', 'ln_b', 'local_mask')}
    del _L0_tok_all

    def _L0_attn_setup():
        import jax, jax.numpy as jnp
        import numpy as np
        import math
        DIM = 256
        NUM_HEADS = 16
        HEAD_DIM = DIM // NUM_HEADS
        B, S = (2, 512)
        key = jax.random.key(seed)
        ks = jax.random.split(key, 9)
        sc = 0.02
        return {'x': jax.random.normal(ks[0], (B, S, DIM), jnp.float32), 'Wq': jax.random.normal(ks[1], (DIM, DIM), jnp.float32) * sc, 'bq': jax.random.normal(ks[2], (DIM,), jnp.float32) * sc, 'Wk': jax.random.normal(ks[3], (DIM, DIM), jnp.float32) * sc, 'bk': jax.random.normal(ks[4], (DIM,), jnp.float32) * sc, 'Wv': jax.random.normal(ks[5], (DIM, DIM), jnp.float32) * sc, 'bv': jax.random.normal(ks[6], (DIM,), jnp.float32) * sc, 'Wo': jax.random.normal(ks[7], (DIM, DIM), jnp.float32) * sc, 'bo': jax.random.normal(ks[8], (DIM,), jnp.float32) * sc}
    _L0_attn_all = _L0_attn_setup()
    _L0_attn_in = {k: v for k, v in _L0_attn_all.items() if k in ('Wq', 'bq', 'Wk', 'bk', 'Wv', 'bv', 'Wo', 'bo')}
    del _L0_attn_all

    def _L0_ffn_setup():
        import jax, jax.numpy as jnp
        import numpy as np
        D_MODEL = 256
        EXPANSION = 4
        D_HIDDEN = D_MODEL * EXPANSION
        NUM_STAGES = int(np.log2(D_HIDDEN))

        def butterfly(y, weights, dim):
            lead = y.shape[:-1]
            for stage in range(weights.shape[0]):
                s = 2 ** stage
                nb = dim // (2 * s)
                yr = y.reshape(*lead, nb, 2, s)
                a = yr[..., 0, :]
                b = yr[..., 1, :]
                w = weights[stage].reshape(nb, s, 2, 2)
                na = w[..., 0, 0] * a + w[..., 0, 1] * b
                nb2 = w[..., 1, 0] * a + w[..., 1, 1] * b
                y = jnp.stack([na, nb2], axis=-2).reshape(*lead, dim)
            return y
        key = jax.random.key(seed)
        ks = jax.random.split(key, 6)
        B, S = (4, 512)
        x = jax.random.normal(ks[0], (B, S, D_MODEL), jnp.float32)
        W_exp = jax.random.normal(ks[1], (D_MODEL, D_HIDDEN), jnp.float32) * 0.02
        b_exp = jnp.zeros((D_HIDDEN,), jnp.float32)
        up_weights = jax.random.normal(ks[2], (NUM_STAGES, D_HIDDEN // 2, 2, 2), jnp.float32) * 0.02
        up_bias = jnp.zeros((D_HIDDEN,), jnp.float32)
        down_weights = jax.random.normal(ks[3], (NUM_STAGES, D_HIDDEN // 2, 2, 2), jnp.float32) * 0.02
        W_con = jax.random.normal(ks[4], (D_HIDDEN, D_MODEL), jnp.float32) * 0.02
        b_con = jnp.zeros((D_MODEL,), jnp.float32)
        down_bias = jnp.zeros((D_MODEL,), jnp.float32)
        return dict(x=x, W_exp=W_exp, b_exp=b_exp, up_weights=up_weights, up_bias=up_bias, down_weights=down_weights, W_con=W_con, b_con=b_con, down_bias=down_bias)
    _L0_ffn_all = _L0_ffn_setup()
    _L0_ffn_in = {k: v for k, v in _L0_ffn_all.items() if k in ('W_exp', 'b_exp', 'up_weights', 'up_bias', 'down_weights', 'W_con', 'b_con', 'down_bias')}
    del _L0_ffn_all
    return {'x': x, 'txt': txt, 'L0_tok_Wq_w': _L0_tok_in['Wq_w'], 'L0_tok_Wq_b': _L0_tok_in['Wq_b'], 'L0_tok_Wk_w': _L0_tok_in['Wk_w'], 'L0_tok_Wk_b': _L0_tok_in['Wk_b'], 'L0_tok_Wv_w': _L0_tok_in['Wv_w'], 'L0_tok_Wv_b': _L0_tok_in['Wv_b'], 'L0_tok_w_bias': _L0_tok_in['w_bias'], 'L0_tok_out_w': _L0_tok_in['out_w'], 'L0_tok_out_b': _L0_tok_in['out_b'], 'L0_tok_ln_g': _L0_tok_in['ln_g'], 'L0_tok_ln_b': _L0_tok_in['ln_b'], 'L0_tok_local_mask': _L0_tok_in['local_mask'], 'L0_attn_Wq': _L0_attn_in['Wq'], 'L0_attn_bq': _L0_attn_in['bq'], 'L0_attn_Wk': _L0_attn_in['Wk'], 'L0_attn_bk': _L0_attn_in['bk'], 'L0_attn_Wv': _L0_attn_in['Wv'], 'L0_attn_bv': _L0_attn_in['bv'], 'L0_attn_Wo': _L0_attn_in['Wo'], 'L0_attn_bo': _L0_attn_in['bo'], 'L0_ffn_W_exp': _L0_ffn_in['W_exp'], 'L0_ffn_b_exp': _L0_ffn_in['b_exp'], 'L0_ffn_up_weights': _L0_ffn_in['up_weights'], 'L0_ffn_up_bias': _L0_ffn_in['up_bias'], 'L0_ffn_down_weights': _L0_ffn_in['down_weights'], 'L0_ffn_W_con': _L0_ffn_in['W_con'], 'L0_ffn_b_con': _L0_ffn_in['b_con'], 'L0_ffn_down_bias': _L0_ffn_in['down_bias']}

def reference(x, txt, L0_tok_Wq_w, L0_tok_Wq_b, L0_tok_Wk_w, L0_tok_Wk_b, L0_tok_Wv_w, L0_tok_Wv_b, L0_tok_w_bias, L0_tok_out_w, L0_tok_out_b, L0_tok_ln_g, L0_tok_ln_b, L0_tok_local_mask, L0_attn_Wq, L0_attn_bq, L0_attn_Wk, L0_attn_bk, L0_attn_Wv, L0_attn_bv, L0_attn_Wo, L0_attn_bo, L0_ffn_W_exp, L0_ffn_b_exp, L0_ffn_up_weights, L0_ffn_up_bias, L0_ffn_down_weights, L0_ffn_W_con, L0_ffn_b_con, L0_ffn_down_bias):
    import jax
    import jax.numpy as jnp

    def _L0_tok_ref(x, Wq_w, Wq_b, Wk_w, Wk_b, Wv_w, Wv_b, w_bias, out_w, out_b, ln_g, ln_b, local_mask):
        import jax, jax.numpy as jnp
        import numpy as np
        B, F, L, H, D = (8, 64, 256, 4, 64)
        MODEL = H * F
        WIN = 128

        def _local_mask():
            m = np.ones((L, L), dtype=bool)
            m = np.tril(m, WIN - 1)
            m = np.triu(m, -(WIN - 1))
            return jnp.asarray(m)

        def _flatten(y):
            n = y.shape[0]
            return y.transpose(0, 2, 3, 1).reshape(n, L, -1)

        def proj(w, b):
            y = jnp.einsum('nclh,dc->ndlh', x, w) + b[None, :, None, None]
            return _flatten(y)
        q = proj(Wq_w, Wq_b)
        k = proj(Wk_w, Wk_b)
        v = proj(Wv_w, Wv_b)
        wb = w_bias * local_mask.astype(w_bias.dtype)
        ew = jnp.exp(wb)
        ek = jnp.exp(k)
        num = jnp.einsum('ts,nsd->ntd', ew, ek * v)
        den = jnp.einsum('ts,nsd->ntd', ew, ek)
        y = jax.nn.sigmoid(q) * num / den
        h = y @ out_w + out_b + _flatten(x)
        mu = jnp.mean(h, axis=-1, keepdims=True)
        var = jnp.mean(jnp.square(h - mu), axis=-1, keepdims=True)
        return (h - mu) * jax.lax.rsqrt(var + 1e-05) * ln_g + ln_b

    def _L0_attn_ref(x, Wq, bq, Wk, bk, Wv, bv, Wo, bo):
        import jax, jax.numpy as jnp
        import numpy as np
        import math
        DIM = 256
        NUM_HEADS = 16
        HEAD_DIM = DIM // NUM_HEADS
        B, S = (2, 512)
        b, s, d = x.shape
        h, hd = (NUM_HEADS, HEAD_DIM)

        def split_heads(t):
            return t.reshape(b, s, h, hd).transpose(0, 2, 1, 3)
        q = split_heads(x @ Wq + bq)
        k = split_heads(x @ Wk + bk)
        v = split_heads(x @ Wv + bv)
        scores = jnp.einsum('bhqd,bhkd->bhqk', q, k) / math.sqrt(hd)
        causal = jnp.tril(jnp.ones((s, s), dtype=bool))
        scores = jnp.where(causal[None, None], scores, jnp.asarray(-10000.0, scores.dtype))
        probs = jax.nn.softmax(scores, axis=-1)
        ctx = jnp.einsum('bhqk,bhkd->bhqd', probs, v)
        ctx = ctx.transpose(0, 2, 1, 3).reshape(b, s, d)
        return ctx @ Wo + bo

    def _L0_ffn_ref(x, W_exp, b_exp, up_weights, up_bias, down_weights, W_con, b_con, down_bias):
        import jax, jax.numpy as jnp
        import numpy as np
        D_MODEL = 256
        EXPANSION = 4
        D_HIDDEN = D_MODEL * EXPANSION
        NUM_STAGES = int(np.log2(D_HIDDEN))

        def butterfly(y, weights, dim):
            lead = y.shape[:-1]
            for stage in range(weights.shape[0]):
                s = 2 ** stage
                nb = dim // (2 * s)
                yr = y.reshape(*lead, nb, 2, s)
                a = yr[..., 0, :]
                b = yr[..., 1, :]
                w = weights[stage].reshape(nb, s, 2, 2)
                na = w[..., 0, 0] * a + w[..., 0, 1] * b
                nb2 = w[..., 1, 0] * a + w[..., 1, 1] * b
                y = jnp.stack([na, nb2], axis=-2).reshape(*lead, dim)
            return y
        h = jnp.einsum('bsd,dh->bsh', x, W_exp) + b_exp
        h = butterfly(h, up_weights, D_HIDDEN)
        h = jax.nn.gelu(h + up_bias, approximate=False)
        h = butterfly(h, down_weights, D_HIDDEN)
        y = jnp.einsum('bsh,hd->bsd', h, W_con) + b_con
        return y + down_bias
    h = _L0_tok_ref(x, L0_tok_Wq_w, L0_tok_Wq_b, L0_tok_Wk_w, L0_tok_Wk_b, L0_tok_Wv_w, L0_tok_Wv_b, L0_tok_w_bias, L0_tok_out_w, L0_tok_out_b, L0_tok_ln_g, L0_tok_ln_b, L0_tok_local_mask)
    h = jnp.concatenate([h, txt], axis=1)
    h = h + _L0_attn_ref(_layernorm(h, axis=-1), L0_attn_Wq, L0_attn_bq, L0_attn_Wk, L0_attn_bk, L0_attn_Wv, L0_attn_bv, L0_attn_Wo, L0_attn_bo)
    h = h + _L0_ffn_ref(_layernorm(h, axis=-1), L0_ffn_W_exp, L0_ffn_b_exp, L0_ffn_up_weights, L0_ffn_up_bias, L0_ffn_down_weights, L0_ffn_W_con, L0_ffn_b_con, L0_ffn_down_bias)
    return h

_drawn_inputs = setup_inputs


def setup_inputs(seed=0):
    import zlib

    import numpy as np

    out = dict(_drawn_inputs(seed))
    spreads = {'L0_tok_Wq_b': (0.0, 2.0),
     'L0_tok_Wk_b': (0.0, 2.0),
     'L0_tok_Wv_b': (0.0, 0.1),
     'L0_tok_out_b': (0.0, 0.1),
     'L0_tok_ln_g': (1.0, 0.2),
     'L0_tok_ln_b': (0.0, 0.1),
     'L0_ffn_b_exp': (0.0, 0.1),
     'L0_ffn_up_bias': (0.0, 0.1),
     'L0_ffn_b_con': (0.0, 0.1),
     'L0_ffn_down_bias': (0.0, 0.1)}
    factors = {'L0_tok_w_bias': 8.0,
     'L0_attn_Wq': 8.0,
     'L0_attn_bq': 42.628,
     'L0_attn_Wk': 8.0,
     'L0_attn_bk': 64.0,
     'L0_attn_bv': 8.0,
     'L0_attn_bo': 3.077}
    for name, (base, spread) in spreads.items():
        noise = np.random.default_rng([zlib.crc32(name.encode()), seed]).standard_normal(out[name].shape)
        drawn = base * np.exp(spread * noise) if base else spread * noise
        out[name] = jnp.asarray(drawn.astype(out[name].dtype))
    for name, factor in factors.items():
        out[name] = (out[name] * factor).astype(out[name].dtype)
    return out
```

```python
from contextlib import ExitStack

import concourse.bass as bass
import numpy as np
from concourse import mybir

ALU = mybir.AluOpType
ACT = mybir.ActivationFunctionType
F32 = mybir.dt.float32
F32R = mybir.dt.float32r
BF16 = mybir.dt.bfloat16
U8 = mybir.dt.uint8
U32 = mybir.dt.uint32
AX_X = mybir.AxisListType.X

P = 128
BATCH, C, L, H = 16, 64, 256, 4
LT = 32
S = L + LT
D = C * H
NH, HD = 16, 16
HID = 1024
STAGES = 10
TILES = BATCH * L // P + BATCH * LT // P
IMG_TILES = BATCH * L // P
EPS = 1e-5
MASKED = -1e30
KEEP = 3e38
SLOTS_Q = (0, 0, 0, 1, 1, 2)
SLOTS_K = (0, 1, 2, 0, 1, 0)
SR = HD * len(SLOTS_Q)
NPARTS = 3
M_COLS = 2 * NH + 4
GROUPS = 4
W_KT1 = S - P
UP_COLS = D + 1
HSLOTS = 8
FF_TOK = 512
FF_STEPS = TILES * P // FF_TOK

LAYOUT_OF_STAGE = (0, 0, 0, 1, 1, 1, 2, 2, 2, 3)
LAYOUT_SHIFT = (0, 3, 6, 7)


def layout_units(layout):
    p, f = np.arange(P)[:, None], np.arange(8)[None, :]
    if layout == 0:
        return p * 8 + f
    if layout == 1:
        return (p % 16) * 64 + f * 8 + p // 16
    if layout == 2:
        return (p // 64) * 512 + f * 64 + p % 64
    return f * P + p


def layout_pieces(dram, tile, layout):
    if layout == 0:
        return [(dram.rearrange("(p f) c -> p f c", f=8), tile)]
    if layout == 1:
        v = dram.rearrange("(a f b) c -> b a f c", a=16, f=8)
        return [(v[b], tile[16 * b:16 * b + 16]) for b in range(8)]
    if layout == 2:
        v = dram.rearrange("(a f b) c -> a b f c", a=2, f=8)
        return [(v[a], tile[64 * a:64 * a + 64]) for a in range(2)]
    return [(dram.rearrange("(f p) c -> p f c", p=P), tile)]


class Batch:

    def __init__(self, n, half, parity):
        self.n, self.half, self.parity = n, half, parity
        self.fixed = isinstance(n, int)


class Turn:

    def __init__(self, loop, start, count=BATCH):
        self.loop, self.start, self.count = loop, start, count

    def batch(self, lag):
        c = self.start - lag
        if self.loop is None:
            return Batch(c, c // 2, c % 2) if 0 <= c < self.count else None
        return Batch(self.loop * 2 + c, self.loop + c // 2, c % 2)


def run_steps(eng, step, peel, count, lags):
    for i in range(peel):
        step(Turn(None, i, count))
    with eng.Fori(0, (count - peel) // 2) as loop:
        for u in range(2):
            step(Turn(loop, peel + u, count))
    for i in range(count, count + lags):
        step(Turn(None, i, count))


def wait_since(eng, sem, value):
    if isinstance(value, int) and value <= 0:
        return
    eng.wait_ge(sem, value)


def apart(eng, passed):
    eng.sem_inc(passed, 1)


def split_product(pe, out, a, b, start=True, stop=True, check=False):
    pe.matmul(out, a[0], b[0], start=start, stop=False, skip_group_check=check)
    pe.matmul(out, a[0], b[1], start=False, stop=False, skip_group_check=check)
    return pe.matmul(out, a[1], b[0], start=False, stop=stop, skip_group_check=check)


def build(nc, io):
    ctx = ExitStack()
    with ctx:
        def sb(name, shape, dt=F32, where=ctx):
            return where.enter_context(nc.sbuf_tensor(name, shape, dt))

        def sem(name):
            return ctx.enter_context(nc.semaphore(name))

        class K:
            pass

        k = K()
        k.io = io
        k.sem, k.sb = sem, sb
        k.psum = ctx.enter_context(nc.psum_tensor("psum", [P, 8, 512], F32))
        k.passed_sp, k.passed_dve, k.passed_pool = sem("passed_sp"), sem("passed_dve"), sem("passed_pool")
        k.h_all = sb("h_all", [P, TILES, D])
        k.stat_img = sb("stat_img", [P, IMG_TILES, 2])
        k.stat_txt = sb("stat_txt", [LT, BATCH, 2])
        k.ident = sb("ident", [P, P])
        k.ident_bf = sb("ident_bf", [P, P], BF16)
        k.mask_q = sb("mask_q", [P, 512], BF16)
        k.mask_txt = sb("mask_txt", [P, LT], BF16)
        k.keep_txt = sb("keep_txt", [P, LT])
        k.half_neg = sb("half_neg", [P, 64])
        k.rows = sb("rows", [P, 7, D])
        k.w_att = [sb(f"w_att_{x}", [P, 4, 2, D], F32R) for x in ("hi", "lo")]
        k.b_qk = sb("b_qk", [P, 2, 2])
        k.w_up = [sb(f"w_up_{x}", [P, 2, 8, P], F32R) for x in ("hi", "lo")]
        k.w_dn = [sb(f"w_dn_{x}", [P, 8, D], F32R) for x in ("hi", "lo")]
        k.b_gelu = sb("b_gelu", [P, 8])
        k.parts_dram = nc.dram_tensor("parts_dram", (2, 2, NPARTS, HD, 8, 2 * S), BF16, kind="Internal").ap()
        k.mrow_dram = nc.dram_tensor("mrow_dram", (2, NPARTS, M_COLS, P), BF16, kind="Internal").ap()
        k.h_txt_dram = nc.dram_tensor("h_txt_dram", (BATCH * LT, D), F32, kind="Internal").ap()
        k.fold_dram = {
            x: [nc.dram_tensor(f"fold_{x}{i}", (HID, UP_COLS if x == "up" else D), F32, kind="Internal").ap()
                for i in range(3)] for x in ("up", "dn")}
        k.b_up_dram = nc.dram_tensor("b_up_dram", (HID, 1), F32, kind="Internal").ap()
        with ExitStack() as mixing:
            k.w_tok = [sb(f"w_tok_{x}", [P, 3, P], F32R, mixing) for x in ("hi", "lo")]
            k.b_kv = [sb(f"b_kv_{x}", [P, 512], F32R, mixing) for x in ("hi", "lo")]
            k.ones = sb("ones", [P, P], F32R, mixing)
            k.nb_q = sb("nb_q", [P, 1], F32, mixing)
            k.ew = sb("ew", [P, 2, L], F32, mixing)
            k.w_out = [sb(f"w_out_{x}", [P, 2, D], F32R, mixing) for x in ("hi", "lo")]
            with ExitStack() as own:
                prepare(nc, k, own)
            with ExitStack() as own:
                mix_tokens(nc, k, own)
        with ExitStack() as own:
            attend(nc, k, own)
        with ExitStack() as own:
            feed_forward(nc, k, own)


def prepare(nc, k, own):
    sb, sem, io = lambda n, s, d=F32: k.sb(n, s, d, own), k.sem, k.io
    cols = {"up": UP_COLS, "dn": D}
    fold = {x: [sb(f"fold_{x}_{i}", [P, 8, cols[x]]) for i in range(2)] for x in cols}
    cross = sb("cross", [P, 2, UP_COLS])
    coef = {x: sb(f"coef_{x}", [P, STAGES, 8, 2]) for x in cols}
    raw_tok = sb("raw_tok", [P, 3, P])
    raw_kv = sb("raw_kv", [P, 512])
    raw_att = sb("raw_att", [P, 4, 2, D])
    raw_out = sb("raw_out", [P, 2, D])
    raw_ew = sb("raw_ew", [P, 2, L])
    raw_mask = sb("raw_mask", [P, 2, L // 4], U32)
    masked_ew = sb("masked_ew", [P, 2, L])
    raw_bq = sb("raw_bq", [P, 1])
    raw_bqk = sb("raw_bqk", [P, 2, 2])
    b_up = sb("b_up", [P, 8])
    up_bias = sb("up_bias", [P, 8])
    txt = sb("txt", [P, 4, D])
    txt_stats = sb("txt_stats", [P, 4, 6])
    txt_mv = sb("txt_mv", [P, 4, 2])
    txt_ve = sb("txt_ve", [P, 4])
    txt_rn = sb("txt_rn", [P, 4, 2])

    zeroed = sem("raw_zeroed")
    coef_in = sem("coef_in")
    fold_in = {x: sem(f"fold_in_{x}") for x in cols}
    fold_out = {x: sem(f"fold_out_{x}") for x in cols}
    crossed = sem("crossed")
    folded = sem("folded")
    tok_in, att_in, out_in, ew_in, small_in, txt_in = (
        sem(x) for x in ("tok_in", "att_in", "out_in", "ew_in", "small_in", "txt_in"))
    split_hi, split_lo = sem("split_hi"), sem("split_lo")
    mask_steps, tri_copied = sem("mask_steps"), sem("tri_copied")
    ew_masked, small_done = sem("ew_masked"), sem("small_done")
    stats_txt, rn_txt, stat_moved = sem("stats_txt"), sem("rn_txt"), sem("stat_moved")
    up_turned, up_hi, up_lo, dn_hi, dn_lo = (
        sem(x) for x in ("up_turned", "up_hi", "up_lo", "dn_hi", "dn_lo"))
    b_up_out, b_up_in = sem("b_up_out"), sem("b_up_in")
    act_done = sem("prep_act_done")

    steps = []
    for i in range(STAGES):
        for x in ("up", "dn"):
            s = i if x == "up" else STAGES - 1 - i
            steps.append((x, i, s, LAYOUT_OF_STAGE[s]))
    order = {(x, i): n for n, (x, i, _, _) in enumerate(steps)}

    def layout_at(x, i):
        s = i if x == "up" else STAGES - 1 - i
        return LAYOUT_OF_STAGE[s]

    def moves(x):
        return [i for i in range(1, STAGES) if layout_at(x, i) != layout_at(x, i - 1)]

    in_count = {}
    out_count = {}
    for x in cols:
        total_in = 16 * len(layout_pieces(k.fold_dram[x][0], fold[x][0][:], layout_at(x, 0)))
        in_count[x, 0] = total_in
        total_out = 0
        for i in moves(x):
            total_out += 16 * len(layout_pieces(k.fold_dram[x][0], fold[x][0][:], layout_at(x, i - 1)))
            out_count[x, i] = total_out
            total_in += 16 * len(layout_pieces(k.fold_dram[x][0], fold[x][0][:], layout_at(x, i)))
            in_count[x, i] = total_in

    with nc.Block() as block:
        @block.sync
        def _(sp):
            for x in ("up", "dn"):
                sp.dma_start(coef[x][:], io[f"coef_{x}"]).then_inc(coef_in, 16)
                for d, t in layout_pieces(io["w_exp" if x == "up" else "w_con"], fold[x][0][:], layout_at(x, 0)):
                    sp.dma_start(t, d).then_inc(fold_in[x], 16)
            sp.dma_start(txt[:], io["txt"].rearrange("(t p) d -> p t d", p=P)).then_inc(txt_in, 16)
            n_move = {"up": 0, "dn": 0}
            for x, i, s, layout in steps:
                if i in moves(x):
                    dram = k.fold_dram[x][n_move[x]]
                    n_move[x] += 1
                    buf = fold[x][i % 2][:]
                    sp.wait_ge(folded, 8 * (order[x, i - 1] + 1))
                    for d, t in layout_pieces(dram, buf, layout_at(x, i - 1)):
                        sp.dma_start(d, t).then_inc(fold_out[x], 16)
                    sp.wait_ge(fold_out[x], out_count[x, i])
                    for d, t in layout_pieces(dram, buf, layout):
                        sp.dma_start(t, d).then_inc(fold_in[x], 16)
                if i == 4 and x == "dn":
                    sp.wait_ge(rn_txt, 2)
                    for j in range(4):
                        sp.dma_start(k.stat_txt[:].rearrange("p (t j) v -> p j t v", j=4)[:, j],
                                     txt_rn[LT * j:LT * j + LT]).then_inc(stat_moved, 16)
            sp.wait_ge(folded, 8 * (order["up", STAGES - 1] + 1))
            with nc.allow_non_contiguous_dma(reason="one bias vector"):
                sp.dma_start(k.b_up_dram.rearrange("(f p) c -> p (f c)", p=P),
                             fold["up"][STAGES % 2][:, :, D]).then_inc(b_up_out, 16)
                sp.wait_ge(b_up_out, 16)
                sp.dma_start(b_up[:], k.b_up_dram.rearrange("(p f) c -> p (f c)", f=8)).then_inc(b_up_in, 16)
            sp.wait_ge(stat_moved, 64)

        @block.scalar
        def _(act):
            act.wait_ge(zeroed, 2)
            for j in range(2):
                for w in range(3):
                    act.dma_start(raw_tok[C * j:C * j + C, w, C * j:C * j + C], io["w_tok"][w]).then_inc(tok_in, 16)
            for v in range(2):
                act.dma_start(raw_kv[0:1, :].rearrange("o (a v b c) -> o v a b c", a=2, v=2, b=2)[:, v].rearrange("o a b c -> o a (b c)"),
                              io["b_tok_rows"][1 + v:2 + v]).then_inc(tok_in, 16)
            act.dma_start(raw_bq[:], io["b_tok_q"]).then_inc(tok_in, 16)
            act.dma_start(raw_ew[:], io["ew"].rearrange("(t p) q -> p t q", p=P)).then_inc(ew_in, 16)
            act.dma_start(raw_mask[:], io["mask"].rearrange("(t p) q -> p t q", p=P)).then_inc(ew_in, 16)
            act.dma_start(raw_out[:], io["w_out"].rearrange("(a p) n -> p a n", p=P)).then_inc(out_in, 16)
            act.dma_start(k.rows[:], io["rows"].partition_broadcast(P)).then_inc(small_in, 16)
            act.dma_start(raw_bqk[:], io["b_qk"]).then_inc(small_in, 16)
            act.dma_start(up_bias[:], io["up_bias"].rearrange("(p f) -> p f", f=8)).then_inc(small_in, 16)
            for w in range(4):
                act.dma_start(raw_att[:, w], io["w_att"][w].rearrange("(a p) n -> p a n", p=P)).then_inc(att_in, 16)
            act.wait_ge(ew_masked, 1)
            act.activation(k.ew[:], masked_ew[:], ACT.Exp).then_inc(act_done, 1)
            act.wait_ge(coef_in, 32)
            for n, (x, i, s, layout) in enumerate(steps):
                bit = 1 << (s - LAYOUT_SHIFT[layout])
                if i in moves(x) or i == 0:
                    act.wait_ge(fold_in[x], in_count[x, i])
                for f in range(8):
                    if i:
                        act.wait_ge(folded, 8 * order[x, i - 1] + (f ^ bit) + 1)
                    wait_since(act, folded, 8 * n + f - 1)
                    act.activation(cross[:, f % 2, 0:cols[x]], fold[x][i % 2][:, f ^ bit, :], ACT.Copy,
                                   scale=coef[x][:, s, f, 1:2]).then_inc(crossed, 1)
            for a in range(2):
                act.wait_ge(up_turned, a + 1)
                for b in range(2):
                    act.activation(
                        k.w_up[0][:, a].rearrange("p c (f q) -> p f q c", f=8)[:, 4 * b:4 * b + 4],
                        k.psum[:, 2 * a + b].rearrange("p (f q c) -> p f q c", f=4, c=8), ACT.Copy).then_inc(up_hi, 1)
            act.wait_ge(folded, 8 * len(steps))
            act.activation(k.w_dn[0][:], fold["dn"][STAGES % 2][:], ACT.Copy).then_inc(dn_hi, 1)

        @block.vector
        def _(dve):
            dve.memset(raw_tok[:], 0.0).then_inc(zeroed, 1)
            dve.memset(raw_kv[:], 0.0).then_inc(zeroed, 1)
            dve.memset(k.ones[:].bitcast(F32), 1.0)
            dve.memset(k.half_neg[:], -0.5).then_inc(zeroed, 1)
            dve.wait_ge(ew_in, 32)
            dve.tensor_tensor(masked_ew[:], raw_ew[:], raw_mask[:].bitcast(U8), ALU.mult).then_inc(ew_masked, 1)
            dve.wait_ge(txt_in, 16)
            for t in range(4):
                dve.bn_stats(txt_stats[:, t], txt[:, t]).then_inc(stats_txt, 1)
            dve.wait_ge(stats_txt, 4)
            for t in range(4):
                dve.bn_aggr(txt_mv[:, t], txt_stats[:, t]).then_inc(stats_txt, 1)
            for n, (x, i, s, layout) in enumerate(steps):
                if i in moves(x) or i == 0:
                    dve.wait_ge(fold_in[x], in_count[x, i])
                for f in range(8):
                    dve.wait_ge(crossed, 8 * n + f + 1)
                    if i:
                        dve.wait_ge(folded, 8 * order[x, i - 1] + f + 1)
                    dve.scalar_tensor_tensor(
                        out=fold[x][(i + 1) % 2][:, f, :], in0=fold[x][i % 2][:, f, :], scalar=coef[x][:, s, f, 0:1],
                        in1=cross[:, f % 2, 0:cols[x]], op0=ALU.mult, op1=ALU.add).then_inc(folded, 1)
            for a in range(2):
                for b in range(2):
                    dve.wait_ge(up_hi, 2 * a + b + 1)
                    view = lambda w: w[:, a].rearrange("p c (f q) -> p f q c", f=8)[:, 4 * b:4 * b + 4]
                    dve.tensor_tensor(view(k.w_up[1]), k.psum[:, 2 * a + b].rearrange("p (f q c) -> p f q c", f=4, c=8),
                                      view(k.w_up[0]).bitcast(F32), ALU.subtract).then_inc(up_lo, 1)
            dve.wait_ge(dn_hi, 1)
            dve.tensor_tensor(k.w_dn[1][:], fold["dn"][STAGES % 2][:], k.w_dn[0][:].bitcast(F32), ALU.subtract).then_inc(dn_lo, 1)
            dve.wait_ge(b_up_in, 16)
            dve.wait_ge(small_in, 48)
            dve.tensor_tensor(k.b_gelu[:], b_up[:], up_bias[:], ALU.add).then_inc(dn_lo, 1)

        @block.tensor
        def _(pe):
            pe.wait_ge(folded, 8 * (order["up", STAGES - 1] + 1))
            pe.wait_ge(mask_steps, 2)
            for a in range(2):
                for b in range(2):
                    for f in range(4):
                        last = pe.transpose(k.psum[:, 2 * a + b, P * f:P * f + P],
                                            fold["up"][STAGES % 2][:, 4 * b + f, P * a:P * a + P], k.ident[:])
                last.then_inc(up_turned, 1)

        @block.gpsimd
        def _(pool):
            pool.memset(k.ident[:], 1.0).then_inc(mask_steps, 1)
            pool.wait_ge(mask_steps, 1)
            pool.affine_select(out=k.ident[:], in_=k.ident[:], compare_op=ALU.is_equal, fill=0.0, base=0,
                               pattern=[[-1, P]], channel_multiplier=1).then_inc(mask_steps, 1)
            pool.memset(k.mask_q[:], 0.0)
            pool.memset(k.keep_txt[:], KEEP).then_inc(mask_steps, 1)
            pool.wait_ge(mask_steps, 3)
            pool.tensor_scalar(k.ident_bf[:], k.ident[:], 1.0, 0.0, ALU.mult, ALU.add).then_inc(mask_steps, 1)
            pool.affine_select(out=k.mask_q[:].rearrange("p (r k) -> p r k", r=4),
                               in_=k.mask_q[:].rearrange("p (r k) -> p r k", r=4), compare_op=ALU.is_ge,
                               fill=MASKED, base=0, pattern=[[0, 4], [-1, P]], channel_multiplier=1).then_inc(mask_steps, 1)
            for j in range(4):
                pool.wait_ge(mask_steps, 5 + j)
                pool.affine_select(out=k.keep_txt[LT * j:LT * j + LT], in_=k.keep_txt[LT * j:LT * j + LT],
                                   compare_op=ALU.is_ge, fill=0.0, base=0, pattern=[[1, LT]],
                                   channel_multiplier=-1).then_inc(mask_steps, 1)
            pool.wait_ge(mask_steps, 9)
            pool.memset(k.mask_txt[:], 0.0).then_inc(tri_copied, 1)
            for j in range(4):
                pool.wait_ge(tri_copied, 1 + j)
                pool.affine_select(out=k.mask_txt[LT * j:LT * j + LT], in_=k.mask_txt[LT * j:LT * j + LT],
                                   compare_op=ALU.is_ge, fill=MASKED, base=0, pattern=[[-1, LT]],
                                   channel_multiplier=1).then_inc(tri_copied, 1)

            def split(hi, lo, raw, n):
                pool.tensor_scalar(hi, raw, 1.0, 0.0, ALU.mult, ALU.add).then_inc(split_hi, 1)
                pool.wait_ge(split_hi, n)
                pool.tensor_tensor(lo, raw, hi.bitcast(F32), ALU.subtract).then_inc(split_lo, 1)

            pool.wait_ge(tri_copied, 5)
            pool.wait_ge(zeroed, 2)
            pool.wait_ge(tok_in, 16 * 9)
            split(k.w_tok[0][:], k.w_tok[1][:], raw_tok[:], 1)
            split(k.b_kv[0][:], k.b_kv[1][:], raw_kv[:], 2)
            pool.wait_ge(out_in, 16)
            split(k.w_out[0][:], k.w_out[1][:], raw_out[:], 3)
            pool.wait_ge(stats_txt, 8)
            pool.wait_ge(zeroed, 3)
            pool.tensor_scalar(txt_ve[:], txt_mv[:, :, 1], 1.0, EPS, ALU.mult, ALU.add).then_inc(small_done, 1)
            pool.tensor_scalar(txt_rn[:, :, 1], txt_mv[:, :, 0], -1.0, 0.0, ALU.mult, ALU.add).then_inc(small_done, 1)
            pool.wait_ge(small_done, 2)
            pool.tensor_tensor(txt_rn[:, :, 0], txt_ve[:], k.half_neg[:, 0:4], ALU.pow).then_inc(rn_txt, 1)
            pool.wait_ge(rn_txt, 1)
            pool.tensor_tensor(txt_rn[:, :, 1], txt_rn[:, :, 1], txt_rn[:, :, 0], ALU.mult).then_inc(rn_txt, 1)
            pool.wait_ge(small_in, 48)
            pool.tensor_scalar(k.b_qk[:, 0], raw_bqk[:, 0], HD ** -0.5, 0.0, ALU.mult, ALU.add)
            pool.tensor_scalar(k.b_qk[:, 1], raw_bqk[:, 1], 1.0, 0.0, ALU.mult, ALU.add).then_inc(small_done, 1)
            pool.tensor_tensor(k.rows[:, 5], k.rows[:, 5], k.rows[:, 6], ALU.add).then_inc(small_done, 1)
            pool.wait_ge(att_in, 64)
            for w in range(4):
                split(k.w_att[0][:, w], k.w_att[1][:, w], raw_att[:, w], 4 + w)
            pool.wait_ge(split_lo, 7)
            pool.tensor_scalar(k.nb_q[:], raw_bq[:], -1.0, 0.0, ALU.mult, ALU.add)


OUT_B, LN_G, LN_B, ATT_BV, ATT_BO, FF_B = range(6)


def mix_tokens(nc, k, own):
    sb, sem, io = lambda n, s, d=F32: k.sb(n, s, d, own), k.sem, k.io
    x_raw = sb("x_raw", [P, 2, 2, L])
    x_hi = sb("x_hi", [P, 2, 2, L], F32R)
    x_lo = sb("x_lo", [P, 2, 2, L], F32R)
    xt_raw = sb("xt_raw", [P, 2, 2, D])
    xtb = sb("xtb", [P, 2, D])
    ek = sb("ek", [P, 2, 2, D])
    ekv = sb("ekv", [P, 2, 2, D])
    eq = sb("eq", [P, 512])
    den = sb("den", [P, 512])
    rec = sb("rec", [P, 512])
    y = sb("y", [P, 2, L])
    y_hi = sb("y_hi", [P, 2, L], F32R)
    y_lo = sb("y_lo", [P, 2, L], F32R)
    h1 = sb("h1", [P, 2, D])
    st1 = sb("st1", [P, 2, 6])
    mv1 = sb("mv1", [P, 2, 2])
    ve1 = sb("ve1", [P, 2])
    rn1 = sb("rn1", [P, 2, 2])
    z = sb("z", [P, 2, D])
    zg = sb("zg", [P, 2, D])
    st2 = sb("st2", [P, 2, 6])
    mv2 = sb("mv2", [P, 2, 2])
    mv_all = sb("mv_all", [P, IMG_TILES, 2])
    ve_all = sb("ve_all", [P, IMG_TILES])

    x_loaded = [sem(f"x_loaded{i}") for i in range(2)]
    xt_loaded = [sem(f"xt_loaded{i}") for i in range(2)]
    names = ("x_hi_ready x_lo_ready q_ps kv_ps ek_ready ekv_ready eq_ready nd_ps den_ready rec_ready y_ready "
             "y_hi_ready y_lo_ready out_ps xtb_ready h1_ready st1_ready mv1_ready ve1_ready rstd1_ready rn1_ready "
             "z_ready zg_ready h_ready st2_ready mv2_ready mv_kept tail").split()
    s = {n: sem("mix_" + n) for n in names}

    QB, KVB, OUTB = 0, 1, 5
    NUMB, DENB = (3, 6), (4, 7)
    bank = lambda i: k.psum[:, i]

    def row(i):
        return k.rows[:, i].unsqueeze(1).broadcast_to([P, 2, D])

    with nc.Block() as block:
        @block.sync
        def _(sp):
            def step(turn):
                if b := turn.batch(0):
                    wait_since(sp, s["x_lo_ready"], b.n - 1)
                    apart(sp, k.passed_sp)
                    sp.dma_start(x_raw[:, b.parity].rearrange("p a l -> p (a l)"), io["x"][b.n] if b.fixed else
                                 io["x"][bass.ds(b.n, 1)].rearrange("o p c -> (o p) c")).then_inc(x_loaded[b.parity], 16)
                if b := turn.batch(3):
                    wait_since(sp, s["xtb_ready"], b.n - 1)
                    apart(sp, k.passed_sp)
                    src = io["xt"][bass.ds(b.n, 1)].rearrange("o (t p) d -> p (o t) d", p=P)
                    sp.dma_start(xt_raw[:, b.parity], src).then_inc(xt_loaded[b.parity], 16)
            run_steps(sp, step, 6, BATCH, 3)

        @block.scalar
        def _(act):
            def step(turn):
                if b := turn.batch(5):
                    act.wait_ge(s["rn1_ready"], b.n + 1)
                    wait_since(act, s["zg_ready"], b.n)
                    for t in range(2):
                        last = act.activation(z[:, t], h1[:, t], ACT.Identity, bias=rn1[:, t, 1:2], scale=rn1[:, t, 0:1])
                    last.then_inc(s["z_ready"], 1)
                if b := turn.batch(0):
                    act.wait_ge(x_loaded[b.parity], (b.half + 1) * 16)
                    wait_since(act, s["q_ps"], b.n - 1)
                    act.activation(x_hi[:, b.parity], x_raw[:, b.parity], ACT.Copy).then_inc(s["x_hi_ready"], 1)
                if b := turn.batch(1):
                    act.wait_ge(s["kv_ps"], b.n + 1)
                    wait_since(act, s["nd_ps"], b.n - 1)
                    act.activation(ek[:, b.parity].rearrange("p t (a c) -> p t a c", a=2),
                                   k.psum[:, KVB:KVB + 2].rearrange("p t (a v c) -> p t a v c", a=2, v=2)[:, :, :, 0],
                                   ACT.Exp).then_inc(s["ek_ready"], 1)
                if b := turn.batch(2):
                    act.wait_ge(s["q_ps"], b.n + 1)
                    wait_since(act, s["den_ready"], b.n)
                    act.activation(eq[:], bank(QB), ACT.Exp, bias=k.nb_q[:], scale=-1.0).then_inc(s["eq_ready"], 1)
                if b := turn.batch(3):
                    act.wait_ge(s["y_ready"], b.n + 1)
                    wait_since(act, s["out_ps"], b.n)
                    act.activation(y_hi[:], y[:], ACT.Copy).then_inc(s["y_hi_ready"], 1)
            run_steps(act, step, 6, BATCH, 5)

        @block.vector
        def _(dve):
            def step(turn):
                if b := turn.batch(3):
                    dve.wait_ge(s["eq_ready"], b.n + 1)
                    dve.wait_ge(s["nd_ps"], b.n + 1)
                    wait_since(dve, s["rec_ready"], b.n)
                    dve.scalar_tensor_tensor(out=den[:], in0=eq[:], scalar=1.0, in1=bank(DENB[b.parity]),
                                             op0=ALU.add, op1=ALU.mult).then_inc(s["den_ready"], 1)
                    dve.wait_ge(s["den_ready"], b.n + 1)
                    wait_since(dve, s["y_ready"], b.n)
                    dve.reciprocal(rec[:], den[:]).then_inc(s["rec_ready"], 1)
                    dve.wait_ge(s["rec_ready"], b.n + 1)
                    wait_since(dve, s["y_lo_ready"], b.n)
                    dve.tensor_tensor(y[:].rearrange("p a l -> p (a l)"), bank(NUMB[b.parity]), rec[:],
                                      ALU.mult).then_inc(s["y_ready"], 1)
                if b := turn.batch(4):
                    dve.wait_ge(s["out_ps"], b.n + 1)
                    dve.wait_ge(s["xtb_ready"], b.n + 1)
                    wait_since(dve, s["z_ready"], b.n)
                    dve.tensor_tensor(h1[:].rearrange("p t d -> p (t d)"), bank(OUTB),
                                      xtb[:].rearrange("p t d -> p (t d)"), ALU.add).then_inc(s["h1_ready"], 1)
                    dve.wait_ge(s["h1_ready"], b.n + 1)
                    wait_since(dve, s["mv1_ready"], b.n * 2)
                    for t in range(2):
                        dve.bn_stats(st1[:, t], h1[:, t]).then_inc(s["st1_ready"], 1)
                    dve.wait_ge(s["st1_ready"], b.n * 2 + 2)
                    wait_since(dve, s["rn1_ready"], b.n)
                    apart(dve, k.passed_dve)
                    for t in range(2):
                        dve.bn_aggr(mv1[:, t], st1[:, t]).then_inc(s["mv1_ready"], 1)
                if b := turn.batch(1):
                    dve.wait_ge(s["ek_ready"], b.n + 1)
                    dve.tensor_tensor(ekv[:, b.parity].rearrange("p t (a c) -> p t a c", a=2),
                                      k.psum[:, KVB:KVB + 2].rearrange("p t (a v c) -> p t a v c", a=2, v=2)[:, :, :, 1],
                                      ek[:, b.parity].rearrange("p t (a c) -> p t a c", a=2),
                                      ALU.mult).then_inc(s["ekv_ready"], 1)
                if b := turn.batch(5):
                    dve.wait_ge(s["h_ready"], b.n + 1)
                    wait_since(dve, s["mv2_ready"], b.n * 2)
                    for t in range(2):
                        dve.bn_stats(st2[:, t],
                                     k.h_all[:, bass.ds(b.n * 2 + t, 1), :].rearrange("p o d -> p (o d)")).then_inc(s["st2_ready"], 1)
                    dve.wait_ge(s["st2_ready"], b.n * 2 + 2)
                    wait_since(dve, s["mv_kept"], b.n)
                    apart(dve, k.passed_dve)
                    for t in range(2):
                        dve.bn_aggr(mv2[:, t], st2[:, t]).then_inc(s["mv2_ready"], 1)
                    dve.wait_ge(s["mv2_ready"], b.n * 2 + 2)
                    dve.tensor_copy(mv_all[:, bass.ds(b.n * 2, 2), :], mv2[:]).then_inc(s["mv_kept"], 1)
            run_steps(dve, step, 6, BATCH, 5)

        @block.tensor
        def _(pe):
            def step(turn):
                if b := turn.batch(4):
                    pe.wait_ge(s["y_hi_ready"], b.n + 1)
                    pe.wait_ge(s["y_lo_ready"], b.n + 1)
                    wait_since(pe, s["h1_ready"], b.n)
                    for t in range(2):
                        for a in range(2):
                            last = split_product(pe, k.psum[:, OUTB, D * t:D * t + D],
                                                 [v[:, a, P * t:P * t + P] for v in (y_hi, y_lo)],
                                                 [w[:, a] for w in k.w_out], start=a == 0, stop=a == 1)
                    last.then_inc(s["out_ps"], 1)
                if b := turn.batch(2):
                    wait_since(pe, s["eq_ready"], b.n)
                    x = (x_hi[:, b.parity], x_lo[:, b.parity])
                    for a in range(2):
                        last = split_product(pe, k.psum[:, QB, L * a:L * a + L], [w[:, 0] for w in k.w_tok],
                                             [v[:, a] for v in x])
                    last.then_inc(s["q_ps"], 1)
                if b := turn.batch(1):
                    pe.wait_ge(s["x_hi_ready"], b.n + 1)
                    pe.wait_ge(s["x_lo_ready"], b.n + 1)
                    wait_since(pe, s["ekv_ready"], b.n)
                    x = (x_hi[:, b.parity], x_lo[:, b.parity])
                    for t in range(2):
                        pe.matmul(bank(KVB + t), k.ones[:], k.b_kv[0][:], start=True, stop=False)
                        pe.matmul(bank(KVB + t), k.ones[:], k.b_kv[1][:], start=False, stop=False)
                        for a in range(2):
                            last = split_product(pe, k.psum[:, KVB + t, 2 * P * a:2 * P * a + 2 * P],
                                                 [v[:, a, P * t:P * t + P] for v in x],
                                                 [w[:, 1:3].rearrange("p v c -> p (v c)") for w in k.w_tok],
                                                 start=False, stop=a == 1)
                    last.then_inc(s["kv_ps"], 1)
                if b := turn.batch(2):
                    pe.wait_ge(s["ekv_ready"], b.n + 1)
                    wait_since(pe, s["y_ready"], b.n - 1)
                    for src, out in ((ek, DENB[b.parity]), (ekv, NUMB[b.parity])):
                        for a in range(2):
                            for t in range(2):
                                last = pe.matmul(k.psum[:, out, L * a:L * a + L], src[:, b.parity, t, P * a:P * a + P],
                                                 k.ew[:, t], start=t == 0, stop=t == 1)
                    last.then_inc(s["nd_ps"], 1)
            run_steps(pe, step, 6, BATCH, 4)

        @block.gpsimd
        def _(pool):
            def step(turn):
                if b := turn.batch(4):
                    pool.wait_ge(xt_loaded[b.parity], (b.half + 1) * 16)
                    wait_since(pool, s["h1_ready"], b.n)
                    pool.tensor_tensor(xtb[:], xt_raw[:, b.parity], row(OUT_B), ALU.add).then_inc(s["xtb_ready"], 1)
                if b := turn.batch(5):
                    pool.wait_ge(s["z_ready"], b.n + 1)
                    wait_since(pool, s["h_ready"], b.n)
                    pool.tensor_tensor(zg[:], z[:], row(LN_G), ALU.mult).then_inc(s["zg_ready"], 1)
                    pool.wait_ge(s["zg_ready"], b.n + 1)
                    pool.tensor_tensor(k.h_all[:, bass.ds(b.n * 2, 2), :], zg[:], row(LN_B),
                                       ALU.add).then_inc(s["h_ready"], 1)
                if b := turn.batch(0):
                    pool.wait_ge(s["x_hi_ready"], b.n + 1)
                    wait_since(pool, s["q_ps"], b.n - 1)
                    pool.tensor_tensor(x_lo[:, b.parity], x_raw[:, b.parity], x_hi[:, b.parity].bitcast(F32),
                                       ALU.subtract).then_inc(s["x_lo_ready"], 1)
                if b := turn.batch(3):
                    pool.wait_ge(s["y_hi_ready"], b.n + 1)
                    wait_since(pool, s["out_ps"], b.n)
                    pool.tensor_tensor(y_lo[:], y[:], y_hi[:].bitcast(F32), ALU.subtract).then_inc(s["y_lo_ready"], 1)
                if b := turn.batch(4):
                    pool.wait_ge(s["mv1_ready"], b.n * 2 + 2)
                    wait_since(pool, s["z_ready"], b.n)
                    apart(pool, k.passed_pool)
                    pool.tensor_scalar(ve1[:], mv1[:, :, 1], 1.0, EPS, ALU.mult, ALU.add).then_inc(s["ve1_ready"], 1)
                    pool.tensor_scalar(rn1[:, :, 1], mv1[:, :, 0], -1.0, 0.0, ALU.mult, ALU.add)
                    pool.wait_ge(s["ve1_ready"], b.n + 1)
                    pool.tensor_tensor(rn1[:, :, 0], ve1[:], k.half_neg[:, 0:2], ALU.pow).then_inc(s["rstd1_ready"], 1)
                    pool.wait_ge(s["rstd1_ready"], b.n + 1)
                    pool.tensor_tensor(rn1[:, :, 1], rn1[:, :, 1], rn1[:, :, 0], ALU.mult).then_inc(s["rn1_ready"], 1)
            run_steps(pool, step, 6, BATCH, 5)
            pool.wait_ge(s["mv_kept"], BATCH)
            pool.tensor_scalar(ve_all[:], mv_all[:, :, 1], 1.0, EPS, ALU.mult, ALU.add).then_inc(s["tail"], 1)
            pool.wait_ge(s["tail"], 1)
            pool.tensor_scalar(k.stat_img[:, :, 1], mv_all[:, :, 0], -1.0, 0.0, ALU.mult, ALU.add)
            pool.tensor_tensor(k.stat_img[:, :, 0], ve_all[:], k.half_neg[:, 0:IMG_TILES], ALU.pow).then_inc(s["tail"], 1)
            pool.wait_ge(s["tail"], 2)
            pool.tensor_tensor(k.stat_img[:, :, 1], k.stat_img[:, :, 1], k.stat_img[:, :, 0], ALU.mult).then_inc(s["tail"], 1)


def attend(nc, k, own):
    sb, sem, io = lambda n, s, d=F32: k.sb(n, s, d, own), k.sem, k.io
    head = [(i % 2) * 8 + i // 2 for i in range(NH)]
    txt_in = sb("txt_in", [LT, D])
    txt_res = sb("txt_res", [LT, D])
    xn = sb("xn", [P, 3, D])
    xt_hi = [sb(f"xt_hi{i}", [P, 2, S], F32R) for i in range(2)]
    xt_lo = [sb(f"xt_lo{i}", [P, 2, S], F32R) for i in range(2)]
    xt_txt4 = [[sb(f"xt_txt4_{x}{i}", [P, 2, 4, LT], F32R) for x in ("hi", "lo")] for i in range(2)]
    qk = sb("qk", [P, 2, 2, S])
    qk_rest = sb("qk_rest", [P, 2, 2, S])
    parts = sb("parts", [P, NPARTS, 2, 2 * S], BF16)
    q_st = [sb(f"q_st{i}", [SR + NPARTS, NH, S], BF16) for i in range(2)]
    k_st = [sb(f"k_st{i}", [SR + NPARTS, NH, S], BF16) for i in range(2)]
    v_aug = [sb(f"v_aug{i}", [P, 3, NH, 2 * HD]) for i in range(2)]
    prob = sb("prob", [P, HSLOTS, W_KT1 + S])
    prob_txt = sb("prob_txt", [P, GROUPS, LT])
    nmax = sb("nmax", [P, M_COLS])
    nmax_rest = sb("nmax_rest", [P, M_COLS])
    mparts = sb("mparts", [P, NPARTS, M_COLS], BF16)
    mrow = sb("mrow", [NPARTS * M_COLS, P], BF16)
    ctx_u = sb("ctx_u", [P, GROUPS, S])
    rsum = sb("rsum", [P, 3, NH])
    ctx_n = sb("ctx_n", [P, 3, D])
    ct_hi = sb("ct_hi", [P, 2, S], F32R)
    ct_lo = sb("ct_lo", [P, 2, S], F32R)
    hb = sb("hb", [P, 2, D])
    hb_txt = sb("hb_txt", [LT, D])
    h_txt = sb("h_txt", [LT, D])

    names = ("txt_loaded res_loaded xn_ready xnT_ps xnT_hi xnT_lo q_ps k_ps v_ps qk_ready part_h rest_h part_m rest_m "
             "parts_ready v_ready m0_ps m1_ps mt_ps m0_max m1_max mt_max mp_h mr_h mp_m mr_m mp_ready mT_ps mT_ready "
             "mrow_stored st_ps stt_ps exp_done expt_done "
             "seen keep_done ctx_ps ctx_u_done o1_ps rsum_ready ctxn_ready ctxT_ps ctxT_hi ctxT_lo o_ps hb_ready "
             "h_done h_txt_stored ones_set").split()
    s = {n: sem("att_" + n) for n in names}
    parts_stored = [sem(f"att_parts_stored{i}") for i in range(2)]
    stack_loaded = [sem(f"att_stack_loaded{i}") for i in range(2)]
    mrow_loaded = [sem(f"att_mrow_loaded{i}") for i in range(2)]
    N_STORE, N_STACK = 2 * NPARTS, 6
    bank = lambda i: k.psum[:, i]
    turned_maxima = k.psum[:, 3].bitcast(BF16)[0:NPARTS * M_COLS, 512 + P:512 + 2 * P]

    with nc.Block() as block:
        @block.sync
        def _(sp):
            def step(turn):
                if b := turn.batch(0):
                    wait_since(sp, s["xn_ready"], b.n)
                    apart(sp, k.passed_sp)
                    wait_since(sp, s["txt_loaded"], b.n * 16)
                    apart(sp, k.passed_sp)
                    sp.dma_start(txt_in[:], io["txt"][bass.ds(b.n * LT, LT), :]).then_inc(s["txt_loaded"], 16)
                if b := turn.batch(4):
                    wait_since(sp, s["hb_ready"], b.n)
                    apart(sp, k.passed_sp)
                    wait_since(sp, s["res_loaded"], b.n * 16)
                    apart(sp, k.passed_sp)
                    sp.dma_start(txt_res[:], io["txt"][bass.ds(b.n * LT, LT), :]).then_inc(s["res_loaded"], 16)
                if b := turn.batch(3):
                    u = b.parity
                    sp.wait_ge(s["mT_ready"], b.n + 1)
                    sp.dma_start(k.mrow_dram[u].rearrange("r c q -> (r c) q"), mrow[:]).then_inc(s["mrow_stored"], 16)
                    sp.wait_ge(s["mrow_stored"], b.n * 16 + 16)
                    for t in range(2):
                        sp.dma_start(q_st[u][SR:SR + NPARTS, :, P * t:P * t + P],
                                     k.mrow_dram[u, :, NH * t:NH * t + NH]).then_inc(mrow_loaded[u], 16)
                    sp.dma_start(q_st[u][SR:SR + NPARTS, :, L:S],
                                 k.mrow_dram[u, :, 2 * NH:].rearrange("r g (j q) -> r (g j) q", j=4)).then_inc(mrow_loaded[u], 16)
                if b := turn.batch(1):
                    u = b.parity
                    sp.wait_ge(s["parts_ready"], b.n + 1)
                    apart(sp, k.passed_sp)
                    wait_since(sp, stack_loaded[u], b.half * (16 * N_STACK))
                    for x in range(2):
                        for r in range(NPARTS):
                            sp.dma_start(k.parts_dram[u, x, r].rearrange("d a q -> a d q"),
                                         parts[:, r, x]).then_inc(parts_stored[u], 16)
                    apart(sp, k.passed_sp)
                    sp.wait_ge(parts_stored[u], (b.half + 1) * (16 * N_STORE))
                    apart(sp, k.passed_sp)
                    wait_since(sp, s["st_ps"], (b.n - 1) * NH)
                    for first, n in ((0, 3), (3, 2), (5, 1)):
                        to = slice(HD * first, HD * (first + n))
                        sp.dma_start(k_st[u][to], k.parts_dram[u, 1, 0:n].rearrange("r d a q -> (r d) (a q)")
                                     ).then_inc(stack_loaded[u], 16)
                        part = k.parts_dram[u, 0, 3 - n].rearrange("d a q -> d (a q)")
                        sp.dma_start(q_st[u][to], part.unsqueeze(0).broadcast_to([n, HD, 8 * 2 * S])
                                     ).then_inc(stack_loaded[u], 16)
                if b := turn.batch(4):
                    sp.wait_ge(s["h_done"], b.n + 1)
                    apart(sp, k.passed_sp)
                    sp.dma_start(k.h_txt_dram[bass.ds(b.n * LT, LT), :], h_txt[:]).then_inc(s["h_txt_stored"], 16)
            run_steps(sp, step, 6, BATCH, 4)
            sp.wait_ge(s["h_txt_stored"], BATCH * 16)

        @block.scalar
        def _(act):
            def normalise(b):
                act.wait_ge(s["txt_loaded"], b.n * 16 + 16)
                wait_since(act, s["xnT_ps"], b.n)
                for t in range(2):
                    act.activation(xn[:, t], k.h_all[:, bass.ds(b.n * 2 + t, 1), :].rearrange("p o d -> p (o d)"), ACT.Identity,
                                   bias=k.stat_img[:, bass.ds(b.n * 2 + t, 1), 1], scale=k.stat_img[:, bass.ds(b.n * 2 + t, 1), 0])
                act.activation(xn[0:LT, 2], txt_in[:], ACT.Identity, bias=k.stat_txt[:, bass.ds(b.n, 1), 1],
                               scale=k.stat_txt[:, bass.ds(b.n, 1), 0]).then_inc(s["xn_ready"], 1)

            def round_xt(b):
                act.wait_ge(s["xnT_ps"], b.n + 1)
                wait_since(act, s["v_ps"], b.n - 1)
                act.activation(xt_hi[b.parity][:], k.psum[:, 0:2, 0:S], ACT.Copy).then_inc(s["xnT_hi"], 1)

            def leave_qk(b):
                for x, base, ps, scale in ((0, 0, "q_ps", HD ** -0.5), (1, 4, "k_ps", 1.0)):
                    act.wait_ge(s[ps], b.n + 1)
                    if x == 0:
                        wait_since(act, s["parts_ready"], b.n)
                    for a in range(2):
                        last = act.activation(qk[:, x, a], k.psum[:, base + a, 0:S], ACT.Identity,
                                              bias=k.b_qk[:, x, a:a + 1], scale=scale)
                last.then_inc(s["qk_ready"], 1)

            def round_ct(b):
                act.wait_ge(s["ctxT_ps"], b.n + 1)
                wait_since(act, s["o_ps"], b.n)
                act.activation(ct_hi[:], k.psum[:, 2:4, 0:S], ACT.Copy).then_inc(s["ctxT_hi"], 1)

            def exps(b, g):
                if g == 0:
                    act.wait_ge(s["stt_ps"], b.n + 1)
                    wait_since(act, s["ctx_ps"], b.n * GROUPS)
                    act.activation(prob_txt[:].rearrange("p g q -> p (g q)"), k.psum[:, 7, 0:GROUPS * LT],
                                   ACT.Exp).then_inc(s["expt_done"], 1)
                wait_since(act, s["ctx_ps"], b.n * GROUPS + (g - 1))
                for j in range(4):
                    i = 4 * g + j
                    act.wait_ge(s["st_ps"], b.n * NH + (i + 1))
                    act.activation(prob[:, i % HSLOTS], k.psum[:, 4 + i % 2, 0:W_KT1 + S], ACT.Exp).then_inc(s["exp_done"], 1)

            def leave_ctx(b, g):
                act.wait_ge(s["ctx_ps"], b.n * GROUPS + (g + 1))
                wait_since(act, s["o1_ps"], b.n)
                act.activation(ctx_u[:, g], k.psum[:, 6, 0:S], ACT.Copy).then_inc(s["ctx_u_done"], 1)

            def step(turn):
                if b := turn.batch(1):
                    round_xt(b)
                if b := turn.batch(4):
                    round_ct(b)
                if b := turn.batch(1):
                    leave_qk(b)
                probs_b, next_b = turn.batch(3), turn.batch(0)
                for g in range(GROUPS):
                    if probs_b:
                        exps(probs_b, g)
                        if g:
                            leave_ctx(probs_b, g - 1)
                    if g == 1 and next_b:
                        normalise(next_b)
                if probs_b:
                    leave_ctx(probs_b, GROUPS - 1)
            run_steps(act, step, 6, BATCH, 4)

        @block.vector
        def _(dve):
            for i in range(2):
                dve.memset(v_aug[i][:], 1.0).then_inc(s["ones_set"], 1)
                dve.memset(k_st[i][SR:SR + NPARTS], 1.0).then_inc(s["ones_set"], 1)

            def normalise_ctx(b):
                dve.wait_ge(s["o1_ps"], b.n + 1)
                for t, ps, n in ((0, 4, P), (1, 5, P), (2, 7, LT)):
                    src = k.psum[0:n, ps].rearrange("p (h c) -> p h c", c=2 * HD)
                    if t == 0:
                        wait_since(dve, s["ctxn_ready"], b.n * 3)
                        wait_since(dve, s["ctxT_ps"], b.n)
                    dve.reciprocal(rsum[0:n, t], src[:, :, HD]).then_inc(s["rsum_ready"], 1)
                for t, ps, n in ((0, 4, P), (1, 5, P), (2, 7, LT)):
                    src = k.psum[0:n, ps].rearrange("p (a x c) -> p a x c", a=8, x=2)
                    dve.wait_ge(s["rsum_ready"], b.n * 3 + (t + 1))
                    dve.tensor_tensor(ctx_n[0:n, t].rearrange("p (x a c) -> p a x c", x=2, a=8), src[:, :, :, 0:HD],
                                      rsum[0:n, t].rearrange("p (a x) -> p a x", a=8).unsqueeze(3).broadcast_to([n, 8, 2, HD]),
                                      ALU.mult).then_inc(s["ctxn_ready"], 1)

            def leave_mrow(b):
                dve.wait_ge(s["mT_ps"], b.n + 1)
                wait_since(dve, s["mrow_stored"], b.n * 16)
                dve.tensor_copy(mrow[:], turned_maxima).then_inc(s["mT_ready"], 1)

            def rest_xt(b):
                dve.wait_ge(s["xnT_hi"], b.n + 1)
                wait_since(dve, s["v_ps"], b.n - 1)
                hi, lo = xt_hi[b.parity], xt_lo[b.parity]
                dve.tensor_tensor(lo[:], k.psum[:, 0:2, 0:S], hi[:].bitcast(F32), ALU.subtract).then_inc(s["xnT_lo"], 1)
                dve.wait_ge(s["xnT_lo"], b.n * 3 + 1)
                for dst, src in zip(xt_txt4[b.parity], (hi, lo)):
                    dve.tensor_copy(dst[:], src[:, :, L:S].bitcast(F32).unsqueeze(2).broadcast_to([P, 2, 4, LT])).then_inc(s["xnT_lo"], 1)

            def rest_ct(b):
                dve.wait_ge(s["ctxT_hi"], b.n + 1)
                wait_since(dve, s["o_ps"], b.n)
                dve.tensor_tensor(ct_lo[:], k.psum[:, 2:4, 0:S], ct_hi[:].bitcast(F32), ALU.subtract).then_inc(s["ctxT_lo"], 1)

            def leave_v(b):
                dve.wait_ge(s["v_ps"], b.n + 1)
                wait_since(dve, s["ctx_ps"], (b.n - 1) * GROUPS)
                if b.fixed and b.n < 2:
                    dve.wait_ge(s["ones_set"], 4)
                out = v_aug[b.parity]
                bias = k.rows[:, ATT_BV].rearrange("p (h c) -> p h c", h=NH)
                dve.tensor_tensor(out[:, 0:2, :, 0:HD], k.psum[:, 6].rearrange("p (t h c) -> p t h c", t=2, h=NH),
                                  bias.unsqueeze(1).broadcast_to([P, 2, NH, HD]), ALU.add)
                dve.tensor_tensor(out[:, 2, :, 0:HD], k.psum[:, 7, 0:D].rearrange("p (h c) -> p h c", h=NH),
                                  bias, ALU.add).then_inc(s["v_ready"], 1)

            def split3(b):
                flat = lambda t: t[:].rearrange("p x a q -> p (x a q)")
                part = lambda i: parts[:, i].rearrange("p x q -> p (x q)")
                dve.wait_ge(s["qk_ready"], b.n + 1)
                if b.parity:
                    dve.wait_ge(parts_stored[0], (b.half + 1) * (16 * N_STORE))
                else:
                    wait_since(dve, parts_stored[1], b.half * (16 * N_STORE))
                dve.tensor_copy(part(0), flat(qk)).then_inc(s["part_h"], 1)
                dve.wait_ge(s["part_h"], b.n + 1)
                wait_since(dve, s["parts_ready"], b.n)
                dve.tensor_tensor(flat(qk_rest), flat(qk), part(0), ALU.subtract).then_inc(s["rest_h"], 1)
                dve.wait_ge(s["rest_h"], b.n + 1)
                dve.tensor_copy(part(1), flat(qk_rest)).then_inc(s["part_m"], 1)
                dve.wait_ge(s["part_m"], b.n + 1)
                dve.tensor_tensor(part(2), flat(qk_rest), part(1), ALU.subtract).then_inc(s["parts_ready"], 1)

            def add_residual(b):
                dve.wait_ge(s["o_ps"], b.n + 1)
                dve.wait_ge(s["hb_ready"], b.n + 1)
                wait_since(dve, s["h_txt_stored"], b.n * 16)
                dve.tensor_tensor(k.h_all[:, bass.ds(b.n * 2, 2), :], k.psum[:, 2].rearrange("p (t d) -> p t d", t=2),
                                  hb[:], ALU.add)
                dve.tensor_tensor(h_txt[:], k.psum[0:LT, 3, 0:D], hb_txt[:], ALU.add).then_inc(s["h_done"], 1)

            def maxima(b, g):
                if g == 0:
                    wait_since(dve, s["mp_ready"], b.n)
                dve.wait_ge(s["m0_ps"], b.n * GROUPS + (g + 1))
                dve.tensor_reduce(nmax[:, 4 * g:4 * g + 4], k.psum[:, 0].rearrange("p (h c) -> p h c", h=4), AX_X, ALU.max,
                                  negate=True).then_inc(s["m0_max"], 1)
                dve.wait_ge(s["m1_ps"], b.n * GROUPS + (g + 1))
                dve.tensor_reduce(nmax[:, NH + 4 * g:NH + 4 * g + 4], k.psum[:, 1:3].rearrange("p t (h c) -> p (t h) c", h=2),
                                  AX_X, ALU.max, negate=True).then_inc(s["m1_max"], 1)
                dve.wait_ge(s["mt_ps"], b.n * GROUPS + (g + 1))
                dve.tensor_reduce(nmax[:, 2 * NH + g:2 * NH + g + 1], k.psum[:, 3, 0:S], AX_X, ALU.max,
                                  negate=True).then_inc(s["mt_max"], 1)

            def split_maxima(b):
                n = b.n
                dve.wait_ge(s["mt_max"], n * GROUPS + GROUPS)
                wait_since(dve, s["mT_ps"], n)
                dve.tensor_copy(mparts[:, 0], nmax[:]).then_inc(s["mp_h"], 1)
                dve.wait_ge(s["mp_h"], n + 1)
                dve.tensor_tensor(nmax_rest[:], nmax[:], mparts[:, 0], ALU.subtract).then_inc(s["mr_h"], 1)
                dve.wait_ge(s["mr_h"], n + 1)
                dve.tensor_copy(mparts[:, 1], nmax_rest[:]).then_inc(s["mp_m"], 1)
                dve.wait_ge(s["mp_m"], n + 1)
                dve.tensor_tensor(mparts[:, 2], nmax_rest[:], mparts[:, 1], ALU.subtract).then_inc(s["mp_ready"], 1)

            def limit_txt(b):
                dve.wait_ge(s["expt_done"], b.n + 1)
                dve.tensor_tensor(prob_txt[:], prob_txt[:], k.keep_txt[:].unsqueeze(1).broadcast_to([P, GROUPS, LT]),
                                  ALU.min).then_inc(s["keep_done"], 1)

            def step(turn):
                own_b, max_b, probs_b, out_b = (turn.batch(lag) for lag in (1, 2, 3, 4))
                if probs_b:
                    leave_mrow(probs_b)
                if out_b:
                    normalise_ctx(out_b)
                if own_b:
                    rest_xt(own_b)
                if out_b:
                    rest_ct(out_b)
                if max_b:
                    leave_v(max_b)
                if out_b:
                    add_residual(out_b)
                if probs_b:
                    limit_txt(probs_b)
                for g in range(GROUPS):
                    if max_b:
                        maxima(max_b, g)
                    if g == 0 and own_b:
                        split3(own_b)
                if max_b:
                    split_maxima(max_b)
            run_steps(dve, step, 6, BATCH, 4)

        @block.tensor
        def _(pe):
            w = lambda i, a, half: [v[:, i, a, P * half:P * half + P] for v in k.w_att]

            def turn_maxima(b):
                pe.wait_ge(s["mp_ready"], b.n + 1)
                pe.transpose(turned_maxima, mparts[:].rearrange("p r c -> p (r c)"),
                             k.ident_bf[:]).then_inc(s["mT_ps"], 1)

            def turn_ctx(b):
                pe.wait_ge(s["ctx_u_done"], b.n * GROUPS + GROUPS)
                pe.wait_ge(s["exp_done"], b.n * NH + NH)
                pe.wait_ge(s["expt_done"], b.n + 1)
                for t, ps, n in ((0, 4, P), (1, 5, P), (2, 7, LT)):
                    for g in range(GROUPS):
                        last = pe.transpose(k.psum[0:n, ps, P * g:P * g + P], ctx_u[:, g, P * t:P * t + n], k.ident[:])
                last.then_inc(s["o1_ps"], 1)

            def turn_xn(b):
                pe.wait_ge(s["xn_ready"], b.n + 1)
                wait_since(pe, s["m1_max"], (b.n - 1) * GROUPS)
                for a in range(2):
                    for t, n in ((0, P), (1, P), (2, LT)):
                        last = pe.transpose(k.psum[:, a, P * t:P * t + n], xn[0:n, t, P * a:P * a + P], k.ident[0:n, 0:n])
                last.then_inc(s["xnT_ps"], 1)

            def turn_ctxn(b):
                pe.wait_ge(s["ctxn_ready"], b.n * 3 + 3)
                if b.fixed and b.n >= BATCH - 1:
                    pe.wait_ge(s["mt_max"], BATCH * GROUPS)
                else:
                    pe.wait_ge(s["mt_max"], (b.n + 2) * GROUPS)
                for a in range(2):
                    for t, n in ((0, P), (1, P), (2, LT)):
                        last = pe.transpose(k.psum[:, 2 + a, P * t:P * t + n], ctx_n[0:n, t, P * a:P * a + P], k.ident[0:n, 0:n])
                last.then_inc(s["ctxT_ps"], 1)

            def project_qk(b):
                xt = (xt_hi[b.parity], xt_lo[b.parity])
                pe.wait_ge(s["xnT_lo"], b.n * 3 + 3)
                for x, base, ps in ((0, 0, "q_ps"), (1, 4, "k_ps")):
                    if x == 1:
                        wait_since(pe, s["ctxn_ready"], (b.n - 2) * 3)
                    for half in range(2):
                        for a in range(2):
                            last = split_product(pe, k.psum[:, base + half, 0:S], w(x, a, half), [v[:, a] for v in xt],
                                                 start=a == 0, stop=a == 1)
                    last.then_inc(s[ps], 1)

            def project_v(b):
                xt = (xt_hi[b.parity], xt_lo[b.parity])
                wait_since(pe, s["ctx_u_done"], (b.n - 1) * GROUPS)
                for t in range(2):
                    for a in range(2):
                        split_product(pe, k.psum[:, 6, D * t:D * t + D], [v[:, a, P * t:P * t + P] for v in xt],
                                      [v[:, 2, a] for v in k.w_att], start=a == 0, stop=a == 1)
                wait_since(pe, s["ctxn_ready"], (b.n - 1) * 3)
                for a in range(2):
                    last = split_product(pe, k.psum[:, 7, 0:D], [v[:, a].rearrange("p r q -> p (r q)") for v in xt_txt4[b.parity]],
                                         [v[:, 2, a] for v in k.w_att], start=a == 0, stop=a == 1)
                last.then_inc(s["v_ps"], 1)

            def project_out(b):
                ct = (ct_hi, ct_lo)
                pe.wait_ge(s["ctxT_lo"], b.n + 1)
                for t, ps, n in ((0, 2, P), (1, 2, P), (2, 3, LT)):
                    out = k.psum[0:n, ps, D * (t % 2):D * (t % 2) + D]
                    for a in range(2):
                        last = split_product(pe, out, [v[:, a, P * t:P * t + n] for v in ct],
                                             [v[:, 3, a] for v in k.w_att], start=a == 0, stop=a == 1)
                last.then_inc(s["o_ps"], 1)

            def scores_for_max(b, g, which):
                q, kk = q_st[b.parity], k_st[b.parity]
                heads = range(4 * g, 4 * g + 4)
                if which == 0:
                    if g == 0:
                        pe.wait_ge(stack_loaded[b.parity], (b.half + 1) * (16 * N_STACK))
                        pe.wait_ge(s["qk_ready"], BATCH if b.fixed and b.n == BATCH - 1 else b.n + 2)
                    wait_since(pe, s["m0_max"], b.n * GROUPS + g)
                    pe.matmul(bank(0), k.ident_bf[:], k.mask_q[:], start=True, stop=False, skip_group_check=True)
                    for j, h in enumerate(heads):
                        last = pe.matmul(k.psum[:, 0, P * j:P * j + P], q[0:SR, h, 0:P], kk[0:SR, h, 0:P], start=False,
                                         stop=True, skip_group_check=True)
                    last.then_inc(s["m0_ps"], 1)
                elif which == 1:
                    if g == 0:
                        wait_since(pe, s["h_done"], b.n - 1)
                    wait_since(pe, s["m1_max"], b.n * GROUPS + g)
                    for c in range(2):
                        pe.matmul(k.psum[:, 1 + c].rearrange("p (h c) -> p h c", h=2)[:, :, P:L], k.ident_bf[:],
                                  k.mask_q[:, 0:L].rearrange("p (h c) -> p h c", h=2), start=True, stop=False,
                                  skip_group_check=True)
                        for j in range(2):
                            h = heads[2 * c + j]
                            last = pe.matmul(k.psum[:, 1 + c, L * j:L * j + L], q[0:SR, h, P:L], kk[0:SR, h, 0:L], start=False,
                                             stop=True, skip_group_check=True)
                    last.then_inc(s["m1_ps"], 1)
                else:
                    wait_since(pe, s["mt_max"], b.n * GROUPS + g)
                    pe.matmul(k.psum[:, 3, L:S], k.ident_bf[:], k.mask_txt[:], start=True, stop=False, skip_group_check=True)
                    for j, h in enumerate(heads):
                        last = pe.matmul(k.psum[LT * j:LT * j + LT, 3, 0:S], q[0:SR, h, L:S], kk[0:SR, h, 0:S], start=False,
                                         stop=True, skip_group_check=True)
                    last.then_inc(s["mt_ps"], 1)

            def scores_transposed(b, pair):
                q, kk = q_st[b.parity], k_st[b.parity]
                rows = slice(0, SR + NPARTS)
                if pair == 0:
                    pe.wait_ge(mrow_loaded[b.parity], (b.half + 1) * 48)
                    pe.wait_ge(s["v_ready"], min(b.n + 2, BATCH) if b.fixed else b.n + 2)
                    pe.wait_ge(s["qk_ready"], min(b.n + 3, BATCH) if b.fixed else b.n + 3)
                    for h in range(NH):
                        j = h % 4
                        last = pe.matmul(k.psum[LT * j:LT * j + LT, 7, LT * (h // 4):LT * (h // 4) + LT],
                                         kk[rows, h, L:S], q[rows, h, L:S], start=True, stop=True)
                    last.then_inc(s["stt_ps"], 1)
                for h in (2 * pair, 2 * pair + 1):
                    wait_since(pe, s["exp_done"], b.n * NH + (h - 1))
                    pe.matmul(k.psum[:, 4 + h % 2, 0:W_KT1], kk[rows, h, P:L], q[rows, h, P:S], start=True, stop=True)
                    pe.matmul(k.psum[:, 4 + h % 2, W_KT1:W_KT1 + S], kk[rows, h, 0:P], q[rows, h, 0:S], start=True,
                              stop=True).then_inc(s["st_ps"], 1)

            def weigh_values(b, g):
                v = v_aug[b.parity]
                pe.wait_ge(s["seen"], b.n * NH + (4 * g + 4))
                wait_since(pe, s["ctx_u_done"], b.n * GROUPS + g)
                pe.wait_ge(s["keep_done"], b.n + 1)
                for j in range(4):
                    h = 4 * g + j
                    pe.matmul(k.psum[LT * j:LT * j + LT, 6, 0:S], v[:, 0, head[h]], prob[:, h % HSLOTS, W_KT1:], start=True,
                              stop=False)
                for j in range(4):
                    h = 4 * g + j
                    pe.matmul(k.psum[LT * j:LT * j + LT, 6, P:S], v[:, 1, head[h]], prob[:, h % HSLOTS, 0:W_KT1], start=False,
                              stop=False)
                for j in range(4):
                    h = 4 * g + j
                    last = pe.matmul(k.psum[LT * j:LT * j + LT, 6, L:S], v[LT * j:LT * j + LT, 2, head[h]],
                                     prob_txt[LT * j:LT * j + LT, g], start=False, stop=True)
                last.then_inc(s["ctx_ps"], 1)

            def step(turn):
                own_b, max_b, probs_b, out_b = (turn.batch(lag) for lag in (1, 2, 3, 4))
                if own_b:
                    turn_xn(own_b)
                if out_b:
                    turn_ctx(out_b)
                if probs_b:
                    turn_maxima(probs_b)
                if max_b:
                    project_v(max_b)
                if out_b:
                    turn_ctxn(out_b)
                if own_b:
                    project_qk(own_b)
                if out_b:
                    project_out(out_b)
                for what, i in ORDER:
                    if what == "scores" and probs_b:
                        scores_transposed(probs_b, i)
                    if what == "values" and probs_b:
                        weigh_values(probs_b, i)
                    if what == "maxima" and max_b:
                        scores_for_max(max_b, i // 3, i % 3)
            run_steps(pe, step, 6, BATCH, 4)

        @block.gpsimd
        def _(pool):
            def step(turn):
                if b := turn.batch(4):
                    pool.wait_ge(s["res_loaded"], b.n * 16 + 16)
                    wait_since(pool, s["h_done"], b.n)
                    pool.tensor_tensor(hb[:], k.h_all[:, bass.ds(b.n * 2, 2), :],
                                       k.rows[:, ATT_BO].unsqueeze(1).broadcast_to([P, 2, D]), ALU.add)
                    pool.tensor_tensor(hb_txt[:], txt_res[:], k.rows[0:LT, ATT_BO], ALU.add).then_inc(s["hb_ready"], 1)
                if b := turn.batch(3):
                    for h in range(NH):
                        pool.wait_ge(s["exp_done"], b.n * NH + (h + 1))
                        apart(pool, k.passed_pool)
                        v = prob[:, h % HSLOTS, 0:2 * W_KT1].rearrange("p (t q) -> p t q", t=2)[:, :, 0:P]
                        pool.affine_select(out=v, in_=v, compare_op=ALU.is_ge, fill=0.0, base=0, pattern=[[0, 2], [1, P]],
                                           channel_multiplier=-1).then_inc(s["seen"], 1)
            run_steps(pool, step, 6, BATCH, 4)


ORDER = []
for _g in range(GROUPS):
    ORDER += [("scores", 2 * _g), ("maxima", 3 * _g), ("scores", 2 * _g + 1), ("maxima", 3 * _g + 1)]
    ORDER += [("values", _g - 1)] if _g else []
    ORDER += [("maxima", 3 * _g + 2)]
ORDER += [("values", GROUPS - 1)]


STATS_AT, NORMALISE_AT, TURN_AT = 0, 2, 5


def feed_forward(nc, k, own):
    sb, sem, io = lambda n, s, d=F32: k.sb(n, s, d, own), k.sem, k.io
    T = FF_TOK // P
    st = sb("ff_st", [P, T, 6])
    mv = sb("ff_mv", [P, T, 2])
    ve = sb("ff_ve", [P, T])
    rn = sb("ff_rn", [P, T, 2])
    xn = sb("ff_xn", [P, T, D])
    xt = [[sb(f"ff_xt_{x}{i}", [P, 2, FF_TOK], F32R) for x in ("hi", "lo")] for i in range(2)]
    g = sb("ff_g", [P, 2, FF_TOK])
    g_hi = sb("ff_g_hi", [P, 2, FF_TOK], F32R)
    g_lo = sb("ff_g_lo", [P, 2, FF_TOK], F32R)
    hb = sb("ff_hb", [P, 2, T, D])
    out = sb("ff_out", [P, 2, T, D])
    names = ("txt_in st_ready mv_ready ve_ready rstd_ready rn_ready xn_ready xnT_ps xnT_hi xnT_lo u_ps g_ready g_hi g_lo "
             "y_ps hb_ready out_ready").split()
    s = {n: sem("ff_" + n) for n in names}
    stored = [sem(f"ff_stored{i}") for i in range(2)]
    XT, UB, YB = (4, 7), (2, 3), ((0, 1), (5, 6))

    with nc.Block() as block:
        @block.sync
        def _(sp):
            sp.dma_start(k.h_all[:, IMG_TILES:], k.h_txt_dram.rearrange("(t p) d -> p t d", p=P)).then_inc(s["txt_in"], 16)

            def step(turn):
                if b := turn.batch(1):
                    sp.wait_ge(s["out_ready"], b.n + 1)
                    u = b.parity
                    if b.fixed and b.n == FF_STEPS - 1:
                        for t in range(T):
                            for j in range(4):
                                sp.dma_start(io["out"][4 * t + j, L:S], out[LT * j:LT * j + LT, u, t]).then_inc(stored[u], 16)
                    else:
                        apart(sp, k.passed_sp)
                        for j in range(2):
                            dst = io["out"][bass.ds(b.n * 2 + j, 1), 0:L].rearrange("o (t p) d -> p (o t) d", p=P)
                            sp.dma_start(dst, out[:, u, 2 * j:2 * j + 2]).then_inc(stored[u], 16)
            run_steps(sp, step, 3, FF_STEPS, 1)
            sp.wait_ge(stored[1], 16 * 2 * 4)
            sp.wait_ge(stored[0], 16 * (2 * 4 + 16))

        @block.scalar
        def _(act):
            def normalise(b):
                act.wait_ge(s["rn_ready"], b.n + 1)
                wait_since(act, s["xnT_ps"], b.n)
                for t in range(T):
                    last = act.activation(xn[:, t], k.h_all[:, bass.ds(b.n * T + t, 1), :].rearrange("p o d -> p (o d)"),
                                          ACT.Identity, bias=rn[:, t, 1:2], scale=rn[:, t, 0:1])
                last.then_inc(s["xn_ready"], 1)

            def round_xt(b):
                for a in range(2):
                    act.wait_ge(s["xnT_ps"], b.n + 1)
                    wait_since(act, s["u_ps"], (b.n - 1) * 8)
                    act.activation(xt[b.parity][0][:, a], k.psum[:, XT[a]], ACT.Copy).then_inc(s["xnT_hi"], 1)

            def step(turn):
                next_b, b = turn.batch(0), turn.batch(1)
                for c in range(8):
                    if b:
                        act.wait_ge(s["u_ps"], b.n * 8 + (c + 1))
                        wait_since(act, s["g_lo"], b.n * 8 + (c - 1))
                        act.activation(g[:, c % 2], k.psum[:, UB[c % 2]], ACT.Gelu, bias=k.b_gelu[:, c:c + 1]).then_inc(s["g_ready"], 1)
                    if c == NORMALISE_AT and next_b:
                        normalise(next_b)
                    if c == TURN_AT and next_b:
                        round_xt(next_b)
            run_steps(act, step, 3, FF_STEPS, 1)

        @block.vector
        def _(dve):
            def stats(b):
                if b.fixed and b.n == 0:
                    dve.wait_ge(s["txt_in"], 16)
                wait_since(dve, s["mv_ready"], b.n * T)
                for t in range(T):
                    dve.bn_stats(st[:, t], k.h_all[:, bass.ds(b.n * T + t, 1), :].rearrange("p o d -> p (o d)")).then_inc(s["st_ready"], 1)
                dve.wait_ge(s["st_ready"], b.n * T + T)
                wait_since(dve, s["rn_ready"], b.n)
                apart(dve, k.passed_dve)
                for t in range(T):
                    dve.bn_aggr(mv[:, t], st[:, t]).then_inc(s["mv_ready"], 1)

            def rest_xt(b):
                for a in range(2):
                    dve.wait_ge(s["xnT_hi"], b.n * 2 + (a + 1))
                    wait_since(dve, s["u_ps"], (b.n - 1) * 8)
                    dve.tensor_tensor(xt[b.parity][1][:, a], k.psum[:, XT[a]], xt[b.parity][0][:, a].bitcast(F32),
                                      ALU.subtract).then_inc(s["xnT_lo"], 1)

            def step(turn):
                next_b, b = turn.batch(0), turn.batch(1)
                for c in range(8):
                    if b:
                        dve.wait_ge(s["g_ready"], b.n * 8 + (c + 1))
                        wait_since(dve, s["y_ps"], b.n * 8 + (c - 1))
                        dve.tensor_scalar(g_hi[:, c % 2], g[:, c % 2], 1.0, None, ALU.mult).then_inc(s["g_hi"], 1)
                        dve.wait_ge(s["g_hi"], b.n * 8 + (c + 1))
                        dve.tensor_tensor(g_lo[:, c % 2], g[:, c % 2], g_hi[:, c % 2].bitcast(F32), ALU.subtract).then_inc(s["g_lo"], 1)
                    if c == STATS_AT and next_b:
                        stats(next_b)
                    if c == TURN_AT and next_b:
                        rest_xt(next_b)
                if b:
                    dve.wait_ge(s["y_ps"], b.n * 8 + 8)
                    dve.wait_ge(s["hb_ready"], b.n + 1)
                    if b.parity:
                        wait_since(dve, stored[1], b.half * 32)
                    else:
                        wait_since(dve, stored[0], b.half * 32)
                    for c in range(2):
                        last = dve.tensor_tensor(out[:, b.parity, 2 * c:2 * c + 2], k.psum[:, YB[b.parity][c]].rearrange("p (t d) -> p t d", t=2),
                                                 hb[:, b.parity, 2 * c:2 * c + 2], ALU.add)
                    last.then_inc(s["out_ready"], 1)
            run_steps(dve, step, 3, FF_STEPS, 1)

        @block.tensor
        def _(pe):
            def down(b, c):
                pe.wait_ge(s["g_lo"], b.n * 8 + (c + 1))
                if c == 0:
                    wait_since(pe, s["out_ready"], b.n - 1)
                for t in range(T):
                    first = c == 0 and t % 2 == 0
                    last = split_product(pe, k.psum[:, YB[b.parity][t // 2], D * (t % 2):D * (t % 2) + D],
                                         [v[:, c % 2, P * t:P * t + P] for v in (g_hi, g_lo)], [v[:, c] for v in k.w_dn],
                                         start=first, stop=c == 7, check=True)
                last.then_inc(s["y_ps"], 1)

            def up(b, c):
                x = xt[b.parity]
                wait_since(pe, s["g_ready"], b.n * 8 + (c - 1))
                for a in range(2):
                    last = split_product(pe, k.psum[:, UB[c % 2]], [w[:, a, c] for w in k.w_up], [v[:, a] for v in x],
                                         start=a == 0, stop=a == 1)
                last.then_inc(s["u_ps"], 1)

            def turn_xn(b):
                pe.wait_ge(s["xn_ready"], b.n + 1)
                wait_since(pe, s["xnT_lo"], b.n * 2)
                for a in range(2):
                    for t in range(T):
                        last = pe.transpose(k.psum[:, XT[a], P * t:P * t + P], xn[:, t, P * a:P * a + P], k.ident[:])
                last.then_inc(s["xnT_ps"], 1)

            def step(turn):
                next_b, b = turn.batch(0), turn.batch(1)
                if b:
                    pe.wait_ge(s["xnT_lo"], b.n * 2 + 2)
                for c in range(8):
                    if b:
                        up(b, c)
                        if c:
                            down(b, c - 1)
                    if c == TURN_AT and next_b:
                        turn_xn(next_b)
                if b:
                    down(b, 7)
            run_steps(pe, step, 3, FF_STEPS, 1)

        @block.gpsimd
        def _(pool):
            def step(turn):
                if b := turn.batch(0):
                    pool.wait_ge(s["mv_ready"], b.n * T + T)
                    wait_since(pool, s["xn_ready"], b.n)
                    apart(pool, k.passed_pool)
                    pool.tensor_scalar(ve[:], mv[:, :, 1], 1.0, EPS, ALU.mult, ALU.add).then_inc(s["ve_ready"], 1)
                    pool.tensor_scalar(rn[:, :, 1], mv[:, :, 0], -1.0, 0.0, ALU.mult, ALU.add)
                    pool.wait_ge(s["ve_ready"], b.n + 1)
                    pool.tensor_tensor(rn[:, :, 0], ve[:], k.half_neg[:, 0:T], ALU.pow).then_inc(s["rstd_ready"], 1)
                    pool.wait_ge(s["rstd_ready"], b.n + 1)
                    pool.tensor_tensor(rn[:, :, 1], rn[:, :, 1], rn[:, :, 0], ALU.mult).then_inc(s["rn_ready"], 1)
                    if b.fixed and b.n == 0:
                        pool.wait_ge(s["txt_in"], 16)
                    wait_since(pool, s["out_ready"], b.n - 1)
                    pool.tensor_tensor(hb[:, b.parity], k.h_all[:, bass.ds(b.n * T, T), :],
                                       k.rows[:, FF_B].unsqueeze(1).broadcast_to([P, T, D]), ALU.add).then_inc(s["hb_ready"], 1)
            run_steps(pool, step, 3, FF_STEPS, 1)


def butterfly_coefficients(weights, transposed):
    out = np.empty((P, STAGES, 8, 2), weights.dtype)
    for s in range(STAGES):
        hid = layout_units(LAYOUT_OF_STAGE[s])
        bit = (hid >> s) & 1
        pair = ((hid >> (s + 1)) << s) | (hid & ((1 << s) - 1))
        out[:, s, :, 0] = weights[s][pair, bit, bit]
        out[:, s, :, 1] = weights[s][pair, 1 - bit, bit] if transposed else weights[s][pair, bit, 1 - bit]
    return out


def kernel(x, txt, L0_tok_Wq_w, L0_tok_Wq_b, L0_tok_Wk_w, L0_tok_Wk_b, L0_tok_Wv_w, L0_tok_Wv_b, L0_tok_w_bias,
           L0_tok_out_w, L0_tok_out_b, L0_tok_ln_g, L0_tok_ln_b, L0_tok_local_mask, L0_attn_Wq, L0_attn_bq, L0_attn_Wk,
           L0_attn_bk, L0_attn_Wv, L0_attn_bv, L0_attn_Wo, L0_attn_bo, L0_ffn_W_exp, L0_ffn_b_exp, L0_ffn_up_weights,
           L0_ffn_up_bias, L0_ffn_down_weights, L0_ffn_W_con, L0_ffn_b_con, L0_ffn_down_bias):
    import concourse.bacc as bacc
    from concourse.bass_utils import run_bass_kernel_spmd

    a = np.asarray
    x = a(x)
    arrays = {
        "x": x.reshape(BATCH, C, L, 2, 2).transpose(0, 4, 1, 3, 2).reshape(BATCH, P, 2 * L),
        "xt": x.transpose(0, 2, 3, 1).reshape(BATCH, L, D),
        "txt": a(txt).reshape(BATCH * LT, D),
        "w_tok": np.stack([a(w).T for w in (L0_tok_Wq_w, L0_tok_Wk_w, L0_tok_Wv_w)]),
        "b_tok_rows": np.stack([np.tile(a(b), 4) for b in (L0_tok_Wq_b, L0_tok_Wk_b, L0_tok_Wv_b)]),
        "b_tok_q": np.tile(a(L0_tok_Wq_b), 2).reshape(P, 1),
        "ew": a(L0_tok_w_bias).T,
        "mask": np.ascontiguousarray(a(L0_tok_local_mask).T).view(np.uint32),
        "w_out": a(L0_tok_out_w),
        "rows": np.stack([a(v) for v in (L0_tok_out_b, L0_tok_ln_g, L0_tok_ln_b, L0_attn_bv, L0_attn_bo, L0_ffn_b_con,
                                         L0_ffn_down_bias)]),
        "w_att": np.stack([a(v) for v in (L0_attn_Wq, L0_attn_Wk, L0_attn_Wv, L0_attn_Wo)]),
        "b_qk": np.stack([a(v).reshape(2, P) for v in (L0_attn_bq, L0_attn_bk)]).transpose(2, 0, 1),
        "w_exp": np.concatenate([a(L0_ffn_W_exp).T, a(L0_ffn_b_exp)[:, None]], axis=1),
        "w_con": a(L0_ffn_W_con),
        "coef_up": butterfly_coefficients(a(L0_ffn_up_weights), False),
        "coef_dn": butterfly_coefficients(a(L0_ffn_down_weights), True),
        "up_bias": a(L0_ffn_up_bias),
    }
    nc = bacc.Bacc("TRN2", target_bir_lowering=False, num_devices=1)
    io, feeds = {}, {}
    for name, v in arrays.items():
        v = np.ascontiguousarray(v)
        feeds[f"in_{name}"] = v
        io[name] = nc.dram_tensor(f"in_{name}", v.shape, mybir.dt.from_np(v.dtype), kind="ExternalInput").ap()
    io["out"] = nc.dram_tensor("out_h", (BATCH, S, D), F32, kind="ExternalOutput").ap()
    build(nc, io)
    return run_bass_kernel_spmd(nc, [feeds], core_ids=[0]).results[0]["out_h"]
```

```python
from contextlib import ExitStack

import concourse.bass as bass
import numpy as np
from concourse import mybir

ALU = mybir.AluOpType
ACT = mybir.ActivationFunctionType
F32 = mybir.dt.float32
F32R = mybir.dt.float32r
BF16 = mybir.dt.bfloat16
U8 = mybir.dt.uint8
U32 = mybir.dt.uint32
AX_X = mybir.AxisListType.X

P = 128
BATCH, C, L, H = 16, 64, 256, 4
LT = 32
S = L + LT
D = C * H
NH, HD = 16, 16
HID = 1024
STAGES = 10
TILES = BATCH * L // P + BATCH * LT // P
IMG_TILES = BATCH * L // P
EPS = 1e-5
MASKED = -1e30
KEEP = 3e38
SLOTS_Q = (0, 0, 0, 1, 1, 2)
SLOTS_K = (0, 1, 2, 0, 1, 0)
SR = HD * len(SLOTS_Q)
NPARTS = 3
M_COLS = 2 * NH + 4
GROUPS = 4
W_KT1 = S - P
UP_COLS = D + 1
N_CROSS = 4
HSLOTS = 8
FF_TOK = 512
FF_STEPS = TILES * P // FF_TOK

IN_BLOCK = 7
PATHS = 8 * (2 * P - 2)


def stage_columns(stage, inputs_free):
    n = 2 ** (IN_BLOCK - stage) if inputs_free else 2 ** (stage + 1)
    return 8 * (n - 2), n


class Batch:

    def __init__(self, n, half, parity):
        self.n, self.half, self.parity = n, half, parity
        self.fixed = isinstance(n, int)


class Turn:

    def __init__(self, loop, start, count=BATCH):
        self.loop, self.start, self.count = loop, start, count

    def batch(self, lag):
        c = self.start - lag
        if self.loop is None:
            return Batch(c, c // 2, c % 2) if 0 <= c < self.count else None
        return Batch(self.loop * 2 + c, self.loop + c // 2, c % 2)


def run_steps(eng, step, peel, count, lags, first=0):
    for i in range(first, peel):
        step(Turn(None, i, count))
    with eng.Fori(0, (count - peel) // 2) as loop:
        for u in range(2):
            step(Turn(loop, peel + u, count))
    for i in range(count, count + lags):
        step(Turn(None, i, count))


def wait_since(eng, sem, value):
    if isinstance(value, int) and value <= 0:
        return
    eng.wait_ge(sem, value)


def apart(eng, passed):
    eng.sem_inc(passed, 1)


def split_product(pe, out, a, b, start=True, stop=True, check=False):
    pe.matmul(out, a[0], b[0], start=start, stop=False, skip_group_check=check)
    pe.matmul(out, a[0], b[1], start=False, stop=False, skip_group_check=check)
    return pe.matmul(out, a[1], b[0], start=False, stop=stop, skip_group_check=check)


def build(nc, io):
    ctx = ExitStack()
    with ctx:
        def sb(name, shape, dt=F32, where=ctx):
            return where.enter_context(nc.sbuf_tensor(name, shape, dt))

        def sem(name):
            return ctx.enter_context(nc.semaphore(name))

        class K:
            pass

        k = K()
        k.io = io
        k.sem, k.sb = sem, sb
        k.psum = ctx.enter_context(nc.psum_tensor("psum", [P, 8, 512], F32))
        k.passed_sp, k.passed_dve, k.passed_pool = sem("passed_sp"), sem("passed_dve"), sem("passed_pool")
        k.h_all = sb("h_all", [P, TILES, D])
        k.mv_all = sb("mv_all", [P, IMG_TILES, 2])
        k.stats_kept = sem("stats_kept")
        k.h_done = sem("h_done")
        k.stat_img = sb("stat_img", [P, IMG_TILES, 2])
        k.stat_txt = sb("stat_txt", [LT, BATCH, 2])
        k.ident = sb("ident", [P, P])
        k.ident_bf = sb("ident_bf", [P, P], BF16)
        k.mask_q = sb("mask_q", [P, 512], BF16)
        k.mask_txt = sb("mask_txt", [P, LT], BF16)
        k.keep_txt = sb("keep_txt", [P, LT])
        k.half_neg = sb("half_neg", [P, 64])
        k.rows = sb("rows", [P, 7, D])
        k.w_att = [sb(f"w_att_{x}", [P, 4, 2, D], F32R) for x in ("hi", "lo")]
        k.b_qk = sb("b_qk", [P, 2, 2])
        k.w_up = [sb(f"w_up_{x}", [P, 2, 8, P], F32R) for x in ("hi", "lo")]
        k.w_dn = [sb(f"w_dn_{x}", [P, 8, D], F32R) for x in ("hi", "lo")]
        k.b_gelu = sb("b_gelu", [P, 8])
        k.parts_dram = nc.dram_tensor("parts_dram", (2, 2, NPARTS, HD, 8, 2 * S), BF16, kind="Internal").ap()
        k.mrow_dram = nc.dram_tensor("mrow_dram", (2, NPARTS, M_COLS, P), BF16, kind="Internal").ap()
        k.h_txt_dram = nc.dram_tensor("h_txt_dram", (BATCH * LT, D), F32, kind="Internal").ap()
        with ExitStack() as mixing:
            k.w_tok = [sb(f"w_tok_{x}", [P, 3, P], F32R, mixing) for x in ("hi", "lo")]
            k.b_kv = [sb(f"b_kv_{x}", [P, 512], F32R, mixing) for x in ("hi", "lo")]
            k.ones = sb("ones", [P, P], F32R, mixing)
            k.nb_q = sb("nb_q", [P, 1], F32, mixing)
            k.ew = sb("ew", [P, 2, L], F32, mixing)
            k.w_out = [sb(f"w_out_{x}", [P, 2, D], F32R, mixing) for x in ("hi", "lo")]
            with ExitStack() as own:
                prepare(nc, k, own)
            with ExitStack() as own:
                mix_tokens(nc, k, own)
        with ExitStack() as own:
            feeding = feed_forward(nc, k, own)
        with ExitStack() as own:
            attending = attend(nc, k, own)
            run_phases(nc, attending, feeding)


def run_phases(nc, *phases):
    with nc.Block() as block:
        @block.sync
        def _(sp):
            for phase in phases:
                phase["sync"](sp)

        @block.scalar
        def _(act):
            for phase in phases:
                phase["scalar"](act)

        @block.vector
        def _(dve):
            for phase in phases:
                phase["vector"](dve)

        @block.tensor
        def _(pe):
            for phase in phases:
                phase["tensor"](pe)

        @block.gpsimd
        def _(pool):
            for phase in phases:
                phase["gpsimd"](pool)


def prepare(nc, k, own):
    sb, sem, io = lambda n, s, d=F32: k.sb(n, s, d, own), k.sem, k.io
    cols = {"up": UP_COLS, "dn": D}
    fold = {x: [sb(f"fold_{x}_{i}", [P, 8, cols[x]]) for i in range(2)] for x in cols}
    table = {x: sb(f"table_{x}", [P, PATHS]) for x in cols}
    paths = {x: sb(f"paths_{x}", [P, PATHS]) for x in cols}
    cross = sb("cross", [P, N_CROSS, UP_COLS])
    coef = {x: sb(f"coef_{x}", [P, STAGES - IN_BLOCK, 8, 2]) for x in cols}
    raw_tok = sb("raw_tok", [P, 3, P])
    raw_kv = sb("raw_kv", [P, 512])
    raw_att = sb("raw_att", [P, 4, 2, D])
    raw_out = sb("raw_out", [P, 2, D])
    raw_ew = sb("raw_ew", [P, 2, L])
    raw_mask = sb("raw_mask", [P, 2, L // 4], U32)
    masked_ew = sb("masked_ew", [P, 2, L])
    raw_bq = sb("raw_bq", [P, 1])
    raw_bqk = sb("raw_bqk", [P, 2, 2])
    up_bias = sb("up_bias", [P, 8])
    txt = sb("txt", [P, 4, D])
    txt_stats = sb("txt_stats", [P, 4, 6])
    txt_mv = sb("txt_mv", [P, 4, 2])
    txt_ve = sb("txt_ve", [P, 4])
    txt_rn = sb("txt_rn", [P, 4, 2])

    zeroed = sem("raw_zeroed")
    coef_in = sem("coef_in")
    fold_in = {x: sem(f"fold_in_{x}") for x in cols}
    table_in = {x: sem(f"table_in_{x}") for x in cols}
    path_steps = {x: sem(f"path_steps_{x}") for x in cols}
    block_ps = {x: sem(f"block_ps_{x}") for x in cols}
    crossed = sem("crossed")
    folded = sem("folded")
    tok_in, att_in, out_in, ew_in, small_in, txt_in = (
        sem(x) for x in ("tok_in", "att_in", "out_in", "ew_in", "small_in", "txt_in"))
    split_hi, split_lo = sem("split_hi"), sem("split_lo")
    mask_steps, tri_copied = sem("mask_steps"), sem("tri_copied")
    ew_masked, small_done = sem("ew_masked"), sem("small_done")
    stats_txt, rn_txt, stat_moved = sem("stats_txt"), sem("rn_txt"), sem("stat_moved")
    up_turned, up_hi, up_lo, dn_hi, dn_lo = (
        sem(x) for x in ("up_turned", "up_hi", "up_lo", "dn_hi", "dn_lo"))
    act_done = sem("prep_act_done")

    steps = []
    for i in range(STAGES - IN_BLOCK):
        steps += [("dn", i, STAGES - 1 - i), ("up", i, IN_BLOCK + i)]
    order = {(x, i): n for n, (x, i, _) in enumerate(steps)}
    LAST = STAGES - IN_BLOCK - 1

    def unit(x, i, f):
        return k.psum[:, f, 0:UP_COLS] if x == "up" and i == 0 else fold[x][i % 2][:, f, :]

    with nc.Block() as block:
        @block.sync
        def _(sp):
            sp.dma_start(table["up"][:], io["table_up"]).then_inc(table_in["up"], 16)
            for x in ("dn", "up"):
                sp.dma_start(coef[x][:], io[f"coef_{x}"]).then_inc(coef_in, 16)
            sp.dma_start(fold["dn"][0][:], io["w_con"].rearrange("(f p) c -> p f c", p=P)).then_inc(fold_in["dn"], 16)
            sp.dma_start(fold["up"][0][:], io["w_exp"].rearrange("(f p) c -> p f c", p=P)).then_inc(fold_in["up"], 16)
            sp.dma_start(table["dn"][:], io["table_dn"]).then_inc(table_in["dn"], 16)
            sp.dma_start(k.rows[:], io["rows"].partition_broadcast(P)).then_inc(small_in, 16)
            sp.dma_start(raw_out[:], io["w_out"].rearrange("(a p) n -> p a n", p=P)).then_inc(out_in, 16)
            sp.dma_start(txt[:], io["txt"].rearrange("(t p) d -> p t d", p=P)).then_inc(txt_in, 16)
            for w in range(4):
                sp.dma_start(raw_att[:, w], io["w_att"][w].rearrange("(a p) n -> p a n", p=P)).then_inc(att_in, 16)
            sp.wait_ge(rn_txt, 2)
            for j in range(4):
                sp.dma_start(k.stat_txt[:].rearrange("p (t j) v -> p j t v", j=4)[:, j],
                             txt_rn[LT * j:LT * j + LT]).then_inc(stat_moved, 16)
            sp.wait_ge(stat_moved, 64)

        @block.scalar
        def _(act):
            act.wait_ge(zeroed, 2)
            for j in range(2):
                for w in range(3):
                    act.dma_start(raw_tok[C * j:C * j + C, w, C * j:C * j + C], io["w_tok"][w]).then_inc(tok_in, 16)
            for v in range(2):
                act.dma_start(raw_kv[0:1, :].rearrange("o (a v b c) -> o v a b c", a=2, v=2, b=2)[:, v].rearrange("o a b c -> o a (b c)"),
                              io["b_tok_rows"][1 + v:2 + v]).then_inc(tok_in, 16)
            act.dma_start(raw_bq[:], io["b_tok_q"]).then_inc(tok_in, 16)
            act.dma_start(raw_ew[:], io["ew"].rearrange("(t p) q -> p t q", p=P)).then_inc(ew_in, 16)
            act.dma_start(raw_mask[:], io["mask"].rearrange("(t p) q -> p t q", p=P)).then_inc(ew_in, 16)
            act.dma_start(raw_bqk[:], io["b_qk"]).then_inc(small_in, 16)
            act.dma_start(up_bias[:], io["up_bias"]).then_inc(small_in, 16)
            act.wait_ge(coef_in, 32)
            for n, (x, i, s) in enumerate(steps):
                bit = 1 << (s - IN_BLOCK)
                if x == "dn" and i == 0:
                    act.wait_ge(fold_in[x], 16)
                for f in range(8):
                    if i:
                        act.wait_ge(folded, 8 * order[x, i - 1] + (f ^ bit) + 1)
                    elif x == "up":
                        act.wait_ge(block_ps["up"], (f ^ bit) + 1)
                    wait_since(act, folded, 8 * n + f + 1 - N_CROSS)
                    act.activation(cross[:, f % N_CROSS, 0:cols[x]], unit(x, i, f ^ bit), ACT.Copy,
                                   scale=coef[x][:, s - IN_BLOCK, f, 1:2]).then_inc(crossed, 1)
            act.wait_ge(ew_masked, 1)
            act.activation(k.ew[:], masked_ew[:], ACT.Exp).then_inc(act_done, 1)
            act.wait_ge(block_ps["dn"], 8)
            act.activation(k.w_dn[0][:].rearrange("p f c -> p (f c)"), k.psum[:, 0:4].rearrange("p b c -> p (b c)"),
                           ACT.Copy).then_inc(dn_hi, 1)
            for a in range(2):
                act.wait_ge(up_turned, a + 1)
                act.activation(k.w_up[0][:, a].rearrange("p c q -> p (c q)"),
                               k.psum[:, 4 + 2 * a:6 + 2 * a].rearrange("p b c -> p (b c)"), ACT.Copy).then_inc(up_hi, 1)

        @block.vector
        def _(dve):
            def multiply_paths(x):
                free_in = x == "dn"
                stages = list(range(IN_BLOCK))[::-1] if free_in else list(range(IN_BLOCK))
                dve.wait_ge(table_in[x], 16)
                source, (at, n) = table[x], stage_columns(stages[0], free_in)
                for i, s in enumerate(stages[1:]):
                    to, m = stage_columns(s, free_in)
                    if i:
                        dve.wait_ge(path_steps[x], i)
                    before = source[:, at:at + 8 * n].rearrange("p (f n) -> p f n", f=8)
                    if free_in:
                        before, split = before.unsqueeze(3).broadcast_to([P, 8, n, 2]), "p (f n b) -> p f n b"
                    else:
                        before, split = before.unsqueeze(2).broadcast_to([P, 8, 2, n]), "p (f b n) -> p f b n"
                    dve.tensor_tensor(paths[x][:, to:to + 8 * m].rearrange(split, f=8, b=2), before,
                                      table[x][:, to:to + 8 * m].rearrange(split, f=8, b=2), ALU.mult).then_inc(path_steps[x], 1)
                    source, at, n = paths[x], to, m

            dve.memset(raw_tok[:], 0.0).then_inc(zeroed, 1)
            dve.memset(raw_kv[:], 0.0).then_inc(zeroed, 1)
            dve.memset(k.ones[:].bitcast(F32), 1.0)
            dve.memset(k.half_neg[:], -0.5).then_inc(zeroed, 1)
            multiply_paths("up")
            dve.wait_ge(coef_in, 32)
            for n, (x, i, s) in enumerate(steps):
                if n == 3:
                    dve.wait_ge(ew_in, 32)
                    dve.tensor_tensor(masked_ew[:], raw_ew[:], raw_mask[:].bitcast(U8), ALU.mult).then_inc(ew_masked, 1)
                if n == 4:
                    multiply_paths("dn")
                if n == 5:
                    dve.wait_ge(txt_in, 16)
                    for t in range(4):
                        dve.bn_stats(txt_stats[:, t], txt[:, t]).then_inc(stats_txt, 1)
                    dve.wait_ge(stats_txt, 4)
                    for t in range(4):
                        dve.bn_aggr(txt_mv[:, t], txt_stats[:, t]).then_inc(stats_txt, 1)
                for f in range(8):
                    dve.wait_ge(crossed, 8 * n + (f | 1 if (x, i) == ("up", 0) else f) + 1)
                    if i:
                        dve.wait_ge(folded, 8 * order[x, i - 1] + f + 1)
                    elif x == "up":
                        dve.wait_ge(block_ps["up"], f + 1)
                    dve.scalar_tensor_tensor(
                        out=fold[x][(i + 1) % 2][:, f, :], in0=unit(x, i, f), scalar=coef[x][:, s - IN_BLOCK, f, 0:1],
                        in1=cross[:, f % N_CROSS, 0:cols[x]], op0=ALU.mult, op1=ALU.add).then_inc(folded, 1)
            dve.wait_ge(small_in, 48)
            dve.wait_ge(folded, 8 * (order["up", LAST] + 1))
            dve.tensor_tensor(k.b_gelu[:], fold["up"][(LAST + 1) % 2][:, :, D], up_bias[:], ALU.add).then_inc(dn_lo, 1)
            dve.wait_ge(dn_hi, 1)
            dve.tensor_tensor(k.w_dn[1][:].rearrange("p f c -> p (f c)"), k.psum[:, 0:4].rearrange("p b c -> p (b c)"),
                              k.w_dn[0][:].bitcast(F32).rearrange("p f c -> p (f c)"), ALU.subtract).then_inc(dn_lo, 1)
            for a in range(2):
                dve.wait_ge(up_hi, a + 1)
                flat = lambda w: w[:, a].rearrange("p c q -> p (c q)")
                dve.tensor_tensor(flat(k.w_up[1]), k.psum[:, 4 + 2 * a:6 + 2 * a].rearrange("p b c -> p (b c)"),
                                  flat(k.w_up[0]).bitcast(F32), ALU.subtract).then_inc(up_lo, 1)

        @block.tensor
        def _(pe):
            def through_block(x, f):
                at, n = stage_columns(IN_BLOCK - 1 if x == "up" else 0, x == "dn")
                out = k.psum[:, f, 0:UP_COLS] if x == "up" else k.psum[:, f // 2, D * (f % 2):D * (f % 2) + D]
                pe.matmul(out, paths[x][:, at + n * f:at + n * (f + 1)], fold[x][0 if x == "up" else (LAST + 1) % 2][:, f, :],
                          start=True, stop=True).then_inc(block_ps[x], 1)

            pe.wait_ge(path_steps["up"], IN_BLOCK - 1)
            pe.wait_ge(fold_in["up"], 16)
            for f in range(8):
                through_block("up", f)
            pe.wait_ge(path_steps["dn"], IN_BLOCK - 1)
            pe.wait_ge(folded, 8 * (order["dn", LAST] + 1))
            for f in range(8):
                through_block("dn", f)
            pe.wait_ge(folded, 8 * (order["up", LAST] + 1))
            pe.wait_ge(mask_steps, 2)
            for a in range(2):
                for f in range(8):
                    last = pe.transpose(k.psum[:, 4 + 2 * a + f // 4, P * (f % 4):P * (f % 4) + P],
                                        fold["up"][(LAST + 1) % 2][:, f, P * a:P * a + P], k.ident[:])
                last.then_inc(up_turned, 1)

        @block.gpsimd
        def _(pool):
            pool.memset(k.ident[:], 1.0).then_inc(mask_steps, 1)
            pool.wait_ge(mask_steps, 1)
            pool.affine_select(out=k.ident[:], in_=k.ident[:], compare_op=ALU.is_equal, fill=0.0, base=0,
                               pattern=[[-1, P]], channel_multiplier=1).then_inc(mask_steps, 1)
            pool.memset(k.mask_q[:], 0.0)
            pool.memset(k.keep_txt[:], KEEP).then_inc(mask_steps, 1)
            pool.wait_ge(mask_steps, 3)
            pool.tensor_scalar(k.ident_bf[:], k.ident[:], 1.0, 0.0, ALU.mult, ALU.add).then_inc(mask_steps, 1)
            pool.affine_select(out=k.mask_q[:].rearrange("p (r k) -> p r k", r=4),
                               in_=k.mask_q[:].rearrange("p (r k) -> p r k", r=4), compare_op=ALU.is_ge,
                               fill=MASKED, base=0, pattern=[[0, 4], [-1, P]], channel_multiplier=1).then_inc(mask_steps, 1)
            for j in range(4):
                pool.wait_ge(mask_steps, 5 + j)
                pool.affine_select(out=k.keep_txt[LT * j:LT * j + LT], in_=k.keep_txt[LT * j:LT * j + LT],
                                   compare_op=ALU.is_ge, fill=0.0, base=0, pattern=[[1, LT]],
                                   channel_multiplier=-1).then_inc(mask_steps, 1)
            pool.wait_ge(mask_steps, 9)
            pool.memset(k.mask_txt[:], 0.0).then_inc(tri_copied, 1)
            for j in range(4):
                pool.wait_ge(tri_copied, 1 + j)
                pool.affine_select(out=k.mask_txt[LT * j:LT * j + LT], in_=k.mask_txt[LT * j:LT * j + LT],
                                   compare_op=ALU.is_ge, fill=MASKED, base=0, pattern=[[-1, LT]],
                                   channel_multiplier=1).then_inc(tri_copied, 1)

            def split(hi, lo, raw, n):
                pool.tensor_scalar(hi, raw, 1.0, 0.0, ALU.mult, ALU.add).then_inc(split_hi, 1)
                pool.wait_ge(split_hi, n)
                pool.tensor_tensor(lo, raw, hi.bitcast(F32), ALU.subtract).then_inc(split_lo, 1)

            pool.wait_ge(tri_copied, 5)
            pool.wait_ge(zeroed, 2)
            pool.wait_ge(tok_in, 16 * 9)
            split(k.w_tok[0][:], k.w_tok[1][:], raw_tok[:], 1)
            split(k.b_kv[0][:], k.b_kv[1][:], raw_kv[:], 2)
            pool.wait_ge(out_in, 16)
            split(k.w_out[0][:], k.w_out[1][:], raw_out[:], 3)
            pool.wait_ge(stats_txt, 8)
            pool.wait_ge(zeroed, 3)
            pool.tensor_scalar(txt_ve[:], txt_mv[:, :, 1], 1.0, EPS, ALU.mult, ALU.add).then_inc(small_done, 1)
            pool.tensor_scalar(txt_rn[:, :, 1], txt_mv[:, :, 0], -1.0, 0.0, ALU.mult, ALU.add).then_inc(small_done, 1)
            pool.wait_ge(small_done, 2)
            pool.tensor_tensor(txt_rn[:, :, 0], txt_ve[:], k.half_neg[:, 0:4], ALU.pow).then_inc(rn_txt, 1)
            pool.wait_ge(rn_txt, 1)
            pool.tensor_tensor(txt_rn[:, :, 1], txt_rn[:, :, 1], txt_rn[:, :, 0], ALU.mult).then_inc(rn_txt, 1)
            pool.wait_ge(small_in, 48)
            pool.tensor_scalar(k.b_qk[:, 0], raw_bqk[:, 0], HD ** -0.5, 0.0, ALU.mult, ALU.add)
            pool.tensor_scalar(k.b_qk[:, 1], raw_bqk[:, 1], 1.0, 0.0, ALU.mult, ALU.add).then_inc(small_done, 1)
            pool.tensor_tensor(k.rows[:, 5], k.rows[:, 5], k.rows[:, 6], ALU.add).then_inc(small_done, 1)
            pool.wait_ge(att_in, 64)
            for w in range(4):
                split(k.w_att[0][:, w], k.w_att[1][:, w], raw_att[:, w], 4 + w)
            pool.wait_ge(split_lo, 7)
            pool.tensor_scalar(k.nb_q[:], raw_bq[:], -1.0, 0.0, ALU.mult, ALU.add)


OUT_B, LN_G, LN_B, ATT_BV, ATT_BO, FF_B = range(6)


def mix_tokens(nc, k, own):
    sb, sem, io = lambda n, s, d=F32: k.sb(n, s, d, own), k.sem, k.io
    x_raw = sb("x_raw", [P, 2, 2, L])
    x_hi = sb("x_hi", [P, 2, 2, L], F32R)
    x_lo = sb("x_lo", [P, 2, 2, L], F32R)
    xt_raw = sb("xt_raw", [P, 2, 2, D])
    xtb = sb("xtb", [P, 2, D])
    ek = sb("ek", [P, 2, 2, D])
    ekv = sb("ekv", [P, 2, 2, D])
    eq = sb("eq", [P, 512])
    den = sb("den", [P, 512])
    rec = sb("rec", [P, 512])
    y = sb("y", [P, 2, L])
    y_hi = sb("y_hi", [P, 2, L], F32R)
    y_lo = sb("y_lo", [P, 2, L], F32R)
    h1 = sb("h1", [P, 2, D])
    st1 = sb("st1", [P, 2, 6])
    mv1 = sb("mv1", [P, 2, 2])
    ve1 = sb("ve1", [P, 2])
    rn1 = sb("rn1", [P, 2, 2])
    z = sb("z", [P, 2, D])
    zg = sb("zg", [P, 2, D])
    st2 = sb("st2", [P, 2, 6])
    mv2 = sb("mv2", [P, 2, 2])

    x_loaded = [sem(f"x_loaded{i}") for i in range(2)]
    xt_loaded = [sem(f"xt_loaded{i}") for i in range(2)]
    names = ("x_hi_ready x_lo_ready q_ps kv_ps ek_ready ekv_ready eq_ready nd_ps den_ready rec_ready y_ready "
             "y_hi_ready y_lo_ready out_ps xtb_ready h1_ready st1_ready mv1_ready ve1_ready rstd1_ready rn1_ready "
             "z_ready zg_ready h_ready st2_ready mv2_ready").split()
    s = {n: sem("mix_" + n) for n in names}

    QB, KVB, OUTB = 0, 1, 5
    NUMB, DENB = (3, 6), (4, 7)
    bank = lambda i: k.psum[:, i]

    def row(i):
        return k.rows[:, i].unsqueeze(1).broadcast_to([P, 2, D])

    with nc.Block() as block:
        @block.sync
        def _(sp):
            def step(turn):
                if b := turn.batch(0):
                    wait_since(sp, s["x_lo_ready"], b.n - 1)
                    apart(sp, k.passed_sp)
                    sp.dma_start(x_raw[:, b.parity].rearrange("p a l -> p (a l)"), io["x"][b.n] if b.fixed else
                                 io["x"][bass.ds(b.n, 1)].rearrange("o p c -> (o p) c")).then_inc(x_loaded[b.parity], 16)
                if b := turn.batch(3):
                    wait_since(sp, s["xtb_ready"], b.n - 1)
                    apart(sp, k.passed_sp)
                    src = io["xt"][bass.ds(b.n, 1)].rearrange("o (t p) d -> p (o t) d", p=P)
                    sp.dma_start(xt_raw[:, b.parity], src).then_inc(xt_loaded[b.parity], 16)
            run_steps(sp, step, 6, BATCH, 3)

        @block.scalar
        def _(act):
            def step(turn):
                if b := turn.batch(5):
                    act.wait_ge(s["rn1_ready"], b.n + 1)
                    wait_since(act, s["zg_ready"], b.n)
                    for t in range(2):
                        last = act.activation(z[:, t], h1[:, t], ACT.Identity, bias=rn1[:, t, 1:2], scale=rn1[:, t, 0:1])
                    last.then_inc(s["z_ready"], 1)
                if b := turn.batch(0):
                    act.wait_ge(x_loaded[b.parity], (b.half + 1) * 16)
                    wait_since(act, s["q_ps"], b.n - 1)
                    act.activation(x_hi[:, b.parity], x_raw[:, b.parity], ACT.Copy).then_inc(s["x_hi_ready"], 1)
                if b := turn.batch(1):
                    act.wait_ge(s["kv_ps"], b.n + 1)
                    wait_since(act, s["nd_ps"], b.n - 1)
                    act.activation(ek[:, b.parity].rearrange("p t (a c) -> p t a c", a=2),
                                   k.psum[:, KVB:KVB + 2].rearrange("p t (a v c) -> p t a v c", a=2, v=2)[:, :, :, 0],
                                   ACT.Exp).then_inc(s["ek_ready"], 1)
                if b := turn.batch(2):
                    act.wait_ge(s["q_ps"], b.n + 1)
                    wait_since(act, s["den_ready"], b.n)
                    act.activation(eq[:], bank(QB), ACT.Exp, bias=k.nb_q[:], scale=-1.0).then_inc(s["eq_ready"], 1)
                if b := turn.batch(3):
                    act.wait_ge(s["y_ready"], b.n + 1)
                    wait_since(act, s["out_ps"], b.n)
                    act.activation(y_hi[:], y[:], ACT.Copy).then_inc(s["y_hi_ready"], 1)
            run_steps(act, step, 6, BATCH, 5)

        @block.vector
        def _(dve):
            def step(turn):
                if b := turn.batch(3):
                    dve.wait_ge(s["eq_ready"], b.n + 1)
                    dve.wait_ge(s["nd_ps"], b.n + 1)
                    wait_since(dve, s["rec_ready"], b.n)
                    dve.scalar_tensor_tensor(out=den[:], in0=eq[:], scalar=1.0, in1=bank(DENB[b.parity]),
                                             op0=ALU.add, op1=ALU.mult).then_inc(s["den_ready"], 1)
                    dve.wait_ge(s["den_ready"], b.n + 1)
                    wait_since(dve, s["y_ready"], b.n)
                    dve.reciprocal(rec[:], den[:]).then_inc(s["rec_ready"], 1)
                    dve.wait_ge(s["rec_ready"], b.n + 1)
                    wait_since(dve, s["y_lo_ready"], b.n)
                    dve.tensor_tensor(y[:].rearrange("p a l -> p (a l)"), bank(NUMB[b.parity]), rec[:],
                                      ALU.mult).then_inc(s["y_ready"], 1)
                if b := turn.batch(4):
                    dve.wait_ge(s["out_ps"], b.n + 1)
                    dve.wait_ge(s["xtb_ready"], b.n + 1)
                    wait_since(dve, s["z_ready"], b.n)
                    dve.tensor_tensor(h1[:].rearrange("p t d -> p (t d)"), bank(OUTB),
                                      xtb[:].rearrange("p t d -> p (t d)"), ALU.add).then_inc(s["h1_ready"], 1)
                    dve.wait_ge(s["h1_ready"], b.n + 1)
                    wait_since(dve, s["mv1_ready"], b.n * 2)
                    for t in range(2):
                        dve.bn_stats(st1[:, t], h1[:, t]).then_inc(s["st1_ready"], 1)
                    dve.wait_ge(s["st1_ready"], b.n * 2 + 2)
                    wait_since(dve, s["rn1_ready"], b.n)
                    apart(dve, k.passed_dve)
                    for t in range(2):
                        dve.bn_aggr(mv1[:, t], st1[:, t]).then_inc(s["mv1_ready"], 1)
                if b := turn.batch(1):
                    dve.wait_ge(s["ek_ready"], b.n + 1)
                    dve.tensor_tensor(ekv[:, b.parity].rearrange("p t (a c) -> p t a c", a=2),
                                      k.psum[:, KVB:KVB + 2].rearrange("p t (a v c) -> p t a v c", a=2, v=2)[:, :, :, 1],
                                      ek[:, b.parity].rearrange("p t (a c) -> p t a c", a=2),
                                      ALU.mult).then_inc(s["ekv_ready"], 1)
                if b := turn.batch(5):
                    dve.wait_ge(s["h_ready"], b.n + 1)
                    wait_since(dve, s["mv2_ready"], b.n * 2)
                    for t in range(2):
                        dve.bn_stats(st2[:, t],
                                     k.h_all[:, bass.ds(b.n * 2 + t, 1), :].rearrange("p o d -> p (o d)")).then_inc(s["st2_ready"], 1)
                    dve.wait_ge(s["st2_ready"], b.n * 2 + 2)
                    wait_since(dve, k.stats_kept, b.n)
                    apart(dve, k.passed_dve)
                    for t in range(2):
                        dve.bn_aggr(mv2[:, t], st2[:, t]).then_inc(s["mv2_ready"], 1)
                    dve.wait_ge(s["mv2_ready"], b.n * 2 + 2)
                    dve.tensor_copy(k.mv_all[:, bass.ds(b.n * 2, 2), :], mv2[:]).then_inc(k.stats_kept, 1)
            run_steps(dve, step, 6, BATCH, 5)

        @block.tensor
        def _(pe):
            def step(turn):
                if b := turn.batch(4):
                    pe.wait_ge(s["y_hi_ready"], b.n + 1)
                    pe.wait_ge(s["y_lo_ready"], b.n + 1)
                    wait_since(pe, s["h1_ready"], b.n)
                    for t in range(2):
                        for a in range(2):
                            last = split_product(pe, k.psum[:, OUTB, D * t:D * t + D],
                                                 [v[:, a, P * t:P * t + P] for v in (y_hi, y_lo)],
                                                 [w[:, a] for w in k.w_out], start=a == 0, stop=a == 1)
                    last.then_inc(s["out_ps"], 1)
                if b := turn.batch(2):
                    wait_since(pe, s["eq_ready"], b.n)
                    x = (x_hi[:, b.parity], x_lo[:, b.parity])
                    for a in range(2):
                        last = split_product(pe, k.psum[:, QB, L * a:L * a + L], [w[:, 0] for w in k.w_tok],
                                             [v[:, a] for v in x])
                    last.then_inc(s["q_ps"], 1)
                if b := turn.batch(1):
                    pe.wait_ge(s["x_hi_ready"], b.n + 1)
                    pe.wait_ge(s["x_lo_ready"], b.n + 1)
                    wait_since(pe, s["ekv_ready"], b.n)
                    x = (x_hi[:, b.parity], x_lo[:, b.parity])
                    for t in range(2):
                        pe.matmul(bank(KVB + t), k.ones[:], k.b_kv[0][:], start=True, stop=False)
                        pe.matmul(bank(KVB + t), k.ones[:], k.b_kv[1][:], start=False, stop=False)
                        for a in range(2):
                            last = split_product(pe, k.psum[:, KVB + t, 2 * P * a:2 * P * a + 2 * P],
                                                 [v[:, a, P * t:P * t + P] for v in x],
                                                 [w[:, 1:3].rearrange("p v c -> p (v c)") for w in k.w_tok],
                                                 start=False, stop=a == 1)
                    last.then_inc(s["kv_ps"], 1)
                if b := turn.batch(2):
                    pe.wait_ge(s["ekv_ready"], b.n + 1)
                    wait_since(pe, s["y_ready"], b.n - 1)
                    for src, out in ((ek, DENB[b.parity]), (ekv, NUMB[b.parity])):
                        for a in range(2):
                            for t in range(2):
                                last = pe.matmul(k.psum[:, out, L * a:L * a + L], src[:, b.parity, t, P * a:P * a + P],
                                                 k.ew[:, t], start=t == 0, stop=t == 1)
                    last.then_inc(s["nd_ps"], 1)
            run_steps(pe, step, 6, BATCH, 4)

        @block.gpsimd
        def _(pool):
            def step(turn):
                if b := turn.batch(4):
                    pool.wait_ge(xt_loaded[b.parity], (b.half + 1) * 16)
                    wait_since(pool, s["h1_ready"], b.n)
                    pool.tensor_tensor(xtb[:], xt_raw[:, b.parity], row(OUT_B), ALU.add).then_inc(s["xtb_ready"], 1)
                if b := turn.batch(5):
                    pool.wait_ge(s["z_ready"], b.n + 1)
                    wait_since(pool, s["h_ready"], b.n)
                    pool.tensor_tensor(zg[:], z[:], row(LN_G), ALU.mult).then_inc(s["zg_ready"], 1)
                    pool.wait_ge(s["zg_ready"], b.n + 1)
                    pool.tensor_tensor(k.h_all[:, bass.ds(b.n * 2, 2), :], zg[:], row(LN_B),
                                       ALU.add).then_inc(s["h_ready"], 1)
                if b := turn.batch(0):
                    pool.wait_ge(s["x_hi_ready"], b.n + 1)
                    wait_since(pool, s["q_ps"], b.n - 1)
                    pool.tensor_tensor(x_lo[:, b.parity], x_raw[:, b.parity], x_hi[:, b.parity].bitcast(F32),
                                       ALU.subtract).then_inc(s["x_lo_ready"], 1)
                if b := turn.batch(3):
                    pool.wait_ge(s["y_hi_ready"], b.n + 1)
                    wait_since(pool, s["out_ps"], b.n)
                    pool.tensor_tensor(y_lo[:], y[:], y_hi[:].bitcast(F32), ALU.subtract).then_inc(s["y_lo_ready"], 1)
                if b := turn.batch(4):
                    pool.wait_ge(s["mv1_ready"], b.n * 2 + 2)
                    wait_since(pool, s["z_ready"], b.n)
                    apart(pool, k.passed_pool)
                    pool.tensor_scalar(ve1[:], mv1[:, :, 1], 1.0, EPS, ALU.mult, ALU.add).then_inc(s["ve1_ready"], 1)
                    pool.tensor_scalar(rn1[:, :, 1], mv1[:, :, 0], -1.0, 0.0, ALU.mult, ALU.add)
                    pool.wait_ge(s["ve1_ready"], b.n + 1)
                    pool.tensor_tensor(rn1[:, :, 0], ve1[:], k.half_neg[:, 0:2], ALU.pow).then_inc(s["rstd1_ready"], 1)
                    pool.wait_ge(s["rstd1_ready"], b.n + 1)
                    pool.tensor_tensor(rn1[:, :, 1], rn1[:, :, 1], rn1[:, :, 0], ALU.mult).then_inc(s["rn1_ready"], 1)
            run_steps(pool, step, 6, BATCH, 5)


def attend(nc, k, own):
    sb, sem, io = lambda n, s, d=F32: k.sb(n, s, d, own), k.sem, k.io
    head = [(i % 2) * 8 + i // 2 for i in range(NH)]
    q_st = [sb(f"q_st{i}", [SR + NPARTS, NH, S], BF16) for i in range(2)]
    k_st = [sb(f"k_st{i}", [SR + NPARTS, NH, S], BF16) for i in range(2)]
    qk = sb("qk", [P, 2, 2, S])
    qk_rest = sb("qk_rest", [P, 2, 2, S])
    parts = sb("parts", [P, NPARTS, 2, 2 * S], BF16)
    prob = sb("prob", [P, HSLOTS, W_KT1 + S])
    txt_in = sb("txt_in", [LT, D])
    txt_res = sb("txt_res", [LT, D])
    xn = sb("xn", [P, 3, D])
    xt_hi = [sb(f"xt_hi{i}", [P, 2, S], F32R) for i in range(2)]
    xt_lo = [sb(f"xt_lo{i}", [P, 2, S], F32R) for i in range(2)]
    xt_txt4 = [[sb(f"xt_txt4_{x}{i}", [P, 2, 4, LT], F32R) for x in ("hi", "lo")] for i in range(2)]
    v_aug = [sb(f"v_aug{i}", [P, 3, NH, 2 * HD]) for i in range(2)]
    prob_txt = sb("prob_txt", [P, GROUPS, LT])
    nmax = sb("nmax", [P, M_COLS])
    nmax_rest = sb("nmax_rest", [P, M_COLS])
    mparts = sb("mparts", [P, NPARTS, M_COLS], BF16)
    ve = sb("ve", [P, IMG_TILES])
    mrow = sb("mrow", [NPARTS * M_COLS, P], BF16)
    ctx_u = sb("ctx_u", [P, GROUPS, S])
    rsum = sb("rsum", [P, 3, NH])
    ctx_n = sb("ctx_n", [P, 3, D])
    ct_hi = sb("ct_hi", [P, 2, S], F32R)
    ct_lo = sb("ct_lo", [P, 2, S], F32R)
    hb = sb("hb", [P, 2, D])
    hb_txt = sb("hb_txt", [LT, D])
    h_txt = sb("h_txt", [LT, D])

    names = ("txt_loaded res_loaded xn_ready xnT_ps xnT_hi xnT_lo q_ps k_ps v_ps qk_ready part_h rest_h part_m rest_m "
             "parts_ready v_ready m0_ps m1_ps mt_ps m0_max m1_max mt_max mp_h mr_h mp_m mr_m mp_ready mT_ps mT_ready "
             "mrow_stored st_ps stt_ps exp_done expt_done "
             "seen keep_done ctx_ps ctx_u_done o1_ps rsum_ready ctxn_ready ctxT_ps ctxT_hi ctxT_lo o_ps hb_ready "
             "h_txt_stored ones_set ve_ready rstd_ready stat_ready").split()
    s = {n: sem("att_" + n) for n in names}
    parts_stored = [sem(f"att_parts_stored{i}") for i in range(2)]
    stack_loaded = [sem(f"att_stack_loaded{i}") for i in range(2)]
    mrow_loaded = [sem(f"att_mrow_loaded{i}") for i in range(2)]
    N_STORE, N_STACK = 2 * NPARTS, 6
    bank = lambda i: k.psum[:, i]
    turned_maxima = k.psum[:, 3].bitcast(BF16)[0:NPARTS * M_COLS, 512 + P:512 + 2 * P]

    def ends(b):
        return b and b.fixed and b.n == BATCH - 1

    def guard_feed(eng):
        eng.wait_ge(s["st_ps"], BATCH * NH)

    def sync(sp):
        def step(turn):
            if b := turn.batch(0):
                wait_since(sp, s["xn_ready"], b.n)
                apart(sp, k.passed_sp)
                wait_since(sp, s["txt_loaded"], b.n * 16)
                apart(sp, k.passed_sp)
                sp.dma_start(txt_in[:], io["txt"][bass.ds(b.n * LT, LT), :]).then_inc(s["txt_loaded"], 16)
            if b := turn.batch(4):
                wait_since(sp, s["hb_ready"], b.n)
                apart(sp, k.passed_sp)
                wait_since(sp, s["res_loaded"], b.n * 16)
                apart(sp, k.passed_sp)
                sp.dma_start(txt_res[:], io["txt"][bass.ds(b.n * LT, LT), :]).then_inc(s["res_loaded"], 16)
            if b := turn.batch(3):
                u = b.parity
                sp.wait_ge(s["mT_ready"], b.n + 1)
                sp.dma_start(k.mrow_dram[u].rearrange("r c q -> (r c) q"), mrow[:]).then_inc(s["mrow_stored"], 16)
                sp.wait_ge(s["mrow_stored"], b.n * 16 + 16)
                for t in range(2):
                    sp.dma_start(q_st[u][SR:SR + NPARTS, :, P * t:P * t + P],
                                 k.mrow_dram[u, :, NH * t:NH * t + NH]).then_inc(mrow_loaded[u], 16)
                sp.dma_start(q_st[u][SR:SR + NPARTS, :, L:S],
                             k.mrow_dram[u, :, 2 * NH:].rearrange("r g (j q) -> r (g j) q", j=4)).then_inc(mrow_loaded[u], 16)
            if b := turn.batch(1):
                u = b.parity
                wait_since(sp, stack_loaded[u], b.half * (16 * N_STACK))
                for r, ready in enumerate(("part_h", "part_m", "parts_ready")):
                    apart(sp, k.passed_sp)
                    sp.wait_ge(s[ready], b.n + 1)
                    for x in range(2):
                        sp.dma_start(k.parts_dram[u, x, r].rearrange("d a q -> a d q"),
                                     parts[:, r, x]).then_inc(parts_stored[u], 16)
                apart(sp, k.passed_sp)
                sp.wait_ge(parts_stored[u], (b.half + 1) * (16 * N_STORE))
                apart(sp, k.passed_sp)
                wait_since(sp, s["st_ps"], (b.n - 1) * NH)
                for first, n in ((0, 3), (3, 2), (5, 1)):
                    to = slice(HD * first, HD * (first + n))
                    sp.dma_start(k_st[u][to], k.parts_dram[u, 1, 0:n].rearrange("r d a q -> (r d) (a q)")
                                 ).then_inc(stack_loaded[u], 16)
                    part = k.parts_dram[u, 0, 3 - n].rearrange("d a q -> d (a q)")
                    sp.dma_start(q_st[u][to], part.unsqueeze(0).broadcast_to([n, HD, 8 * 2 * S])
                                 ).then_inc(stack_loaded[u], 16)
            if b := turn.batch(4):
                sp.wait_ge(k.h_done, b.n + 1)
                apart(sp, k.passed_sp)
                sp.dma_start(k.h_txt_dram[bass.ds(b.n * LT, LT), :], h_txt[:]).then_inc(s["h_txt_stored"], 16)
        run_steps(sp, step, 6, BATCH, 4)
        sp.wait_ge(s["h_txt_stored"], BATCH * 16)

    def scalar(act):
        def normalise(b):
            act.wait_ge(s["stat_ready"], 1 if b.fixed and b.n < 2 else 2)
            act.wait_ge(s["txt_loaded"], b.n * 16 + 16)
            wait_since(act, s["xnT_ps"], b.n)
            for t in range(2):
                act.activation(xn[:, t], k.h_all[:, bass.ds(b.n * 2 + t, 1), :].rearrange("p o d -> p (o d)"), ACT.Identity,
                               bias=k.stat_img[:, bass.ds(b.n * 2 + t, 1), 1], scale=k.stat_img[:, bass.ds(b.n * 2 + t, 1), 0])
            act.activation(xn[0:LT, 2], txt_in[:], ACT.Identity, bias=k.stat_txt[:, bass.ds(b.n, 1), 1],
                           scale=k.stat_txt[:, bass.ds(b.n, 1), 0]).then_inc(s["xn_ready"], 1)

        def round_xt(b):
            act.wait_ge(s["xnT_ps"], b.n + 1)
            wait_since(act, s["v_ps"], b.n - 1)
            act.activation(xt_hi[b.parity][:], k.psum[:, 0:2, 0:S], ACT.Copy).then_inc(s["xnT_hi"], 1)

        def leave_qk(b):
            for x, base, ps, scale in ((0, 0, "q_ps", HD ** -0.5), (1, 4, "k_ps", 1.0)):
                act.wait_ge(s[ps], b.n + 1)
                if x == 0:
                    wait_since(act, s["parts_ready"], b.n)
                for a in range(2):
                    last = act.activation(qk[:, x, a], k.psum[:, base + a, 0:S], ACT.Identity,
                                          bias=k.b_qk[:, x, a:a + 1], scale=scale)
            last.then_inc(s["qk_ready"], 1)
            act.wait_ge(s["qk_ready"], b.n + 1)
            if b.parity:
                act.wait_ge(parts_stored[0], (b.half + 1) * (16 * N_STORE))
            else:
                wait_since(act, parts_stored[1], b.half * (16 * N_STORE))
            act.activation(parts[:, 0].rearrange("p x q -> p (x q)"), qk[:].rearrange("p x a q -> p (x a q)"),
                           ACT.Copy).then_inc(s["part_h"], 1)

        def round_ct(b):
            act.wait_ge(s["ctxT_ps"], b.n + 1)
            wait_since(act, s["o_ps"], b.n)
            act.activation(ct_hi[:], k.psum[:, 2:4, 0:S], ACT.Copy).then_inc(s["ctxT_hi"], 1)

        def exps(b, g):
            if g == 0:
                act.wait_ge(s["stt_ps"], b.n + 1)
                wait_since(act, s["ctx_ps"], b.n * GROUPS)
                act.activation(prob_txt[:].rearrange("p g q -> p (g q)"), k.psum[:, 7, 0:GROUPS * LT],
                               ACT.Exp).then_inc(s["expt_done"], 1)
            wait_since(act, s["ctx_ps"], b.n * GROUPS + (g - 1))
            for j in range(4):
                i = 4 * g + j
                act.wait_ge(s["st_ps"], b.n * NH + (i + 1))
                act.activation(prob[:, i % HSLOTS], k.psum[:, 4 + i % 2, 0:W_KT1 + S], ACT.Exp).then_inc(s["exp_done"], 1)

        def leave_ctx(b, g):
            act.wait_ge(s["ctx_ps"], b.n * GROUPS + (g + 1))
            wait_since(act, s["o1_ps"], b.n)
            act.activation(ctx_u[:, g], k.psum[:, 6, 0:S], ACT.Copy).then_inc(s["ctx_u_done"], 1)

        def step(turn):
            if b := turn.batch(1):
                round_xt(b)
            b = turn.batch(4)
            if ends(b):
                guard_feed(act)
                k.feed_first["normalise"](act)
            if b:
                round_ct(b)
            if ends(b):
                k.feed_first["round_xt"](act)
            if b := turn.batch(1):
                leave_qk(b)
            probs_b, next_b = turn.batch(3), turn.batch(0)
            for g in range(GROUPS):
                if probs_b:
                    exps(probs_b, g)
                    if g:
                        leave_ctx(probs_b, g - 1)
            if next_b:
                normalise(next_b)
            if probs_b:
                leave_ctx(probs_b, GROUPS - 1)
        run_steps(act, step, 6, BATCH, 4)

    def vector(dve):
        for i in range(2):
            dve.memset(v_aug[i][:, :, :, HD:], 1.0).then_inc(s["ones_set"], 1)

        def normalise_ctx(b):
            dve.wait_ge(s["o1_ps"], b.n + 1)
            for t, ps, n in ((0, 4, P), (1, 5, P), (2, 7, LT)):
                src = k.psum[0:n, ps].rearrange("p (h c) -> p h c", c=2 * HD)
                if t == 0:
                    wait_since(dve, s["ctxn_ready"], b.n * 3)
                    wait_since(dve, s["ctxT_ps"], b.n)
                dve.reciprocal(rsum[0:n, t], src[:, :, HD]).then_inc(s["rsum_ready"], 1)
            for t, ps, n in ((0, 4, P), (1, 5, P), (2, 7, LT)):
                src = k.psum[0:n, ps].rearrange("p (a x c) -> p a x c", a=8, x=2)
                dve.wait_ge(s["rsum_ready"], b.n * 3 + (t + 1))
                dve.tensor_tensor(ctx_n[0:n, t].rearrange("p (x a c) -> p a x c", x=2, a=8), src[:, :, :, 0:HD],
                                  rsum[0:n, t].rearrange("p (a x) -> p a x", a=8).unsqueeze(3).broadcast_to([n, 8, 2, HD]),
                                  ALU.mult).then_inc(s["ctxn_ready"], 1)

        def leave_mrow(b):
            dve.wait_ge(s["mT_ps"], b.n + 1)
            wait_since(dve, s["mrow_stored"], b.n * 16)
            dve.tensor_copy(mrow[:], turned_maxima).then_inc(s["mT_ready"], 1)

        def rest_xt(b):
            dve.wait_ge(s["xnT_hi"], b.n + 1)
            wait_since(dve, s["v_ps"], b.n - 1)
            hi, lo = xt_hi[b.parity], xt_lo[b.parity]
            dve.tensor_tensor(lo[:], k.psum[:, 0:2, 0:S], hi[:].bitcast(F32), ALU.subtract).then_inc(s["xnT_lo"], 1)
            dve.wait_ge(s["xnT_lo"], b.n * 3 + 1)
            for dst, src in zip(xt_txt4[b.parity], (hi, lo)):
                dve.tensor_copy(dst[:], src[:, :, L:S].bitcast(F32).unsqueeze(2).broadcast_to([P, 2, 4, LT])).then_inc(s["xnT_lo"], 1)

        def rest_ct(b):
            dve.wait_ge(s["ctxT_hi"], b.n + 1)
            wait_since(dve, s["o_ps"], b.n)
            dve.tensor_tensor(ct_lo[:], k.psum[:, 2:4, 0:S], ct_hi[:].bitcast(F32), ALU.subtract).then_inc(s["ctxT_lo"], 1)

        def leave_v(b):
            dve.wait_ge(s["v_ps"], b.n + 1)
            wait_since(dve, s["ctx_ps"], (b.n - 1) * GROUPS)
            if b.fixed and b.n < 2:
                dve.wait_ge(s["ones_set"], 4)
            out = v_aug[b.parity]
            bias = k.rows[:, ATT_BV].rearrange("p (h c) -> p h c", h=NH)
            dve.tensor_tensor(out[:, 0:2, :, 0:HD], k.psum[:, 6].rearrange("p (t h c) -> p t h c", t=2, h=NH),
                              bias.unsqueeze(1).broadcast_to([P, 2, NH, HD]), ALU.add)
            dve.tensor_tensor(out[:, 2, :, 0:HD], k.psum[:, 7, 0:D].rearrange("p (h c) -> p h c", h=NH),
                              bias, ALU.add).then_inc(s["v_ready"], 1)

        def split3(b, half):
            flat = lambda t: t[:].rearrange("p x a q -> p (x a q)")
            part = lambda i: parts[:, i].rearrange("p x q -> p (x q)")
            if half == 0:
                dve.wait_ge(s["part_h"], b.n + 1)
                wait_since(dve, s["parts_ready"], b.n)
                dve.tensor_tensor(flat(qk_rest), flat(qk), part(0), ALU.subtract).then_inc(s["rest_h"], 1)
            else:
                dve.wait_ge(s["rest_h"], b.n + 1)
                dve.tensor_copy(part(1), flat(qk_rest)).then_inc(s["part_m"], 1)
                dve.wait_ge(s["part_m"], b.n + 1)
                dve.tensor_tensor(part(2), flat(qk_rest), part(1), ALU.subtract).then_inc(s["parts_ready"], 1)

        def add_residual(b):
            dve.wait_ge(s["o_ps"], b.n + 1)
            dve.wait_ge(s["hb_ready"], b.n + 1)
            wait_since(dve, s["h_txt_stored"], b.n * 16)
            dve.tensor_tensor(k.h_all[:, bass.ds(b.n * 2, 2), :], k.psum[:, 2].rearrange("p (t d) -> p t d", t=2),
                              hb[:], ALU.add)
            dve.tensor_tensor(h_txt[:], k.psum[0:LT, 3, 0:D], hb_txt[:], ALU.add).then_inc(k.h_done, 1)

        def maxima(b, g):
            if g == 0:
                wait_since(dve, s["mp_ready"], b.n)
            dve.wait_ge(s["m0_ps"], b.n * GROUPS + (g + 1))
            dve.tensor_reduce(nmax[:, 4 * g:4 * g + 4], k.psum[:, 0].rearrange("p (h c) -> p h c", h=4), AX_X, ALU.max,
                              negate=True).then_inc(s["m0_max"], 1)
            dve.wait_ge(s["m1_ps"], b.n * GROUPS + (g + 1))
            dve.tensor_reduce(nmax[:, NH + 4 * g:NH + 4 * g + 4], k.psum[:, 1:3].rearrange("p t (h c) -> p (t h) c", h=2),
                              AX_X, ALU.max, negate=True).then_inc(s["m1_max"], 1)
            dve.wait_ge(s["mt_ps"], b.n * GROUPS + (g + 1))
            dve.tensor_reduce(nmax[:, 2 * NH + g:2 * NH + g + 1], k.psum[:, 3, 0:S], AX_X, ALU.max,
                              negate=True).then_inc(s["mt_max"], 1)

        def split_maxima(b):
            n = b.n
            dve.wait_ge(s["mt_max"], n * GROUPS + GROUPS)
            wait_since(dve, s["mT_ps"], n)
            dve.tensor_copy(mparts[:, 0], nmax[:]).then_inc(s["mp_h"], 1)
            dve.wait_ge(s["mp_h"], n + 1)
            dve.tensor_tensor(nmax_rest[:], nmax[:], mparts[:, 0], ALU.subtract).then_inc(s["mr_h"], 1)
            dve.wait_ge(s["mr_h"], n + 1)
            dve.tensor_copy(mparts[:, 1], nmax_rest[:]).then_inc(s["mp_m"], 1)
            dve.wait_ge(s["mp_m"], n + 1)
            dve.tensor_tensor(mparts[:, 2], nmax_rest[:], mparts[:, 1], ALU.subtract).then_inc(s["mp_ready"], 1)

        def limit_txt(b):
            dve.wait_ge(s["expt_done"], b.n + 1)
            dve.tensor_tensor(prob_txt[:], prob_txt[:], k.keep_txt[:].unsqueeze(1).broadcast_to([P, GROUPS, LT]),
                              ALU.min).then_inc(s["keep_done"], 1)

        def step(turn):
            own_b, max_b, probs_b, out_b = (turn.batch(lag) for lag in (1, 2, 3, 4))
            if probs_b:
                leave_mrow(probs_b)
            if own_b:
                rest_xt(own_b)
            if ends(out_b):
                guard_feed(dve)
                k.feed_first["stats"](dve)
            if out_b:
                normalise_ctx(out_b)
                rest_ct(out_b)
            if ends(out_b):
                k.feed_first["rest_xt"](dve)
            if max_b:
                leave_v(max_b)
            if out_b:
                add_residual(out_b)
            if probs_b:
                limit_txt(probs_b)
            for g in range(GROUPS):
                if max_b:
                    maxima(max_b, g)
                if g < 2 and own_b:
                    split3(own_b, g)
            if max_b:
                split_maxima(max_b)
        run_steps(dve, step, 6, BATCH, 4)

    def tensor(pe):
        w = lambda i, a, half: [v[:, i, a, P * half:P * half + P] for v in k.w_att]

        def turn_maxima(b):
            pe.wait_ge(s["mp_ready"], b.n + 1)
            pe.transpose(turned_maxima, mparts[:].rearrange("p r c -> p (r c)"),
                         k.ident_bf[:]).then_inc(s["mT_ps"], 1)

        def turn_ctx(b):
            pe.wait_ge(s["ctx_u_done"], b.n * GROUPS + GROUPS)
            pe.wait_ge(s["exp_done"], b.n * NH + NH)
            pe.wait_ge(s["expt_done"], b.n + 1)
            for t, ps, n in ((0, 4, P), (1, 5, P), (2, 7, LT)):
                for g in range(GROUPS):
                    last = pe.transpose(k.psum[0:n, ps, P * g:P * g + P], ctx_u[:, g, P * t:P * t + n], k.ident[:])
            last.then_inc(s["o1_ps"], 1)

        def turn_xn(b):
            pe.wait_ge(s["xn_ready"], b.n + 1)
            wait_since(pe, s["m1_max"], (b.n - 1) * GROUPS)
            for a in range(2):
                for t, n in ((0, P), (1, P), (2, LT)):
                    last = pe.transpose(k.psum[:, a, P * t:P * t + n], xn[0:n, t, P * a:P * a + P], k.ident[0:n, 0:n])
            last.then_inc(s["xnT_ps"], 1)

        def turn_ctxn(b):
            pe.wait_ge(s["ctxn_ready"], b.n * 3 + 3)
            if b.fixed and b.n >= BATCH - 1:
                pe.wait_ge(s["mt_max"], BATCH * GROUPS)
            else:
                pe.wait_ge(s["mt_max"], (b.n + 2) * GROUPS)
            for a in range(2):
                for t, n in ((0, P), (1, P), (2, LT)):
                    last = pe.transpose(k.psum[:, 2 + a, P * t:P * t + n], ctx_n[0:n, t, P * a:P * a + P], k.ident[0:n, 0:n])
            last.then_inc(s["ctxT_ps"], 1)

        def project_qk(b, x):
            xt = (xt_hi[b.parity], xt_lo[b.parity])
            if x == 0:
                pe.wait_ge(s["xnT_lo"], b.n * 3 + 1)
            else:
                wait_since(pe, s["ctxn_ready"], (b.n - 2) * 3)
            for half in range(2):
                for a in range(2):
                    last = split_product(pe, k.psum[:, 4 * x + half, 0:S], w(x, a, half), [v[:, a] for v in xt],
                                         start=a == 0, stop=a == 1)
            last.then_inc(s[("q_ps", "k_ps")[x]], 1)

        def project_v(b):
            xt = (xt_hi[b.parity], xt_lo[b.parity])
            wait_since(pe, s["ctx_u_done"], (b.n - 1) * GROUPS)
            for t in range(2):
                for a in range(2):
                    split_product(pe, k.psum[:, 6, D * t:D * t + D], [v[:, a, P * t:P * t + P] for v in xt],
                                  [v[:, 2, a] for v in k.w_att], start=a == 0, stop=a == 1)

        def project_v_txt(b):
            wait_since(pe, s["ctxn_ready"], (b.n - 1) * 3)
            pe.wait_ge(s["xnT_lo"], b.n * 3 + 3)
            for a in range(2):
                last = split_product(pe, k.psum[:, 7, 0:D], [v[:, a].rearrange("p r q -> p (r q)") for v in xt_txt4[b.parity]],
                                     [v[:, 2, a] for v in k.w_att], start=a == 0, stop=a == 1)
            last.then_inc(s["v_ps"], 1)

        def project_out(b):
            ct = (ct_hi, ct_lo)
            pe.wait_ge(s["ctxT_lo"], b.n + 1)
            for t, ps, n in ((0, 2, P), (1, 2, P), (2, 3, LT)):
                out = k.psum[0:n, ps, D * (t % 2):D * (t % 2) + D]
                for a in range(2):
                    last = split_product(pe, out, [v[:, a, P * t:P * t + n] for v in ct],
                                         [v[:, 3, a] for v in k.w_att], start=a == 0, stop=a == 1)
            last.then_inc(s["o_ps"], 1)

        def scores_for_max(b, g, which):
            q, kk = q_st[b.parity], k_st[b.parity]
            heads = range(4 * g, 4 * g + 4)
            if which == 0:
                if g == 0:
                    pe.wait_ge(stack_loaded[b.parity], (b.half + 1) * (16 * N_STACK))
                    pe.wait_ge(s["qk_ready"], BATCH if b.fixed and b.n == BATCH - 1 else b.n + 2)
                wait_since(pe, s["m0_max"], b.n * GROUPS + g)
                pe.matmul(bank(0), k.ident_bf[:], k.mask_q[:], start=True, stop=False, skip_group_check=True)
                for j, h in enumerate(heads):
                    last = pe.matmul(k.psum[:, 0, P * j:P * j + P], q[0:SR, h, 0:P], kk[0:SR, h, 0:P], start=False,
                                     stop=True, skip_group_check=True)
                last.then_inc(s["m0_ps"], 1)
            elif which == 1:
                if g == 0:
                    wait_since(pe, k.h_done, b.n - 1)
                wait_since(pe, s["m1_max"], b.n * GROUPS + g)
                for c in range(2):
                    pe.matmul(k.psum[:, 1 + c].rearrange("p (h c) -> p h c", h=2)[:, :, P:L], k.ident_bf[:],
                              k.mask_q[:, 0:L].rearrange("p (h c) -> p h c", h=2), start=True, stop=False,
                              skip_group_check=True)
                    for j in range(2):
                        h = heads[2 * c + j]
                        last = pe.matmul(k.psum[:, 1 + c, L * j:L * j + L], q[0:SR, h, P:L], kk[0:SR, h, 0:L], start=False,
                                         stop=True, skip_group_check=True)
                last.then_inc(s["m1_ps"], 1)
            else:
                wait_since(pe, s["mt_max"], b.n * GROUPS + g)
                pe.matmul(k.psum[:, 3, L:S], k.ident_bf[:], k.mask_txt[:], start=True, stop=False, skip_group_check=True)
                for j, h in enumerate(heads):
                    last = pe.matmul(k.psum[LT * j:LT * j + LT, 3, 0:S], q[0:SR, h, L:S], kk[0:SR, h, 0:S], start=False,
                                     stop=True, skip_group_check=True)
                last.then_inc(s["mt_ps"], 1)

        def scores_transposed(b, pair):
            q, kk = q_st[b.parity], k_st[b.parity]
            rows = slice(0, SR + NPARTS)
            if pair == 0:
                pe.wait_ge(mrow_loaded[b.parity], (b.half + 1) * 48)
                pe.wait_ge(s["v_ready"], min(b.n + 2, BATCH) if b.fixed else b.n + 2)
                pe.wait_ge(s["qk_ready"], min(b.n + 3, BATCH) if b.fixed else b.n + 3)
                for h in range(NH):
                    j = h % 4
                    last = pe.matmul(k.psum[LT * j:LT * j + LT, 7, LT * (h // 4):LT * (h // 4) + LT],
                                     kk[rows, h, L:S], q[rows, h, L:S], start=True, stop=True)
                last.then_inc(s["stt_ps"], 1)
            for h in (2 * pair, 2 * pair + 1):
                wait_since(pe, s["exp_done"], b.n * NH + (h - 1))
                pe.matmul(k.psum[:, 4 + h % 2, 0:W_KT1], kk[rows, h, P:L], q[rows, h, P:S], start=True, stop=True)
                pe.matmul(k.psum[:, 4 + h % 2, W_KT1:W_KT1 + S], kk[rows, h, 0:P], q[rows, h, 0:S], start=True,
                          stop=True).then_inc(s["st_ps"], 1)

        def weigh_values(b, g):
            v = v_aug[b.parity]
            pe.wait_ge(s["seen"], b.n * NH + (4 * g + 4))
            wait_since(pe, s["ctx_u_done"], b.n * GROUPS + g)
            pe.wait_ge(s["keep_done"], b.n + 1)
            for j in range(4):
                h = 4 * g + j
                pe.matmul(k.psum[LT * j:LT * j + LT, 6, 0:S], v[:, 0, head[h]], prob[:, h % HSLOTS, W_KT1:], start=True,
                          stop=False)
            for j in range(4):
                h = 4 * g + j
                pe.matmul(k.psum[LT * j:LT * j + LT, 6, P:S], v[:, 1, head[h]], prob[:, h % HSLOTS, 0:W_KT1], start=False,
                          stop=False)
            for j in range(4):
                h = 4 * g + j
                last = pe.matmul(k.psum[LT * j:LT * j + LT, 6, L:S], v[LT * j:LT * j + LT, 2, head[h]],
                                 prob_txt[LT * j:LT * j + LT, g], start=False, stop=True)
            last.then_inc(s["ctx_ps"], 1)

        def step(turn):
            own_b, max_b, probs_b, out_b = (turn.batch(lag) for lag in (1, 2, 3, 4))
            if own_b:
                turn_xn(own_b)
            if probs_b:
                turn_maxima(probs_b)
            if out_b:
                turn_ctx(out_b)
            if max_b:
                project_v(max_b)
            if own_b:
                project_qk(own_b, 0)
            if max_b:
                project_v_txt(max_b)
            if out_b:
                turn_ctxn(out_b)
            if ends(out_b):
                pe.wait_ge(s["m1_max"], BATCH * GROUPS)
                k.feed_first["turn_xn"](pe)
            if own_b:
                project_qk(own_b, 1)
            if out_b:
                project_out(out_b)
            for what, i in ORDER:
                if what == "scores" and probs_b:
                    scores_transposed(probs_b, i)
                if what == "values" and probs_b:
                    weigh_values(probs_b, i)
                if what == "maxima" and max_b:
                    scores_for_max(max_b, i // 3, i % 3)
        run_steps(pe, step, 6, BATCH, 4)

    def gpsimd(pool):
        pool.wait_ge(k.stats_kept, BATCH)
        for i, tiles in enumerate((slice(0, 4), slice(4, IMG_TILES))):
            n = tiles.stop - tiles.start
            pool.tensor_scalar(k.stat_img[:, tiles, 1], k.mv_all[:, tiles, 0], -1.0, 0.0, ALU.mult, ALU.add)
            pool.tensor_scalar(ve[:, tiles], k.mv_all[:, tiles, 1], 1.0, EPS, ALU.mult, ALU.add).then_inc(s["ve_ready"], 1)
            pool.wait_ge(s["ve_ready"], i + 1)
            pool.tensor_tensor(k.stat_img[:, tiles, 0], ve[:, tiles], k.half_neg[:, 0:n], ALU.pow).then_inc(s["rstd_ready"], 1)
            pool.wait_ge(s["rstd_ready"], i + 1)
            pool.tensor_tensor(k.stat_img[:, tiles, 1], k.stat_img[:, tiles, 1], k.stat_img[:, tiles, 0],
                               ALU.mult).then_inc(s["stat_ready"], 1)
        for i in range(2):
            pool.wait_ge(s["stat_ready"], 2)
            if i:
                pool.wait_ge(s["ones_set"], 3)
            pool.memset(k_st[i][SR:SR + NPARTS], 1.0).then_inc(s["ones_set"], 1)
        pool.wait_ge(s["ones_set"], 4)

        def step(turn):
            if b := turn.batch(4):
                pool.wait_ge(s["res_loaded"], b.n * 16 + 16)
                wait_since(pool, k.h_done, b.n)
                pool.tensor_tensor(hb[:], k.h_all[:, bass.ds(b.n * 2, 2), :],
                                   k.rows[:, ATT_BO].unsqueeze(1).broadcast_to([P, 2, D]), ALU.add)
                pool.tensor_tensor(hb_txt[:], txt_res[:], k.rows[0:LT, ATT_BO], ALU.add).then_inc(s["hb_ready"], 1)
                if ends(b):
                    guard_feed(pool)
                    k.feed_first["moments"](pool)
            if b := turn.batch(3):
                for h in range(NH):
                    pool.wait_ge(s["exp_done"], b.n * NH + (h + 1))
                    apart(pool, k.passed_pool)
                    v = prob[:, h % HSLOTS, 0:2 * W_KT1].rearrange("p (t q) -> p t q", t=2)[:, :, 0:P]
                    pool.affine_select(out=v, in_=v, compare_op=ALU.is_ge, fill=0.0, base=0, pattern=[[0, 2], [1, P]],
                                       channel_multiplier=-1).then_inc(s["seen"], 1)
        run_steps(pool, step, 6, BATCH, 4)

    return {"sync": sync, "scalar": scalar, "vector": vector, "tensor": tensor, "gpsimd": gpsimd}


ORDER = []
for _g in range(GROUPS):
    ORDER += [("scores", 2 * _g), ("maxima", 3 * _g), ("scores", 2 * _g + 1), ("maxima", 3 * _g + 1)]
    ORDER += [("values", _g - 1)] if _g else []
    ORDER += [("maxima", 3 * _g + 2)]
ORDER += [("values", GROUPS - 1)]


STATS_AT, NORMALISE_AT, TURN_AT = 0, 2, 5


def feed_forward(nc, k, own):
    sb, sem, io = lambda n, s, d=F32: k.sb(n, s, d, own), k.sem, k.io
    T = FF_TOK // P
    st = sb("ff_st", [P, T, 6])
    mv = sb("ff_mv", [P, T, 2])
    ve = sb("ff_ve", [P, T])
    rn = sb("ff_rn", [P, T, 2])
    xn = sb("ff_xn", [P, T, D])
    xt = [[sb(f"ff_xt_{x}{i}", [P, 2, FF_TOK], F32R) for x in ("hi", "lo")] for i in range(2)]
    g = sb("ff_g", [P, 2, FF_TOK])
    g_hi = sb("ff_g_hi", [P, 2, FF_TOK], F32R)
    g_lo = sb("ff_g_lo", [P, 2, FF_TOK], F32R)
    hb = sb("ff_hb", [P, 2, T, D])
    out = sb("ff_out", [P, 2, T, D])
    names = ("txt_in st_ready mv_ready ve_ready rstd_ready rn_ready xn_ready xnT_ps xnT_hi xnT_lo u_ps g_ready g_hi g_lo "
             "y_ps hb_ready out_ready").split()
    s = {n: sem("ff_" + n) for n in names}
    stored = [sem(f"ff_stored{i}") for i in range(2)]
    XT, UB, YB = (0, 1), (4, 5), ((6, 7), (2, 3))

    def stats(dve, b):
        if b.fixed and b.n == 2:
            dve.wait_ge(s["txt_in"], 16)
        wait_since(dve, s["mv_ready"], b.n * T)
        for t in range(T):
            dve.bn_stats(st[:, t], k.h_all[:, bass.ds(b.n * T + t, 1), :].rearrange("p o d -> p (o d)")).then_inc(s["st_ready"], 1)
        dve.wait_ge(s["st_ready"], b.n * T + T)
        wait_since(dve, s["rn_ready"], b.n)
        apart(dve, k.passed_dve)
        for t in range(T):
            dve.bn_aggr(mv[:, t], st[:, t]).then_inc(s["mv_ready"], 1)

    def rest_xt(dve, b):
        for a in range(2):
            dve.wait_ge(s["xnT_hi"], b.n * 2 + (a + 1))
            wait_since(dve, s["u_ps"], (b.n - 1) * 8)
            dve.tensor_tensor(xt[b.parity][1][:, a], k.psum[:, XT[a]], xt[b.parity][0][:, a].bitcast(F32),
                              ALU.subtract).then_inc(s["xnT_lo"], 1)

    def normalise(act, b):
        act.wait_ge(s["rn_ready"], b.n + 1)
        wait_since(act, s["xnT_ps"], b.n)
        for t in range(T):
            last = act.activation(xn[:, t], k.h_all[:, bass.ds(b.n * T + t, 1), :].rearrange("p o d -> p (o d)"),
                                  ACT.Identity, bias=rn[:, t, 1:2], scale=rn[:, t, 0:1])
        last.then_inc(s["xn_ready"], 1)

    def round_xt(act, b):
        for a in range(2):
            act.wait_ge(s["xnT_ps"], b.n + 1)
            wait_since(act, s["u_ps"], (b.n - 1) * 8)
            act.activation(xt[b.parity][0][:, a], k.psum[:, XT[a]], ACT.Copy).then_inc(s["xnT_hi"], 1)

    def turn_xn(pe, b):
        pe.wait_ge(s["xn_ready"], b.n + 1)
        wait_since(pe, s["xnT_lo"], b.n * 2)
        for a in range(2):
            for t in range(T):
                last = pe.transpose(k.psum[:, XT[a], P * t:P * t + P], xn[:, t, P * a:P * a + P], k.ident[:])
        last.then_inc(s["xnT_ps"], 1)

    def moments(pool, b):
        pool.wait_ge(s["mv_ready"], b.n * T + T)
        wait_since(pool, s["xn_ready"], b.n)
        apart(pool, k.passed_pool)
        pool.tensor_scalar(ve[:], mv[:, :, 1], 1.0, EPS, ALU.mult, ALU.add).then_inc(s["ve_ready"], 1)
        pool.tensor_scalar(rn[:, :, 1], mv[:, :, 0], -1.0, 0.0, ALU.mult, ALU.add)
        pool.wait_ge(s["ve_ready"], b.n + 1)
        pool.tensor_tensor(rn[:, :, 0], ve[:], k.half_neg[:, 0:T], ALU.pow).then_inc(s["rstd_ready"], 1)
        pool.wait_ge(s["rstd_ready"], b.n + 1)
        pool.tensor_tensor(rn[:, :, 1], rn[:, :, 1], rn[:, :, 0], ALU.mult).then_inc(s["rn_ready"], 1)
        if b.fixed and b.n == 2:
            pool.wait_ge(s["txt_in"], 16)
        wait_since(pool, s["out_ready"], b.n - 1)
        pool.tensor_tensor(hb[:, b.parity], k.h_all[:, bass.ds(b.n * T, T), :],
                           k.rows[:, FF_B].unsqueeze(1).broadcast_to([P, T, D]), ALU.add).then_inc(s["hb_ready"], 1)

    def sync(sp):
        sp.dma_start(k.h_all[:, IMG_TILES:], k.h_txt_dram.rearrange("(t p) d -> p t d", p=P)).then_inc(s["txt_in"], 16)

        def step(turn):
            if b := turn.batch(1):
                sp.wait_ge(s["out_ready"], b.n + 1)
                u = b.parity
                if b.fixed and b.n == FF_STEPS - 1:
                    for t in range(T):
                        for j in range(4):
                            sp.dma_start(io["out"][4 * t + j, L:S], out[LT * j:LT * j + LT, u, t]).then_inc(stored[u], 16)
                else:
                    apart(sp, k.passed_sp)
                    for j in range(2):
                        dst = io["out"][bass.ds(b.n * 2 + j, 1), 0:L].rearrange("o (t p) d -> p (o t) d", p=P)
                        sp.dma_start(dst, out[:, u, 2 * j:2 * j + 2]).then_inc(stored[u], 16)
        run_steps(sp, step, 3, FF_STEPS, 1, first=1)
        sp.wait_ge(stored[1], 16 * 2 * 4)
        sp.wait_ge(stored[0], 16 * (2 * 4 + 16))

    def scalar(act):
        def step(turn):
            next_b, b = turn.batch(0), turn.batch(1)
            for c in range(8):
                if b:
                    act.wait_ge(s["u_ps"], b.n * 8 + (c + 1))
                    wait_since(act, s["g_lo"], b.n * 8 + (c - 1))
                    act.activation(g[:, c % 2], k.psum[:, UB[c % 2]], ACT.Gelu, bias=k.b_gelu[:, c:c + 1]).then_inc(s["g_ready"], 1)
                if c == NORMALISE_AT and next_b:
                    normalise(act, next_b)
                if c == TURN_AT and next_b:
                    round_xt(act, next_b)
        run_steps(act, step, 3, FF_STEPS, 1, first=1)

    def vector(dve):
        def step(turn):
            next_b, b = turn.batch(0), turn.batch(1)
            for c in range(8):
                if b:
                    dve.wait_ge(s["g_ready"], b.n * 8 + (c + 1))
                    wait_since(dve, s["y_ps"], b.n * 8 + (c - 1))
                    dve.tensor_scalar(g_hi[:, c % 2], g[:, c % 2], 1.0, None, ALU.mult).then_inc(s["g_hi"], 1)
                    dve.wait_ge(s["g_hi"], b.n * 8 + (c + 1))
                    dve.tensor_tensor(g_lo[:, c % 2], g[:, c % 2], g_hi[:, c % 2].bitcast(F32), ALU.subtract).then_inc(s["g_lo"], 1)
                if c == STATS_AT and next_b:
                    stats(dve, next_b)
                if c == TURN_AT and next_b:
                    rest_xt(dve, next_b)
            if b:
                dve.wait_ge(s["y_ps"], b.n * 8 + 8)
                dve.wait_ge(s["hb_ready"], b.n + 1)
                if b.parity:
                    wait_since(dve, stored[1], b.half * 32)
                else:
                    wait_since(dve, stored[0], b.half * 32)
                for c in range(2):
                    last = dve.tensor_tensor(out[:, b.parity, 2 * c:2 * c + 2], k.psum[:, YB[b.parity][c]].rearrange("p (t d) -> p t d", t=2),
                                             hb[:, b.parity, 2 * c:2 * c + 2], ALU.add)
                last.then_inc(s["out_ready"], 1)
        run_steps(dve, step, 3, FF_STEPS, 1, first=1)

    def tensor(pe):
        def down(b, c):
            pe.wait_ge(s["g_lo"], b.n * 8 + (c + 1))
            if c == 0:
                wait_since(pe, s["out_ready"], b.n - 1)
                if b.fixed and b.n == 1:
                    pe.wait_ge(k.h_done, BATCH)
            for t in range(T):
                first = c == 0 and t % 2 == 0
                last = split_product(pe, k.psum[:, YB[b.parity][t // 2], D * (t % 2):D * (t % 2) + D],
                                     [v[:, c % 2, P * t:P * t + P] for v in (g_hi, g_lo)], [v[:, c] for v in k.w_dn],
                                     start=first, stop=c == 7, check=True)
            last.then_inc(s["y_ps"], 1)

        def up(b, c):
            x = xt[b.parity]
            wait_since(pe, s["g_ready"], b.n * 8 + (c - 1))
            for a in range(2):
                last = split_product(pe, k.psum[:, UB[c % 2]], [w[:, a, c] for w in k.w_up], [v[:, a] for v in x],
                                     start=a == 0, stop=a == 1)
            last.then_inc(s["u_ps"], 1)

        def step(turn):
            next_b, b = turn.batch(0), turn.batch(1)
            if b:
                pe.wait_ge(s["xnT_lo"], b.n * 2 + 2)
            for c in range(8):
                if b:
                    up(b, c)
                    if c:
                        down(b, c - 1)
                if c == TURN_AT and next_b:
                    turn_xn(pe, next_b)
            if b:
                down(b, 7)
        run_steps(pe, step, 3, FF_STEPS, 1, first=1)

    def gpsimd(pool):
        def step(turn):
            if b := turn.batch(0):
                moments(pool, b)
        run_steps(pool, step, 3, FF_STEPS, 1, first=1)

    first = Batch(0, 0, 0)
    k.feed_first = {"stats": lambda dve: stats(dve, first), "rest_xt": lambda dve: rest_xt(dve, first),
                    "normalise": lambda act: normalise(act, first), "round_xt": lambda act: round_xt(act, first),
                    "turn_xn": lambda pe: turn_xn(pe, first), "moments": lambda pool: moments(pool, first)}
    return {"sync": sync, "scalar": scalar, "vector": vector, "tensor": tensor, "gpsimd": gpsimd}


def stage_weight(weights, s, unit_out, unit_in):
    pair = ((unit_out >> (s + 1)) << s) | (unit_out & ((1 << s) - 1))
    return weights[s][pair, (unit_out >> s) & 1, (unit_in >> s) & 1]


def block_coefficients(weights, transposed):
    unit = np.arange(8)[None, :] * P + np.arange(P)[:, None]
    out = np.empty((P, STAGES - IN_BLOCK, 8, 2), weights.dtype)
    for s in range(IN_BLOCK, STAGES):
        other = unit ^ (1 << s)
        out[:, s - IN_BLOCK, :, 0] = stage_weight(weights, s, unit, unit)
        out[:, s - IN_BLOCK, :, 1] = stage_weight(weights, s, other, unit) if transposed else stage_weight(weights, s, unit, other)
    return out


def path_table(weights, inputs_free):
    out = np.empty((P, PATHS), weights.dtype)
    p, f = np.arange(P)[:, None, None], np.arange(8)[None, :, None] * P
    for s in range(IN_BLOCK):
        at, n = stage_columns(s, inputs_free)
        free = np.arange(n)[None, None, :]
        low = (1 << s) - 1
        output, inp = (p, free << s) if inputs_free else (free, p)
        before = f + ((inp & ~low) | (output & low))
        after = (before & ~(1 << s)) | (output & (1 << s))
        out[:, at:at + 8 * n] = stage_weight(weights, s, after, before).reshape(P, 8 * n)
    return out


def kernel(x, txt, L0_tok_Wq_w, L0_tok_Wq_b, L0_tok_Wk_w, L0_tok_Wk_b, L0_tok_Wv_w, L0_tok_Wv_b, L0_tok_w_bias,
           L0_tok_out_w, L0_tok_out_b, L0_tok_ln_g, L0_tok_ln_b, L0_tok_local_mask, L0_attn_Wq, L0_attn_bq, L0_attn_Wk,
           L0_attn_bk, L0_attn_Wv, L0_attn_bv, L0_attn_Wo, L0_attn_bo, L0_ffn_W_exp, L0_ffn_b_exp, L0_ffn_up_weights,
           L0_ffn_up_bias, L0_ffn_down_weights, L0_ffn_W_con, L0_ffn_b_con, L0_ffn_down_bias):
    import concourse.bacc as bacc
    from concourse.bass_utils import run_bass_kernel_spmd

    a = np.asarray
    x = a(x)
    arrays = {
        "x": x.reshape(BATCH, C, L, 2, 2).transpose(0, 4, 1, 3, 2).reshape(BATCH, P, 2 * L),
        "xt": x.transpose(0, 2, 3, 1).reshape(BATCH, L, D),
        "txt": a(txt).reshape(BATCH * LT, D),
        "w_tok": np.stack([a(w).T for w in (L0_tok_Wq_w, L0_tok_Wk_w, L0_tok_Wv_w)]),
        "b_tok_rows": np.stack([np.tile(a(b), 4) for b in (L0_tok_Wq_b, L0_tok_Wk_b, L0_tok_Wv_b)]),
        "b_tok_q": np.tile(a(L0_tok_Wq_b), 2).reshape(P, 1),
        "ew": a(L0_tok_w_bias).T,
        "mask": np.ascontiguousarray(a(L0_tok_local_mask).T).view(np.uint32),
        "w_out": a(L0_tok_out_w),
        "rows": np.stack([a(v) for v in (L0_tok_out_b, L0_tok_ln_g, L0_tok_ln_b, L0_attn_bv, L0_attn_bo, L0_ffn_b_con,
                                         L0_ffn_down_bias)]),
        "w_att": np.stack([a(v) for v in (L0_attn_Wq, L0_attn_Wk, L0_attn_Wv, L0_attn_Wo)]),
        "b_qk": np.stack([a(v).reshape(2, P) for v in (L0_attn_bq, L0_attn_bk)]).transpose(2, 0, 1),
        "w_exp": np.concatenate([a(L0_ffn_W_exp).T, a(L0_ffn_b_exp)[:, None]], axis=1),
        "w_con": a(L0_ffn_W_con),
        "coef_up": block_coefficients(a(L0_ffn_up_weights), False),
        "coef_dn": block_coefficients(a(L0_ffn_down_weights), True),
        "table_up": path_table(a(L0_ffn_up_weights), False),
        "table_dn": path_table(a(L0_ffn_down_weights), True),
        "up_bias": a(L0_ffn_up_bias).reshape(8, P).T,
    }
    nc = bacc.Bacc("TRN2", target_bir_lowering=False, num_devices=1)
    io, feeds = {}, {}
    for name, v in arrays.items():
        v = np.ascontiguousarray(v)
        feeds[f"in_{name}"] = v
        io[name] = nc.dram_tensor(f"in_{name}", v.shape, mybir.dt.from_np(v.dtype), kind="ExternalInput").ap()
    io["out"] = nc.dram_tensor("out_h", (BATCH, S, D), F32, kind="ExternalOutput").ap()
    build(nc, io)
    return run_bass_kernel_spmd(nc, [feeds], core_ids=[0]).results[0]["out_h"]
```

```python
from contextlib import ExitStack

import concourse.bass as bass
import numpy as np
from concourse import mybir

ALU = mybir.AluOpType
ACT = mybir.ActivationFunctionType
F32 = mybir.dt.float32
F32R = mybir.dt.float32r
BF16 = mybir.dt.bfloat16
U8 = mybir.dt.uint8
U32 = mybir.dt.uint32
AX_X = mybir.AxisListType.X

P = 128
BATCH, C, L, H = 16, 64, 256, 4
LT = 32
S = L + LT
D = C * H
NH, HD = 16, 16
HID = 1024
STAGES = 10
TILES = BATCH * L // P + BATCH * LT // P
IMG_TILES = BATCH * L // P
EPS = 1e-5
MASKED = -1e30
KEEP = 3e38
SLOTS_Q = (0, 0, 0, 1, 1, 2)
SLOTS_K = (0, 1, 2, 0, 1, 0)
SR = HD * len(SLOTS_Q)
NPARTS = 3
M_COLS = 2 * NH + 4
GROUPS = 4
W_KT1 = S - P
UP_COLS = D + 1
LOW_ROW = 32
N_CROSS = 4
HSLOTS = 8
FF_TOK = 512
FF_STEPS = TILES * P // FF_TOK

IN_BLOCK = 7
PATHS = 8 * (2 * P - 2)


def stage_columns(stage, inputs_free):
    n = 2 ** (IN_BLOCK - stage) if inputs_free else 2 ** (stage + 1)
    return 8 * (n - 2), n


class Batch:

    def __init__(self, n, half, parity):
        self.n, self.half, self.parity = n, half, parity
        self.fixed = isinstance(n, int)


class Turn:

    def __init__(self, loop, start, count=BATCH):
        self.loop, self.start, self.count = loop, start, count

    def is_step(self, n):
        return self.loop is None and self.start == n

    def batch(self, lag):
        c = self.start - lag
        if self.loop is None:
            return Batch(c, c // 2, c % 2) if 0 <= c < self.count else None
        return Batch(self.loop * 2 + c, self.loop + c // 2, c % 2)


def run_steps(eng, step, peel, count, lags, first=0):
    for i in range(first, peel):
        step(Turn(None, i, count))
    with eng.Fori(0, (count - peel) // 2) as loop:
        for u in range(2):
            step(Turn(loop, peel + u, count))
    for i in range(count, count + lags):
        step(Turn(None, i, count))


def wait_since(eng, sem, value):
    if isinstance(value, int) and value <= 0:
        return
    eng.wait_ge(sem, value)


def apart(eng, passed):
    eng.sem_inc(passed, 1)


def split_product(pe, out, a, b, start=True, stop=True, check=False):
    pe.matmul(out, a[0], b[0], start=start, stop=False, skip_group_check=check)
    pe.matmul(out, a[0], b[1], start=False, stop=False, skip_group_check=check)
    return pe.matmul(out, a[1], b[0], start=False, stop=stop, skip_group_check=check)


def build(nc, io):
    ctx = ExitStack()
    with ctx:
        def sb(name, shape, dt=F32, where=ctx):
            return where.enter_context(nc.sbuf_tensor(name, shape, dt))

        def sem(name):
            return ctx.enter_context(nc.semaphore(name))

        class K:
            pass

        k = K()
        k.io = io
        k.sem, k.sb = sem, sb
        k.psum = ctx.enter_context(nc.psum_tensor("psum", [P, 8, 512], F32))
        k.passed_sp, k.passed_dve, k.passed_pool = sem("passed_sp"), sem("passed_dve"), sem("passed_pool")
        k.h_all = sb("h_all", [P, TILES, D])
        k.h_ready = sem("h_ready")
        k.h_done = sem("h_done")
        k.stat_txt = sb("stat_txt", [LT, BATCH, 2])
        k.ident = sb("ident", [P, P])
        k.ident_bf = sb("ident_bf", [P, P], BF16)
        k.mask_q = sb("mask_q", [P, 512], BF16)
        k.mask_txt = sb("mask_txt", [P, LT], BF16)
        k.keep_txt = sb("keep_txt", [P, LT])
        k.half_neg = sb("half_neg", [P, 64])
        k.rows = sb("rows", [P, 7, D])
        k.w_att = [sb(f"w_att_{x}", [P, 4, 2, D], F32R) for x in ("hi", "lo")]
        k.b_qk = sb("b_qk", [P, 2, 2])
        with ExitStack() as early:
            k.table = {x: sb(f"table_{x}", [P, HID * D // P], F32, early) for x in ("up", "dn")}
            k.fold_dn = [sb(f"fold_dn_{i}", [P, 8, D], F32, early) for i in range(2)]
        k.w_up = [sb(f"w_up_{x}", [P, 2, 8, P], F32R) for x in ("hi", "lo")]
        k.w_dn = [sb(f"w_dn_{x}", [P, 8, D], F32R) for x in ("hi", "lo")]
        k.b_gelu = sb("b_gelu", [P, 8])
        k.parts_dram = nc.dram_tensor("parts_dram", (2, 2, NPARTS, HD, 8, 2 * S), BF16, kind="Internal").ap()
        k.mrow_dram = nc.dram_tensor("mrow_dram", (2, NPARTS, M_COLS, P), BF16, kind="Internal").ap()
        k.h_txt_dram = nc.dram_tensor("h_txt_dram", (BATCH * LT, D), F32, kind="Internal").ap()
        with ExitStack() as mixing:
            k.w_tok = [sb(f"w_tok_{x}", [P, 3, P], F32R, mixing) for x in ("hi", "lo")]
            k.b_kv = sb("b_kv", [P, 512], F32R, mixing)
            k.ones = sb("ones", [P, P], F32R, mixing)
            k.nb_q = sb("nb_q", [P, 1], F32, mixing)
            k.ew = sb("ew", [P, 2, L], F32, mixing)
            k.w_out = [sb(f"w_out_{x}", [P, 2, D], F32R, mixing) for x in ("hi", "lo")]
            mixing_phase = mix_tokens(nc, k, mixing)
            preparing = prepare(nc, k, mixing)
        with ExitStack() as own:
            feeding = feed_forward(nc, k, own)
        with ExitStack() as own:
            attending = attend(nc, k, own)
            run_phases(nc, preparing, mixing_phase, attending, feeding)


def run_phases(nc, *phases):
    with nc.Block() as block:
        @block.sync
        def _(sp):
            for phase in phases:
                phase["sync"](sp)

        @block.scalar
        def _(act):
            for phase in phases:
                phase["scalar"](act)

        @block.vector
        def _(dve):
            for phase in phases:
                phase["vector"](dve)

        @block.tensor
        def _(pe):
            for phase in phases:
                phase["tensor"](pe)

        @block.gpsimd
        def _(pool):
            for phase in phases:
                phase["gpsimd"](pool)


def prepare(nc, k, own):
    sb, sem, io = lambda n, s, d=F32: k.sb(n, s, d, own), k.sem, k.io
    cols = {"up": UP_COLS, "dn": D}
    fold = {"up": [sb(f"fold_up_{i}", [P, 8, UP_COLS]) for i in range(2)], "dn": k.fold_dn}
    table = {x: k.table[x][:, 0:PATHS] for x in cols}
    cross = sb("cross", [P, N_CROSS, UP_COLS])
    coef = {x: sb(f"coef_{x}", [P, STAGES - IN_BLOCK, 8, 2]) for x in cols}
    raw_tok = sb("raw_tok", [P, 3, P])
    raw_kv = sb("raw_kv", [P, 512])
    warm = sb("warm", [P, 1])
    raw_att = sb("raw_att", [P, 4, 2, D])
    raw_out = sb("raw_out", [P, 2, D])
    raw_ew = sb("raw_ew", [P, 2, L])
    raw_mask = sb("raw_mask", [P, 2, L // 4], U32)
    masked_ew = sb("masked_ew", [P, 2, L])
    raw_bq = sb("raw_bq", [P, 1])
    raw_bqk = sb("raw_bqk", [P, 2, 2])
    up_bias = sb("up_bias", [P, 8])
    txt = sb("txt", [P, 4, D])
    txt_stats = sb("txt_stats", [P, 4, 6])
    txt_mv = sb("txt_mv", [P, 4, 2])
    txt_ve = sb("txt_ve", [P, 4])
    k.txt_rn = sb("txt_rn", [P, 4, 2])

    k.zeroed = sem("raw_zeroed")
    coef_in = sem("coef_in")
    fold_in = {x: sem(f"fold_in_{x}") for x in cols}
    table_in = {x: sem(f"table_in_{x}") for x in cols}
    path_steps = {x: sem(f"path_steps_{x}") for x in cols}
    block_ps = {x: sem(f"block_ps_{x}") for x in cols}
    crossed = sem("crossed")
    folded = sem("folded")
    tok_in, att_in, out_in, ew_in, small_in, txt_in = (
        sem(x) for x in ("tok_in", "att_in", "out_in", "ew_in", "small_in", "txt_in"))
    split_hi, k.split_lo = sem("split_hi"), sem("split_lo")
    mask_steps, tri_copied = sem("mask_steps"), sem("tri_copied")
    ew_masked, small_done = sem("ew_masked"), sem("small_done")
    stats_txt, k.rn_txt, k.stat_moved = sem("stats_txt"), sem("rn_txt"), sem("stat_moved")
    up_turned, up_hi, k.up_lo, dn_hi, k.dn_lo = (
        sem(x) for x in ("up_turned", "up_hi", "up_lo", "dn_hi", "dn_lo"))
    act_done = sem("prep_act_done")

    steps = []
    for x, i in (("dn", 0), ("dn", 1), ("up", 0), ("dn", 2), ("up", 1), ("up", 2)):
        steps.append((x, i, STAGES - 1 - i if x == "dn" else IN_BLOCK + i))
    order = {(x, i): n for n, (x, i, _) in enumerate(steps)}
    LAST = STAGES - IN_BLOCK - 1

    def unit(x, i, f):
        return k.psum[:, f, 0:UP_COLS] if x == "up" and i == 0 else fold[x][i % 2][:, f, :]

    def sync(sp):
        for x in ("dn", "up"):
            sp.dma_start(coef[x][:], io[f"coef_{x}"]).then_inc(coef_in, 16)
        sp.dma_start(fold["dn"][0][:], io["w_con"].rearrange("(f p) c -> p f c", p=P)).then_inc(fold_in["dn"], 16)
        sp.dma_start(table["up"][:], io["table_up"]).then_inc(table_in["up"], 16)
        sp.dma_start(fold["up"][0][:], io["w_exp"].rearrange("(f p) c -> p f c", p=P)).then_inc(fold_in["up"], 16)
        sp.wait_ge(k.zeroed, 2)
        for j in range(2):
            for w in range(3):
                sp.dma_start(raw_tok[C * j:C * j + C, w, C * j:C * j + C], io["w_tok"][w]).then_inc(tok_in, 16)
        for r in (0, LOW_ROW):
            for v in range(2):
                sp.dma_start(raw_kv[r:r + 1, :].rearrange("o (a v b c) -> o v a b c", a=2, v=2, b=2)[:, v].rearrange("o a b c -> o a (b c)"),
                             io["b_tok_rows"][1 + v:2 + v]).then_inc(tok_in, 16)
        sp.dma_start(raw_bq[:], io["b_tok_q"]).then_inc(tok_in, 16)
        sp.dma_start(raw_ew[:], io["ew"].rearrange("(t p) q -> p t q", p=P)).then_inc(ew_in, 16)
        sp.dma_start(raw_mask[:], io["mask"].rearrange("(t p) q -> p t q", p=P)).then_inc(ew_in, 16)
        sp.dma_start(raw_bqk[:], io["b_qk"]).then_inc(small_in, 16)
        sp.dma_start(up_bias[:], io["up_bias"]).then_inc(small_in, 16)
        sp.dma_start(table["dn"][:], io["table_dn"]).then_inc(table_in["dn"], 16)
        sp.dma_start(k.rows[:], io["rows"].partition_broadcast(P)).then_inc(small_in, 16)
        sp.dma_start(raw_out[:], io["w_out"].rearrange("(a p) n -> p a n", p=P)).then_inc(out_in, 16)
        sp.dma_start(txt[:], io["txt"].rearrange("(t p) d -> p t d", p=P)).then_inc(txt_in, 16)
        for w in range(4):
            sp.dma_start(raw_att[:, w], io["w_att"][w].rearrange("(a p) n -> p a n", p=P)).then_inc(att_in, 16)

    def scalar(act):
        act.wait_ge(k.zeroed, 3)
        act.activation(warm[:], k.half_neg[:, 0:1], ACT.Exp)
        act.wait_ge(coef_in, 32)
        for n, (x, i, s) in enumerate(steps):
            bit = 1 << (s - IN_BLOCK)
            if n == 5:
                k.mix_first["x_hi"](act)
            if x == "dn" and i == 0:
                act.wait_ge(fold_in[x], 16)
            for f in range(8):
                if i:
                    act.wait_ge(folded, 8 * order[x, i - 1] + (f ^ bit) + 1)
                elif x == "up":
                    act.wait_ge(block_ps["up"], (f ^ bit) + 1)
                wait_since(act, folded, 8 * n + f + 1 - N_CROSS)
                act.activation(cross[:, f % N_CROSS, 0:cols[x]], unit(x, i, f ^ bit), ACT.Copy,
                               scale=coef[x][:, s - IN_BLOCK, f, 1:2]).then_inc(crossed, 1)
        act.wait_ge(ew_masked, 1)
        act.activation(k.ew[:], masked_ew[:], ACT.Exp).then_inc(act_done, 1)
        act.wait_ge(block_ps["dn"], 8)
        act.activation(k.w_dn[0][:].rearrange("p f c -> p (f c)"), k.psum[:, 0:4].rearrange("p b c -> p (b c)"),
                       ACT.Copy).then_inc(dn_hi, 1)
        for a in range(2):
            act.wait_ge(up_turned, a + 1)
            act.activation(k.w_up[0][:, a].rearrange("p c q -> p (c q)"),
                           k.psum[:, 4 + 2 * a:6 + 2 * a].rearrange("p b c -> p (b c)"), ACT.Copy).then_inc(up_hi, 1)

    def vector(dve):
        def multiply_paths(x):
            free_in = x == "dn"
            stages = list(range(IN_BLOCK))[::-1] if free_in else list(range(IN_BLOCK))
            dve.wait_ge(table_in[x], 16)
            at, n = stage_columns(stages[0], free_in)
            for i, s in enumerate(stages[1:]):
                to, m = stage_columns(s, free_in)
                if i:
                    dve.wait_ge(path_steps[x], i)
                before = table[x][:, at:at + 8 * n].rearrange("p (f n) -> p f n", f=8)
                if free_in:
                    before, split = before.unsqueeze(3).broadcast_to([P, 8, n, 2]), "p (f n b) -> p f n b"
                else:
                    before, split = before.unsqueeze(2).broadcast_to([P, 8, 2, n]), "p (f b n) -> p f b n"
                dve.tensor_tensor(table[x][:, to:to + 8 * m].rearrange(split, f=8, b=2), before,
                                  table[x][:, to:to + 8 * m].rearrange(split, f=8, b=2), ALU.mult).then_inc(path_steps[x], 1)
                at, n = to, m

        dve.memset(raw_tok[:], 0.0).then_inc(k.zeroed, 1)
        dve.memset(raw_kv[:], 0.0).then_inc(k.zeroed, 1)
        dve.memset(k.ones[:].bitcast(F32), 1.0)
        dve.memset(k.half_neg[:], -0.5).then_inc(k.zeroed, 1)
        dve.wait_ge(coef_in, 32)
        for n, (x, i, s) in enumerate(steps):
            if n == 1:
                multiply_paths("up")
            if n == 3:
                dve.wait_ge(ew_in, 32)
                dve.tensor_tensor(masked_ew[:], raw_ew[:], raw_mask[:].bitcast(U8), ALU.mult).then_inc(ew_masked, 1)
            if n == 4:
                multiply_paths("dn")
            if n == 5:
                dve.wait_ge(txt_in, 16)
                for t in range(4):
                    dve.bn_stats(txt_stats[:, t], txt[:, t]).then_inc(stats_txt, 1)
                dve.wait_ge(stats_txt, 4)
                for t in range(4):
                    dve.bn_aggr(txt_mv[:, t], txt_stats[:, t]).then_inc(stats_txt, 1)
            for f in range(8):
                dve.wait_ge(crossed, 8 * n + (f | 1 if (x, i) == ("up", 0) else f) + 1)
                if i:
                    dve.wait_ge(folded, 8 * order[x, i - 1] + f + 1)
                elif x == "up":
                    dve.wait_ge(block_ps["up"], f + 1)
                dve.scalar_tensor_tensor(
                    out=fold[x][(i + 1) % 2][:, f, :], in0=unit(x, i, f), scalar=coef[x][:, s - IN_BLOCK, f, 0:1],
                    in1=cross[:, f % N_CROSS, 0:cols[x]], op0=ALU.mult, op1=ALU.add).then_inc(folded, 1)
        dve.wait_ge(small_in, 48)
        dve.wait_ge(folded, 8 * (order["up", LAST] + 1))
        dve.tensor_tensor(k.b_gelu[:], fold["up"][(LAST + 1) % 2][:, :, D], up_bias[:], ALU.add).then_inc(k.dn_lo, 1)
        dve.wait_ge(dn_hi, 1)
        dve.tensor_tensor(k.w_dn[1][:].rearrange("p f c -> p (f c)"), k.psum[:, 0:4].rearrange("p b c -> p (b c)"),
                          k.w_dn[0][:].bitcast(F32).rearrange("p f c -> p (f c)"), ALU.subtract).then_inc(k.dn_lo, 1)
        for a in range(2):
            dve.wait_ge(up_hi, a + 1)
            flat = lambda w: w[:, a].rearrange("p c q -> p (c q)")
            dve.tensor_tensor(flat(k.w_up[1]), k.psum[:, 4 + 2 * a:6 + 2 * a].rearrange("p b c -> p (b c)"),
                              flat(k.w_up[0]).bitcast(F32), ALU.subtract).then_inc(k.up_lo, 1)

    def tensor(pe):
        def through_block(x, f):
            at, n = stage_columns(IN_BLOCK - 1 if x == "up" else 0, x == "dn")
            out = k.psum[:, f, 0:UP_COLS] if x == "up" else k.psum[:, f // 2, D * (f % 2):D * (f % 2) + D]
            pe.matmul(out, table[x][:, at + n * f:at + n * (f + 1)], fold[x][0 if x == "up" else (LAST + 1) % 2][:, f, :],
                      start=True, stop=True).then_inc(block_ps[x], 1)

        pe.wait_ge(path_steps["up"], IN_BLOCK - 1)
        pe.wait_ge(fold_in["up"], 16)
        for f in range(8):
            through_block("up", f)
        pe.wait_ge(path_steps["dn"], IN_BLOCK - 1)
        pe.wait_ge(folded, 8 * (order["dn", LAST] + 1))
        for f in range(8):
            through_block("dn", f)
        pe.wait_ge(folded, 8 * (order["up", LAST] + 1))
        pe.wait_ge(mask_steps, 2)
        for a in range(2):
            for f in range(8):
                last = pe.transpose(k.psum[:, 4 + 2 * a + f // 4, P * (f % 4):P * (f % 4) + P],
                                    fold["up"][(LAST + 1) % 2][:, f, P * a:P * a + P], k.ident[:])
            last.then_inc(up_turned, 1)

    def gpsimd(pool):
        pool.memset(k.ident[:], 1.0).then_inc(mask_steps, 1)
        pool.wait_ge(mask_steps, 1)
        pool.affine_select(out=k.ident[:], in_=k.ident[:], compare_op=ALU.is_equal, fill=0.0, base=0,
                           pattern=[[-1, P]], channel_multiplier=1).then_inc(mask_steps, 1)
        pool.memset(k.mask_q[:], 0.0)
        pool.memset(k.keep_txt[:], KEEP).then_inc(mask_steps, 1)
        pool.wait_ge(mask_steps, 3)
        pool.tensor_scalar(k.ident_bf[:], k.ident[:], 1.0, 0.0, ALU.mult, ALU.add).then_inc(mask_steps, 1)
        pool.affine_select(out=k.mask_q[:].rearrange("p (r k) -> p r k", r=4),
                           in_=k.mask_q[:].rearrange("p (r k) -> p r k", r=4), compare_op=ALU.is_ge,
                           fill=MASKED, base=0, pattern=[[0, 4], [-1, P]], channel_multiplier=1).then_inc(mask_steps, 1)
        for j in range(4):
            pool.wait_ge(mask_steps, 5 + j)
            pool.affine_select(out=k.keep_txt[LT * j:LT * j + LT], in_=k.keep_txt[LT * j:LT * j + LT],
                               compare_op=ALU.is_ge, fill=0.0, base=0, pattern=[[1, LT]],
                               channel_multiplier=-1).then_inc(mask_steps, 1)
        pool.wait_ge(mask_steps, 9)
        pool.memset(k.mask_txt[:], 0.0).then_inc(tri_copied, 1)
        for j in range(4):
            pool.wait_ge(tri_copied, 1 + j)
            pool.affine_select(out=k.mask_txt[LT * j:LT * j + LT], in_=k.mask_txt[LT * j:LT * j + LT],
                               compare_op=ALU.is_ge, fill=MASKED, base=0, pattern=[[-1, LT]],
                               channel_multiplier=1).then_inc(tri_copied, 1)

        def split(hi, lo, raw, n, rows=slice(0, P)):
            pool.tensor_scalar(hi, raw, 1.0, 0.0, ALU.mult, ALU.add).then_inc(split_hi, 1)
            pool.wait_ge(split_hi, n)
            pool.tensor_tensor(lo, raw[rows], hi[rows].bitcast(F32), ALU.subtract).then_inc(k.split_lo, 1)

        pool.wait_ge(tri_copied, 5)
        pool.wait_ge(k.zeroed, 2)
        pool.wait_ge(tok_in, 16 * 11)
        split(k.w_tok[0][:], k.w_tok[1][:], raw_tok[:], 1)
        low = slice(LOW_ROW, 2 * LOW_ROW)
        split(k.b_kv[:], k.b_kv[low], raw_kv[:], 2, low)
        pool.wait_ge(k.split_lo, 2)
        pool.tensor_scalar(k.nb_q[:], raw_bq[:], -1.0, 0.0, ALU.mult, ALU.add)
        pool.wait_ge(out_in, 16)
        split(k.w_out[0][:], k.w_out[1][:], raw_out[:], 3)
        k.mix_first["x_lo"](pool)
        pool.wait_ge(stats_txt, 8)
        pool.wait_ge(k.zeroed, 3)
        pool.tensor_scalar(txt_ve[:], txt_mv[:, :, 1], 1.0, EPS, ALU.mult, ALU.add).then_inc(small_done, 1)
        pool.tensor_scalar(k.txt_rn[:, :, 1], txt_mv[:, :, 0], -1.0, 0.0, ALU.mult, ALU.add).then_inc(small_done, 1)
        pool.wait_ge(small_done, 2)
        pool.tensor_tensor(k.txt_rn[:, :, 0], txt_ve[:], k.half_neg[:, 0:4], ALU.pow).then_inc(k.rn_txt, 1)
        pool.wait_ge(k.rn_txt, 1)
        pool.tensor_tensor(k.txt_rn[:, :, 1], k.txt_rn[:, :, 1], k.txt_rn[:, :, 0], ALU.mult).then_inc(k.rn_txt, 1)
        pool.wait_ge(small_in, 48)
        pool.tensor_scalar(k.b_qk[:, 0], raw_bqk[:, 0], HD ** -0.5, 0.0, ALU.mult, ALU.add)
        pool.tensor_scalar(k.b_qk[:, 1], raw_bqk[:, 1], 1.0, 0.0, ALU.mult, ALU.add).then_inc(small_done, 1)
        pool.tensor_tensor(k.rows[:, 5], k.rows[:, 5], k.rows[:, 6], ALU.add).then_inc(small_done, 1)
        pool.wait_ge(att_in, 64)
        for w in range(4):
            split(k.w_att[0][:, w], k.w_att[1][:, w], raw_att[:, w], 4 + w)

    return {"sync": sync, "scalar": scalar, "vector": vector, "tensor": tensor, "gpsimd": gpsimd}


OUT_B, LN_G, LN_B, ATT_BV, ATT_BO, FF_B = range(6)


def mix_tokens(nc, k, own):
    sb, sem, io = lambda n, s, d=F32: k.sb(n, s, d, own), k.sem, k.io
    x_raw = sb("x_raw", [P, 2, 2, L])
    x_hi = sb("x_hi", [P, 2, 2, L], F32R)
    x_lo = sb("x_lo", [P, 2, 2, L], F32R)
    xt_raw = sb("xt_raw", [P, 2, 2, D])
    xtb = sb("xtb", [P, 2, D])
    ek = sb("ek", [P, 2, 2, D])
    ekv = sb("ekv", [P, 2, 2, D])
    eq = sb("eq", [P, 512])
    den = sb("den", [P, 512])
    rec = sb("rec", [P, 512])
    y = sb("y", [P, 2, L])
    y_hi = sb("y_hi", [P, 2, L], F32R)
    y_lo = sb("y_lo", [P, 2, L], F32R)
    h1 = sb("h1", [P, 2, D])
    st1 = sb("st1", [P, 2, 6])
    mv1 = sb("mv1", [P, 2, 2])
    ve1 = sb("ve1", [P, 2])
    rn1 = sb("rn1", [P, 2, 2])
    z = sb("z", [P, 2, D])
    zg = sb("zg", [P, 2, D])

    x_loaded = [sem(f"x_loaded{i}") for i in range(2)]
    xt_loaded = [sem(f"xt_loaded{i}") for i in range(2)]
    names = ("x_hi_ready x_lo_ready q_ps kv_ps ek_ready nd_ps den_ready rec_ready "
             "y_hi_ready y_lo_ready out_ps xtb_ready st1_ready mv1_ready ve1_ready rstd1_ready rn1_ready "
             "z_ready zg_ready").split()
    s = {n: sem("mix_" + n) for n in names}
    k.ekv_ready, k.eq_ready, k.y_ready, k.h1_ready = (sem("mix_" + n) for n in ("ekv_ready", "eq_ready", "y_ready", "h1_ready"))

    QB, KVB, OUTB = 0, 1, 5
    NUMB, DENB = (3, 6), (4, 7)
    bank = lambda i: k.psum[:, i]

    def row(i):
        return k.rows[:, i].unsqueeze(1).broadcast_to([P, 2, D])

    def round_x(act, b):
        act.wait_ge(x_loaded[b.parity], (b.half + 1) * 16)
        wait_since(act, s["q_ps"], b.n - 1)
        act.activation(x_hi[:, b.parity], x_raw[:, b.parity], ACT.Copy).then_inc(s["x_hi_ready"], 1)

    def rest_x(pool, b):
        pool.wait_ge(s["x_hi_ready"], b.n + 1)
        wait_since(pool, s["q_ps"], b.n - 1)
        pool.tensor_tensor(x_lo[:, b.parity], x_raw[:, b.parity], x_hi[:, b.parity].bitcast(F32),
                           ALU.subtract).then_inc(s["x_lo_ready"], 1)

    def starts(b):
        return b and b.fixed and b.n == 0

    first = Batch(0, 0, 0)
    k.mix_first = {"x_hi": lambda act: round_x(act, first), "x_lo": lambda pool: rest_x(pool, first)}

    def sync(sp):
        def step(turn):
            if b := turn.batch(0):
                wait_since(sp, s["x_lo_ready"], b.n - 1)
                apart(sp, k.passed_sp)
                sp.dma_start(x_raw[:, b.parity].rearrange("p a l -> p (a l)"), io["x"][b.n] if b.fixed else
                             io["x"][bass.ds(b.n, 1)].rearrange("o p c -> (o p) c")).then_inc(x_loaded[b.parity], 16)
            if b := turn.batch(3):
                wait_since(sp, s["xtb_ready"], b.n - 1)
                apart(sp, k.passed_sp)
                src = io["xt"][bass.ds(b.n, 1)].rearrange("o (t p) d -> p (o t) d", p=P)
                sp.dma_start(xt_raw[:, b.parity], src).then_inc(xt_loaded[b.parity], 16)
        run_steps(sp, step, 6, BATCH, 3)

    def scalar(act):
        act.wait_ge(k.split_lo, 3)
        def step(turn):
            if turn.is_step(BATCH + 3):
                k.attend_first["normalise"](act)
            if turn.is_step(BATCH + 4):
                k.attend_first["round_xt"](act)
            if b := turn.batch(5):
                act.wait_ge(s["rn1_ready"], b.n + 1)
                wait_since(act, s["zg_ready"], b.n)
                for t in range(2):
                    last = act.activation(z[:, t], h1[:, t], ACT.Identity, bias=rn1[:, t, 1:2], scale=rn1[:, t, 0:1])
                last.then_inc(s["z_ready"], 1)
            if (b := turn.batch(0)) and not starts(b):
                round_x(act, b)
            if b := turn.batch(1):
                act.wait_ge(s["kv_ps"], b.n + 1)
                wait_since(act, s["nd_ps"], b.n - 1)
                act.activation(ek[:, b.parity].rearrange("p t (a c) -> p t a c", a=2),
                               k.psum[:, KVB:KVB + 2].rearrange("p t (a v c) -> p t a v c", a=2, v=2)[:, :, :, 0],
                               ACT.Exp).then_inc(s["ek_ready"], 1)
            if b := turn.batch(2):
                act.wait_ge(s["q_ps"], b.n + 1)
                wait_since(act, s["den_ready"], b.n)
                act.activation(eq[:], bank(QB), ACT.Exp, bias=k.nb_q[:], scale=-1.0).then_inc(k.eq_ready, 1)
            if b := turn.batch(3):
                act.wait_ge(k.y_ready, b.n + 1)
                wait_since(act, s["out_ps"], b.n)
                act.activation(y_hi[:], y[:], ACT.Copy).then_inc(s["y_hi_ready"], 1)
        run_steps(act, step, 6, BATCH, 5)

    def vector(dve):
        def step(turn):
            if turn.is_step(BATCH):
                k.attend_first["stats"](dve)
            if turn.is_step(BATCH + 4):
                k.attend_first["rest_xt"](dve)
            if b := turn.batch(3):
                dve.wait_ge(k.eq_ready, b.n + 1)
                dve.wait_ge(s["nd_ps"], b.n + 1)
                wait_since(dve, s["rec_ready"], b.n)
                dve.scalar_tensor_tensor(out=den[:], in0=eq[:], scalar=1.0, in1=bank(DENB[b.parity]),
                                         op0=ALU.add, op1=ALU.mult).then_inc(s["den_ready"], 1)
                dve.wait_ge(s["den_ready"], b.n + 1)
                wait_since(dve, k.y_ready, b.n)
                dve.reciprocal(rec[:], den[:]).then_inc(s["rec_ready"], 1)
                dve.wait_ge(s["rec_ready"], b.n + 1)
                wait_since(dve, s["y_lo_ready"], b.n)
                dve.tensor_tensor(y[:].rearrange("p a l -> p (a l)"), bank(NUMB[b.parity]), rec[:],
                                  ALU.mult).then_inc(k.y_ready, 1)
            if b := turn.batch(4):
                dve.wait_ge(s["out_ps"], b.n + 1)
                dve.wait_ge(s["xtb_ready"], b.n + 1)
                wait_since(dve, s["z_ready"], b.n)
                dve.tensor_tensor(h1[:].rearrange("p t d -> p (t d)"), bank(OUTB),
                                  xtb[:].rearrange("p t d -> p (t d)"), ALU.add).then_inc(k.h1_ready, 1)
                dve.wait_ge(k.h1_ready, b.n + 1)
                wait_since(dve, s["mv1_ready"], b.n * 2)
                for t in range(2):
                    dve.bn_stats(st1[:, t], h1[:, t]).then_inc(s["st1_ready"], 1)
                dve.wait_ge(s["st1_ready"], b.n * 2 + 2)
                wait_since(dve, s["rn1_ready"], b.n)
                apart(dve, k.passed_dve)
                for t in range(2):
                    dve.bn_aggr(mv1[:, t], st1[:, t]).then_inc(s["mv1_ready"], 1)
            if b := turn.batch(1):
                dve.wait_ge(s["ek_ready"], b.n + 1)
                dve.tensor_tensor(ekv[:, b.parity].rearrange("p t (a c) -> p t a c", a=2),
                                  k.psum[:, KVB:KVB + 2].rearrange("p t (a v c) -> p t a v c", a=2, v=2)[:, :, :, 1],
                                  ek[:, b.parity].rearrange("p t (a c) -> p t a c", a=2),
                                  ALU.mult).then_inc(k.ekv_ready, 1)
        run_steps(dve, step, 6, BATCH, 5)

    def tensor(pe):
        pe.wait_ge(k.split_lo, 3)
        pe.wait_ge(k.zeroed, 3)
        pe.wait_ge(k.dn_lo, 2)
        def step(turn):
            if b := turn.batch(4):
                pe.wait_ge(s["y_hi_ready"], b.n + 1)
                pe.wait_ge(s["y_lo_ready"], b.n + 1)
                wait_since(pe, k.h1_ready, b.n)
                for t in range(2):
                    for a in range(2):
                        last = split_product(pe, k.psum[:, OUTB, D * t:D * t + D],
                                             [v[:, a, P * t:P * t + P] for v in (y_hi, y_lo)],
                                             [w[:, a] for w in k.w_out], start=a == 0, stop=a == 1)
                last.then_inc(s["out_ps"], 1)
            if b := turn.batch(2):
                wait_since(pe, k.eq_ready, b.n)
                x = (x_hi[:, b.parity], x_lo[:, b.parity])
                for a in range(2):
                    last = split_product(pe, k.psum[:, QB, L * a:L * a + L], [w[:, 0] for w in k.w_tok],
                                         [v[:, a] for v in x])
                last.then_inc(s["q_ps"], 1)
            if b := turn.batch(1):
                pe.wait_ge(s["x_hi_ready"], b.n + 1)
                pe.wait_ge(s["x_lo_ready"], b.n + 1)
                wait_since(pe, k.ekv_ready, b.n)
                x = (x_hi[:, b.parity], x_lo[:, b.parity])
                for t in range(2):
                    pe.matmul(bank(KVB + t), k.ones[:], k.b_kv[:], start=True, stop=False)
                    for a in range(2):
                        last = split_product(pe, k.psum[:, KVB + t, 2 * P * a:2 * P * a + 2 * P],
                                             [v[:, a, P * t:P * t + P] for v in x],
                                             [w[:, 1:3].rearrange("p v c -> p (v c)") for w in k.w_tok],
                                             start=False, stop=a == 1)
                last.then_inc(s["kv_ps"], 1)
            if b := turn.batch(2):
                pe.wait_ge(k.ekv_ready, b.n + 1)
                wait_since(pe, k.y_ready, b.n - 1)
                for src, out in ((ek, DENB[b.parity]), (ekv, NUMB[b.parity])):
                    for a in range(2):
                        for t in range(2):
                            last = pe.matmul(k.psum[:, out, L * a:L * a + L], src[:, b.parity, t, P * a:P * a + P],
                                             k.ew[:, t], start=t == 0, stop=t == 1)
                last.then_inc(s["nd_ps"], 1)
        run_steps(pe, step, 6, BATCH, 4)

    def gpsimd(pool):
        def step(turn):
            if turn.is_step(BATCH + 1):
                k.attend_first["moments"](pool)
            if b := turn.batch(4):
                pool.wait_ge(xt_loaded[b.parity], (b.half + 1) * 16)
                wait_since(pool, k.h1_ready, b.n)
                pool.tensor_tensor(xtb[:], xt_raw[:, b.parity], row(OUT_B), ALU.add).then_inc(s["xtb_ready"], 1)
            if b := turn.batch(5):
                pool.wait_ge(s["z_ready"], b.n + 1)
                wait_since(pool, k.h_ready, b.n)
                pool.tensor_tensor(zg[:], z[:], row(LN_G), ALU.mult).then_inc(s["zg_ready"], 1)
                pool.wait_ge(s["zg_ready"], b.n + 1)
                pool.tensor_tensor(k.h_all[:, bass.ds(b.n * 2, 2), :], zg[:], row(LN_B),
                                   ALU.add).then_inc(k.h_ready, 1)
            if (b := turn.batch(0)) and not starts(b):
                rest_x(pool, b)
            if b := turn.batch(3):
                pool.wait_ge(s["y_hi_ready"], b.n + 1)
                wait_since(pool, s["out_ps"], b.n)
                pool.tensor_tensor(y_lo[:], y[:], y_hi[:].bitcast(F32), ALU.subtract).then_inc(s["y_lo_ready"], 1)
            if b := turn.batch(4):
                pool.wait_ge(s["mv1_ready"], b.n * 2 + 2)
                wait_since(pool, s["z_ready"], b.n)
                apart(pool, k.passed_pool)
                pool.tensor_scalar(ve1[:], mv1[:, :, 1], 1.0, EPS, ALU.mult, ALU.add).then_inc(s["ve1_ready"], 1)
                pool.tensor_scalar(rn1[:, :, 1], mv1[:, :, 0], -1.0, 0.0, ALU.mult, ALU.add)
                pool.wait_ge(s["ve1_ready"], b.n + 1)
                pool.tensor_tensor(rn1[:, :, 0], ve1[:], k.half_neg[:, 0:2], ALU.pow).then_inc(s["rstd1_ready"], 1)
                pool.wait_ge(s["rstd1_ready"], b.n + 1)
                pool.tensor_tensor(rn1[:, :, 1], rn1[:, :, 1], rn1[:, :, 0], ALU.mult).then_inc(s["rn1_ready"], 1)
        run_steps(pool, step, 6, BATCH, 5)

    return {"sync": sync, "scalar": scalar, "vector": vector, "tensor": tensor, "gpsimd": gpsimd}


def attend(nc, k, own):
    sb, sem, io = lambda n, s, d=F32: k.sb(n, s, d, own), k.sem, k.io
    head = [(i % 2) * 8 + i // 2 for i in range(NH)]
    q_st = [sb(f"q_st{i}", [SR + NPARTS, NH, S], BF16) for i in range(2)]
    k_st = [sb(f"k_st{i}", [SR + NPARTS, NH, S], BF16) for i in range(2)]
    qk = sb("qk", [P, 2, 2, S])
    qk_rest = sb("qk_rest", [P, 2, 2, S])
    parts = sb("parts", [P, NPARTS, 2, 2 * S], BF16)
    prob = sb("prob", [P, HSLOTS, W_KT1 + S])
    txt_in = sb("txt_in", [LT, D])
    txt_res = sb("txt_res", [LT, D])
    xn = sb("xn", [P, 3, D])
    xt_hi = [sb(f"xt_hi{i}", [P, 2, S], F32R) for i in range(2)]
    xt_lo = [sb(f"xt_lo{i}", [P, 2, S], F32R) for i in range(2)]
    xt_txt4 = [[sb(f"xt_txt4_{x}{i}", [P, 2, 4, LT], F32R) for x in ("hi", "lo")] for i in range(2)]
    v_aug = [sb(f"v_aug{i}", [P, 3, NH, 2 * HD]) for i in range(2)]
    prob_txt = sb("prob_txt", [P, GROUPS, LT])
    nmax = sb("nmax", [P, M_COLS])
    nmax_rest = sb("nmax_rest", [P, M_COLS])
    mparts = sb("mparts", [P, NPARTS, M_COLS], BF16)
    st = sb("st", [P, 2, 6])
    mv = sb("mv", [P, 2, 2])
    ve = sb("ve", [P, 2])
    rn = sb("rn", [P, 2, 2, 2])
    mrow = sb("mrow", [NPARTS * M_COLS, P], BF16)
    ctx_u = sb("ctx_u", [P, GROUPS, S])
    rsum = sb("rsum", [P, 3, NH])
    ctx_n = sb("ctx_n", [P, 3, D])
    ct_hi = sb("ct_hi", [P, 2, S], F32R)
    ct_lo = sb("ct_lo", [P, 2, S], F32R)
    hb = sb("hb", [P, 2, D])
    hb_txt = sb("hb_txt", [LT, D])
    h_txt = sb("h_txt", [LT, D])

    names = ("txt_loaded res_loaded xn_ready xnT_ps xnT_hi xnT_lo q_ps k_ps v_ps qk_ready part_h rest_h part_m rest_m "
             "parts_ready v_ready m0_ps m1_ps mt_ps m0_max m1_max mt_max mp_h mr_h mp_m mr_m mp_ready mT_ps mT_ready "
             "mrow_stored st_ps stt_ps exp_done expt_done "
             "seen keep_done ctx_ps ctx_u_done o1_ps rsum_ready ctxn_ready ctxT_ps ctxT_hi ctxT_lo o_ps hb_ready "
             "h_txt_stored ones_set st_ready mv_ready ve_ready rstd_ready rn_ready").split()
    s = {n: sem("att_" + n) for n in names}
    parts_stored = [sem(f"att_parts_stored{i}") for i in range(2)]
    stack_loaded = [sem(f"att_stack_loaded{i}") for i in range(2)]
    mrow_loaded = [sem(f"att_mrow_loaded{i}") for i in range(2)]
    SCORE_BANKS = (4, 5, 7)
    N_STORE, N_STACK = 2 * NPARTS, 6
    bank = lambda i: k.psum[:, i]
    turned_maxima = k.psum[:, 3].bitcast(BF16)[0:NPARTS * M_COLS, 512 + P:512 + 2 * P]

    def stats(dve, b):
        dve.wait_ge(k.h_ready, b.n + 1 if b.fixed else BATCH)
        wait_since(dve, s["mv_ready"], b.n * 2)
        for t in range(2):
            dve.bn_stats(st[:, t], k.h_all[:, bass.ds(b.n * 2 + t, 1), :].rearrange("p o d -> p (o d)")).then_inc(s["st_ready"], 1)
        dve.wait_ge(s["st_ready"], b.n * 2 + 2)
        wait_since(dve, s["rn_ready"], b.n)
        apart(dve, k.passed_dve)
        for t in range(2):
            dve.bn_aggr(mv[:, t], st[:, t]).then_inc(s["mv_ready"], 1)

    def moments(pool, b):
        out = rn[:, b.parity]
        pool.wait_ge(s["mv_ready"], b.n * 2 + 2)
        wait_since(pool, s["xn_ready"], b.n - 1)
        apart(pool, k.passed_pool)
        pool.tensor_scalar(ve[:], mv[:, :, 1], 1.0, EPS, ALU.mult, ALU.add).then_inc(s["ve_ready"], 1)
        pool.tensor_scalar(out[:, :, 1], mv[:, :, 0], -1.0, 0.0, ALU.mult, ALU.add)
        pool.wait_ge(s["ve_ready"], b.n + 1)
        pool.tensor_tensor(out[:, :, 0], ve[:], k.half_neg[:, 0:2], ALU.pow).then_inc(s["rstd_ready"], 1)
        pool.wait_ge(s["rstd_ready"], b.n + 1)
        pool.tensor_tensor(out[:, :, 1], out[:, :, 1], out[:, :, 0], ALU.mult).then_inc(s["rn_ready"], 1)

    def normalise(act, b):
        if starts(b):
            act.wait_ge(k.stat_moved, 64)
            act.wait_ge(k.split_lo, 7)
        act.wait_ge(s["rn_ready"], b.n + 1)
        act.wait_ge(s["txt_loaded"], b.n * 16 + 16)
        wait_since(act, s["xnT_ps"], b.n)
        for t in range(2):
            act.activation(xn[:, t], k.h_all[:, bass.ds(b.n * 2 + t, 1), :].rearrange("p o d -> p (o d)"), ACT.Identity,
                           bias=rn[:, b.parity, t, 1:2], scale=rn[:, b.parity, t, 0:1])
        act.activation(xn[0:LT, 2], txt_in[:], ACT.Identity, bias=k.stat_txt[:, bass.ds(b.n, 1), 1],
                       scale=k.stat_txt[:, bass.ds(b.n, 1), 0]).then_inc(s["xn_ready"], 1)

    def round_xt(act, b):
        act.wait_ge(s["xnT_ps"], b.n + 1)
        wait_since(act, s["v_ps"], b.n - 1)
        act.activation(xt_hi[b.parity][:], k.psum[:, 0:2, 0:S], ACT.Copy).then_inc(s["xnT_hi"], 1)

    def rest_xt(dve, b):
        dve.wait_ge(s["xnT_hi"], b.n + 1)
        wait_since(dve, s["v_ps"], b.n - 1)
        hi, lo = xt_hi[b.parity], xt_lo[b.parity]
        dve.tensor_tensor(lo[:], k.psum[:, 0:2, 0:S], hi[:].bitcast(F32), ALU.subtract).then_inc(s["xnT_lo"], 1)
        dve.wait_ge(s["xnT_lo"], b.n * 3 + 1)
        for dst, src in zip(xt_txt4[b.parity], (hi, lo)):
            dve.tensor_copy(dst[:], src[:, :, L:S].bitcast(F32).unsqueeze(2).broadcast_to([P, 2, 4, LT])).then_inc(s["xnT_lo"], 1)

    def starts(b):
        return b and b.fixed and b.n == 0

    def guard_mix(eng):
        eng.wait_ge(k.h_ready, BATCH)

    def ends(b):
        return b and b.fixed and b.n == BATCH - 1

    def guard_feed(eng):
        eng.wait_ge(s["st_ps"], BATCH * NH)

    def sync(sp):
        sp.wait_ge(k.rn_txt, 2)
        for j in range(4):
            sp.dma_start(k.stat_txt[:].rearrange("p (t j) v -> p j t v", j=4)[:, j],
                         k.txt_rn[LT * j:LT * j + LT]).then_inc(k.stat_moved, 16)

        def step(turn):
            if b := turn.batch(0):
                wait_since(sp, s["xn_ready"], b.n)
                apart(sp, k.passed_sp)
                wait_since(sp, s["txt_loaded"], b.n * 16)
                apart(sp, k.passed_sp)
                sp.dma_start(txt_in[:], io["txt"][bass.ds(b.n * LT, LT), :]).then_inc(s["txt_loaded"], 16)
            if b := turn.batch(4):
                wait_since(sp, s["hb_ready"], b.n)
                apart(sp, k.passed_sp)
                wait_since(sp, s["res_loaded"], b.n * 16)
                apart(sp, k.passed_sp)
                sp.dma_start(txt_res[:], io["txt"][bass.ds(b.n * LT, LT), :]).then_inc(s["res_loaded"], 16)
            if b := turn.batch(3):
                u = b.parity
                sp.wait_ge(s["mT_ready"], b.n + 1)
                sp.dma_start(k.mrow_dram[u].rearrange("r c q -> (r c) q"), mrow[:]).then_inc(s["mrow_stored"], 16)
                sp.wait_ge(s["mrow_stored"], b.n * 16 + 16)
                for t in range(2):
                    sp.dma_start(q_st[u][SR:SR + NPARTS, :, P * t:P * t + P],
                                 k.mrow_dram[u, :, NH * t:NH * t + NH]).then_inc(mrow_loaded[u], 16)
                sp.dma_start(q_st[u][SR:SR + NPARTS, :, L:S],
                             k.mrow_dram[u, :, 2 * NH:].rearrange("r g (j q) -> r (g j) q", j=4)).then_inc(mrow_loaded[u], 16)
            if b := turn.batch(1):
                u = b.parity
                wait_since(sp, stack_loaded[u], b.half * (16 * N_STACK))
                for r, ready in enumerate(("part_h", "part_m", "parts_ready")):
                    apart(sp, k.passed_sp)
                    sp.wait_ge(s[ready], b.n + 1)
                    for x in range(2):
                        sp.dma_start(k.parts_dram[u, x, r].rearrange("d a q -> a d q"),
                                     parts[:, r, x]).then_inc(parts_stored[u], 16)
                apart(sp, k.passed_sp)
                sp.wait_ge(parts_stored[u], (b.half + 1) * (16 * N_STORE))
                apart(sp, k.passed_sp)
                wait_since(sp, s["st_ps"], (b.n - 1) * NH)
                for first, n in ((0, 3), (3, 2), (5, 1)):
                    to = slice(HD * first, HD * (first + n))
                    sp.dma_start(k_st[u][to], k.parts_dram[u, 1, 0:n].rearrange("r d a q -> (r d) (a q)")
                                 ).then_inc(stack_loaded[u], 16)
                    part = k.parts_dram[u, 0, 3 - n].rearrange("d a q -> d (a q)")
                    sp.dma_start(q_st[u][to], part.unsqueeze(0).broadcast_to([n, HD, 8 * 2 * S])
                                 ).then_inc(stack_loaded[u], 16)
            if b := turn.batch(4):
                sp.wait_ge(k.h_done, b.n + 1)
                apart(sp, k.passed_sp)
                sp.dma_start(k.h_txt_dram[bass.ds(b.n * LT, LT), :], h_txt[:]).then_inc(s["h_txt_stored"], 16)
        run_steps(sp, step, 6, BATCH, 4)
        sp.wait_ge(s["h_txt_stored"], BATCH * 16)

    def scalar(act):
        def leave_qk(b):
            for x, base, ps, scale in ((0, 0, "q_ps", HD ** -0.5), (1, 4, "k_ps", 1.0)):
                act.wait_ge(s[ps], b.n + 1)
                if x == 0:
                    if starts(b):
                        guard_mix(act)
                    wait_since(act, s["parts_ready"], b.n)
                for a in range(2):
                    last = act.activation(qk[:, x, a], k.psum[:, base + a, 0:S], ACT.Identity,
                                          bias=k.b_qk[:, x, a:a + 1], scale=scale)
            last.then_inc(s["qk_ready"], 1)
            act.wait_ge(s["qk_ready"], b.n + 1)
            if b.parity:
                act.wait_ge(parts_stored[0], (b.half + 1) * (16 * N_STORE))
            else:
                wait_since(act, parts_stored[1], b.half * (16 * N_STORE))
            act.activation(parts[:, 0].rearrange("p x q -> p (x q)"), qk[:].rearrange("p x a q -> p (x a q)"),
                           ACT.Copy).then_inc(s["part_h"], 1)

        def round_ct(b):
            act.wait_ge(s["ctxT_ps"], b.n + 1)
            wait_since(act, s["o_ps"], b.n)
            act.activation(ct_hi[:], k.psum[:, 2:4, 0:S], ACT.Copy).then_inc(s["ctxT_hi"], 1)

        def exps(b, g):
            if g == 0:
                act.wait_ge(s["stt_ps"], b.n + 1)
                wait_since(act, s["ctx_ps"], b.n * GROUPS)
                act.activation(prob_txt[:].rearrange("p g q -> p (g q)"), k.psum[:, 7, 0:GROUPS * LT],
                               ACT.Exp).then_inc(s["expt_done"], 1)
            wait_since(act, s["ctx_ps"], b.n * GROUPS + (g - 1))
            for j in range(4):
                i = 4 * g + j
                act.wait_ge(s["st_ps"], b.n * NH + (i + 1))
                act.activation(prob[:, i % HSLOTS], k.psum[:, SCORE_BANKS[i % 3], 0:W_KT1 + S], ACT.Exp).then_inc(s["exp_done"], 1)

        def leave_ctx(b, g):
            act.wait_ge(s["ctx_ps"], b.n * GROUPS + (g + 1))
            wait_since(act, s["o1_ps"], b.n)
            act.activation(ctx_u[:, g], k.psum[:, 6, 0:S], ACT.Copy).then_inc(s["ctx_u_done"], 1)

        def step(turn):
            if (b := turn.batch(1)) and not starts(b):
                round_xt(act, b)
            b = turn.batch(4)
            if ends(b):
                guard_feed(act)
                k.feed_first["normalise"](act)
            if b:
                round_ct(b)
            if ends(b):
                k.feed_first["round_xt"](act)
            if b := turn.batch(1):
                leave_qk(b)
            probs_b, next_b = turn.batch(3), turn.batch(0)
            for g in range(GROUPS):
                if probs_b:
                    exps(probs_b, g)
                    if g:
                        leave_ctx(probs_b, g - 1)
            if next_b and not starts(next_b):
                normalise(act, next_b)
            if probs_b:
                leave_ctx(probs_b, GROUPS - 1)
        run_steps(act, step, 6, BATCH, 4)

    def vector(dve):
        for i in range(2):
            dve.memset(v_aug[i][:, :, :, HD:], 1.0).then_inc(s["ones_set"], 1)

        def normalise_ctx(b):
            dve.wait_ge(s["o1_ps"], b.n + 1)
            for t, ps, n in ((0, 4, P), (1, 5, P), (2, 7, LT)):
                src = k.psum[0:n, ps].rearrange("p (h c) -> p h c", c=2 * HD)
                if t == 0:
                    wait_since(dve, s["ctxn_ready"], b.n * 3)
                    wait_since(dve, s["ctxT_ps"], b.n)
                dve.reciprocal(rsum[0:n, t], src[:, :, HD]).then_inc(s["rsum_ready"], 1)
            for t, ps, n in ((0, 4, P), (1, 5, P), (2, 7, LT)):
                src = k.psum[0:n, ps].rearrange("p (a x c) -> p a x c", a=8, x=2)
                dve.wait_ge(s["rsum_ready"], b.n * 3 + (t + 1))
                dve.tensor_tensor(ctx_n[0:n, t].rearrange("p (x a c) -> p a x c", x=2, a=8), src[:, :, :, 0:HD],
                                  rsum[0:n, t].rearrange("p (a x) -> p a x", a=8).unsqueeze(3).broadcast_to([n, 8, 2, HD]),
                                  ALU.mult).then_inc(s["ctxn_ready"], 1)

        def leave_mrow(b):
            dve.wait_ge(s["mT_ps"], b.n + 1)
            wait_since(dve, s["mrow_stored"], b.n * 16)
            dve.tensor_copy(mrow[:], turned_maxima).then_inc(s["mT_ready"], 1)

        def rest_ct(b):
            dve.wait_ge(s["ctxT_hi"], b.n + 1)
            wait_since(dve, s["o_ps"], b.n)
            dve.tensor_tensor(ct_lo[:], k.psum[:, 2:4, 0:S], ct_hi[:].bitcast(F32), ALU.subtract).then_inc(s["ctxT_lo"], 1)

        def leave_v(b):
            dve.wait_ge(s["v_ps"], b.n + 1)
            wait_since(dve, s["ctx_ps"], (b.n - 1) * GROUPS)
            out = v_aug[b.parity]
            bias = k.rows[:, ATT_BV].rearrange("p (h c) -> p h c", h=NH)
            dve.tensor_tensor(out[:, 0:2, :, 0:HD], k.psum[:, 6].rearrange("p (t h c) -> p t h c", t=2, h=NH),
                              bias.unsqueeze(1).broadcast_to([P, 2, NH, HD]), ALU.add)
            dve.tensor_tensor(out[:, 2, :, 0:HD], k.psum[:, 7, 0:D].rearrange("p (h c) -> p h c", h=NH),
                              bias, ALU.add).then_inc(s["v_ready"], 1)

        def split3(b, half):
            flat = lambda t: t[:].rearrange("p x a q -> p (x a q)")
            part = lambda i: parts[:, i].rearrange("p x q -> p (x q)")
            if half == 0:
                dve.wait_ge(s["part_h"], b.n + 1)
                wait_since(dve, s["parts_ready"], b.n)
                dve.tensor_tensor(flat(qk_rest), flat(qk), part(0), ALU.subtract).then_inc(s["rest_h"], 1)
            else:
                dve.wait_ge(s["rest_h"], b.n + 1)
                dve.tensor_copy(part(1), flat(qk_rest)).then_inc(s["part_m"], 1)
                dve.wait_ge(s["part_m"], b.n + 1)
                dve.tensor_tensor(part(2), flat(qk_rest), part(1), ALU.subtract).then_inc(s["parts_ready"], 1)

        def add_residual(b):
            dve.wait_ge(s["o_ps"], b.n + 1)
            dve.wait_ge(s["hb_ready"], b.n + 1)
            wait_since(dve, s["h_txt_stored"], b.n * 16)
            dve.tensor_tensor(k.h_all[:, bass.ds(b.n * 2, 2), :], k.psum[:, 2].rearrange("p (t d) -> p t d", t=2),
                              hb[:], ALU.add)
            dve.tensor_tensor(h_txt[:], k.psum[0:LT, 3, 0:D], hb_txt[:], ALU.add).then_inc(k.h_done, 1)

        def maxima(b, g):
            if g == 0:
                wait_since(dve, s["mp_ready"], b.n)
            dve.wait_ge(s["m0_ps"], b.n * GROUPS + (g + 1))
            dve.tensor_reduce(nmax[:, 4 * g:4 * g + 4], k.psum[:, 0].rearrange("p (h c) -> p h c", h=4), AX_X, ALU.max,
                              negate=True).then_inc(s["m0_max"], 1)
            dve.wait_ge(s["m1_ps"], b.n * GROUPS + (g + 1))
            dve.tensor_reduce(nmax[:, NH + 4 * g:NH + 4 * g + 4], k.psum[:, 1:3].rearrange("p t (h c) -> p (t h) c", h=2),
                              AX_X, ALU.max, negate=True).then_inc(s["m1_max"], 1)
            dve.wait_ge(s["mt_ps"], b.n * GROUPS + (g + 1))
            dve.tensor_reduce(nmax[:, 2 * NH + g:2 * NH + g + 1], k.psum[:, 3, 0:S], AX_X, ALU.max,
                              negate=True).then_inc(s["mt_max"], 1)

        def split_maxima(b):
            n = b.n
            dve.wait_ge(s["mt_max"], n * GROUPS + GROUPS)
            wait_since(dve, s["mT_ps"], n)
            dve.tensor_copy(mparts[:, 0], nmax[:]).then_inc(s["mp_h"], 1)
            dve.wait_ge(s["mp_h"], n + 1)
            dve.tensor_tensor(nmax_rest[:], nmax[:], mparts[:, 0], ALU.subtract).then_inc(s["mr_h"], 1)
            dve.wait_ge(s["mr_h"], n + 1)
            dve.tensor_copy(mparts[:, 1], nmax_rest[:]).then_inc(s["mp_m"], 1)
            dve.wait_ge(s["mp_m"], n + 1)
            dve.tensor_tensor(mparts[:, 2], nmax_rest[:], mparts[:, 1], ALU.subtract).then_inc(s["mp_ready"], 1)

        def limit_txt(b):
            dve.wait_ge(s["expt_done"], b.n + 1)
            dve.tensor_tensor(prob_txt[:], prob_txt[:], k.keep_txt[:].unsqueeze(1).broadcast_to([P, GROUPS, LT]),
                              ALU.min).then_inc(s["keep_done"], 1)

        def step(turn):
            own_b, max_b, probs_b, out_b = (turn.batch(lag) for lag in (1, 2, 3, 4))
            if probs_b:
                leave_mrow(probs_b)
            if own_b and not starts(own_b):
                rest_xt(dve, own_b)
            if ends(out_b):
                guard_feed(dve)
                k.feed_first["stats"](dve)
            if out_b:
                normalise_ctx(out_b)
                rest_ct(out_b)
            if ends(out_b):
                k.feed_first["rest_xt"](dve)
            if max_b:
                leave_v(max_b)
            if (next_b := turn.batch(0)) and not starts(next_b):
                stats(dve, next_b)
            if out_b:
                add_residual(out_b)
            if probs_b:
                limit_txt(probs_b)
            for g in range(GROUPS):
                if max_b:
                    maxima(max_b, g)
                if g < 2 and own_b:
                    split3(own_b, g)
            if max_b:
                split_maxima(max_b)
        run_steps(dve, step, 6, BATCH, 4)

    def tensor(pe):
        pe.wait_ge(k.split_lo, 7)

        w = lambda i, a, half: [v[:, i, a, P * half:P * half + P] for v in k.w_att]

        def turn_maxima(b):
            pe.wait_ge(s["mp_ready"], b.n + 1)
            pe.transpose(turned_maxima, mparts[:].rearrange("p r c -> p (r c)"),
                         k.ident_bf[:]).then_inc(s["mT_ps"], 1)

        def turn_ctx(b):
            pe.wait_ge(s["ctx_u_done"], b.n * GROUPS + GROUPS)
            pe.wait_ge(s["exp_done"], b.n * NH + NH)
            pe.wait_ge(s["expt_done"], b.n + 1)
            for t, ps, n in ((0, 4, P), (1, 5, P), (2, 7, LT)):
                for g in range(GROUPS):
                    last = pe.transpose(k.psum[0:n, ps, P * g:P * g + P], ctx_u[:, g, P * t:P * t + n], k.ident[:])
            last.then_inc(s["o1_ps"], 1)

        def turn_xn(b):
            pe.wait_ge(s["xn_ready"], b.n + 1)
            wait_since(pe, s["m1_max"], (b.n - 1) * GROUPS)
            for a in range(2):
                for t, n in ((0, P), (1, P), (2, LT)):
                    last = pe.transpose(k.psum[:, a, P * t:P * t + n], xn[0:n, t, P * a:P * a + P], k.ident[0:n, 0:n])
            last.then_inc(s["xnT_ps"], 1)

        def turn_ctxn(b):
            pe.wait_ge(s["ctxn_ready"], b.n * 3 + 3)
            if b.fixed and b.n >= BATCH - 1:
                pe.wait_ge(s["mt_max"], BATCH * GROUPS)
            else:
                pe.wait_ge(s["mt_max"], (b.n + 2) * GROUPS)
            for a in range(2):
                for t, n in ((0, P), (1, P), (2, LT)):
                    last = pe.transpose(k.psum[:, 2 + a, P * t:P * t + n], ctx_n[0:n, t, P * a:P * a + P], k.ident[0:n, 0:n])
            last.then_inc(s["ctxT_ps"], 1)

        def project_qk(b, x):
            xt = (xt_hi[b.parity], xt_lo[b.parity])
            if x == 0:
                pe.wait_ge(s["xnT_lo"], b.n * 3 + 1)
            else:
                wait_since(pe, s["ctxn_ready"], (b.n - 2) * 3)
            for half in range(2):
                for a in range(2):
                    last = split_product(pe, k.psum[:, 4 * x + half, 0:S], w(x, a, half), [v[:, a] for v in xt],
                                         start=a == 0, stop=a == 1)
            last.then_inc(s[("q_ps", "k_ps")[x]], 1)

        def project_v(b):
            xt = (xt_hi[b.parity], xt_lo[b.parity])
            wait_since(pe, s["ctx_u_done"], (b.n - 1) * GROUPS)
            for t in range(2):
                for a in range(2):
                    split_product(pe, k.psum[:, 6, D * t:D * t + D], [v[:, a, P * t:P * t + P] for v in xt],
                                  [v[:, 2, a] for v in k.w_att], start=a == 0, stop=a == 1)

        def project_v_txt(b):
            wait_since(pe, s["ctxn_ready"], (b.n - 1) * 3)
            pe.wait_ge(s["xnT_lo"], b.n * 3 + 3)
            for a in range(2):
                last = split_product(pe, k.psum[:, 7, 0:D], [v[:, a].rearrange("p r q -> p (r q)") for v in xt_txt4[b.parity]],
                                     [v[:, 2, a] for v in k.w_att], start=a == 0, stop=a == 1)
            last.then_inc(s["v_ps"], 1)

        def project_out(b):
            ct = (ct_hi, ct_lo)
            pe.wait_ge(s["ctxT_lo"], b.n + 1)
            for t, ps, n in ((0, 2, P), (1, 2, P), (2, 3, LT)):
                out = k.psum[0:n, ps, D * (t % 2):D * (t % 2) + D]
                for a in range(2):
                    last = split_product(pe, out, [v[:, a, P * t:P * t + n] for v in ct],
                                         [v[:, 3, a] for v in k.w_att], start=a == 0, stop=a == 1)
            last.then_inc(s["o_ps"], 1)

        def scores_for_max(b, g, which):
            q, kk = q_st[b.parity], k_st[b.parity]
            heads = range(4 * g, 4 * g + 4)
            if which == 0:
                if g == 0:
                    pe.wait_ge(stack_loaded[b.parity], (b.half + 1) * (16 * N_STACK))
                    pe.wait_ge(s["qk_ready"], BATCH if b.fixed and b.n == BATCH - 1 else b.n + 2)
                wait_since(pe, s["m0_max"], b.n * GROUPS + g)
                pe.matmul(bank(0), k.ident_bf[:], k.mask_q[:], start=True, stop=False, skip_group_check=True)
                for j, h in enumerate(heads):
                    last = pe.matmul(k.psum[:, 0, P * j:P * j + P], q[0:SR, h, 0:P], kk[0:SR, h, 0:P], start=False,
                                     stop=True, skip_group_check=True)
                last.then_inc(s["m0_ps"], 1)
            elif which == 1:
                if g == 0:
                    wait_since(pe, k.h_done, b.n - 1)
                wait_since(pe, s["m1_max"], b.n * GROUPS + g)
                for c in range(2):
                    pe.matmul(k.psum[:, 1 + c].rearrange("p (h c) -> p h c", h=2)[:, :, P:L], k.ident_bf[:],
                              k.mask_q[:, 0:L].rearrange("p (h c) -> p h c", h=2), start=True, stop=False,
                              skip_group_check=True)
                    for j in range(2):
                        h = heads[2 * c + j]
                        last = pe.matmul(k.psum[:, 1 + c, L * j:L * j + L], q[0:SR, h, P:L], kk[0:SR, h, 0:L], start=False,
                                         stop=True, skip_group_check=True)
                last.then_inc(s["m1_ps"], 1)
            else:
                wait_since(pe, s["mt_max"], b.n * GROUPS + g)
                pe.matmul(k.psum[:, 3, L:S], k.ident_bf[:], k.mask_txt[:], start=True, stop=False, skip_group_check=True)
                for j, h in enumerate(heads):
                    last = pe.matmul(k.psum[LT * j:LT * j + LT, 3, 0:S], q[0:SR, h, L:S], kk[0:SR, h, 0:S], start=False,
                                     stop=True, skip_group_check=True)
                last.then_inc(s["mt_ps"], 1)

        def scores_transposed(b, pair):
            q, kk = q_st[b.parity], k_st[b.parity]
            rows = slice(0, SR + NPARTS)
            if pair == 0:
                if b.fixed and b.n == 0:
                    pe.wait_ge(s["ones_set"], 4)
                pe.wait_ge(mrow_loaded[b.parity], (b.half + 1) * 48)
                pe.wait_ge(s["v_ready"], min(b.n + 2, BATCH) if b.fixed else b.n + 2)
                pe.wait_ge(s["qk_ready"], min(b.n + 3, BATCH) if b.fixed else b.n + 3)
                for h in range(NH):
                    j = h % 4
                    last = pe.matmul(k.psum[LT * j:LT * j + LT, 7, LT * (h // 4):LT * (h // 4) + LT],
                                     kk[rows, h, L:S], q[rows, h, L:S], start=True, stop=True)
                last.then_inc(s["stt_ps"], 1)
            for h in (2 * pair, 2 * pair + 1):
                out = k.psum[:, SCORE_BANKS[h % 3]]
                if h == 2:
                    pe.wait_ge(s["expt_done"], b.n + 1)
                if h > 2:
                    pe.wait_ge(s["exp_done"], b.n * NH + (h - 2))
                pe.matmul(out[:, 0:W_KT1], kk[rows, h, P:L], q[rows, h, P:S], start=True, stop=True)
                pe.matmul(out[:, W_KT1:W_KT1 + S], kk[rows, h, 0:P], q[rows, h, 0:S], start=True,
                          stop=True).then_inc(s["st_ps"], 1)

        def weigh_values(b, g):
            v = v_aug[b.parity]
            pe.wait_ge(s["seen"], b.n * NH + (4 * g + 4))
            wait_since(pe, s["ctx_u_done"], b.n * GROUPS + g)
            pe.wait_ge(s["keep_done"], b.n + 1)
            for j in range(4):
                h = 4 * g + j
                pe.matmul(k.psum[LT * j:LT * j + LT, 6, 0:S], v[:, 0, head[h]], prob[:, h % HSLOTS, W_KT1:], start=True,
                          stop=False)
            for j in range(4):
                h = 4 * g + j
                pe.matmul(k.psum[LT * j:LT * j + LT, 6, P:S], v[:, 1, head[h]], prob[:, h % HSLOTS, 0:W_KT1], start=False,
                          stop=False)
            for j in range(4):
                h = 4 * g + j
                last = pe.matmul(k.psum[LT * j:LT * j + LT, 6, L:S], v[LT * j:LT * j + LT, 2, head[h]],
                                 prob_txt[LT * j:LT * j + LT, g], start=False, stop=True)
            last.then_inc(s["ctx_ps"], 1)

        def step(turn):
            own_b, max_b, probs_b, out_b = (turn.batch(lag) for lag in (1, 2, 3, 4))
            if starts(own_b):
                pe.wait_ge(k.ekv_ready, BATCH)
                pe.wait_ge(k.eq_ready, BATCH)
            if own_b:
                turn_xn(own_b)
            if probs_b:
                turn_maxima(probs_b)
            if out_b:
                turn_ctx(out_b)
            if max_b:
                project_v(max_b)
            if own_b:
                project_qk(own_b, 0)
            if max_b:
                project_v_txt(max_b)
            if out_b:
                turn_ctxn(out_b)
            if ends(out_b):
                pe.wait_ge(s["m1_max"], BATCH * GROUPS)
                k.feed_first["turn_xn"](pe)
            if starts(own_b):
                pe.wait_ge(k.y_ready, BATCH)
                pe.wait_ge(k.h1_ready, BATCH)
            if own_b:
                project_qk(own_b, 1)
            if out_b:
                project_out(out_b)
            for part in ORDER:
                what, i = part[0], int(part[1:])
                if what == "s" and probs_b:
                    scores_transposed(probs_b, i)
                if what == "v" and probs_b:
                    weigh_values(probs_b, i)
                if what == "m" and max_b:
                    scores_for_max(max_b, i // 3, i % 3)
        run_steps(pe, step, 6, BATCH, 4)

    def gpsimd(pool):
        guard_mix(pool)
        def set_ones():
            pool.wait_ge(s["rn_ready"], 2)
            for i in range(2):
                if i:
                    pool.wait_ge(s["ones_set"], 3)
                pool.memset(k_st[i][SR:SR + NPARTS], 1.0).then_inc(s["ones_set"], 1)
            pool.wait_ge(s["ones_set"], 4)

        def step(turn):
            if b := turn.batch(4):
                pool.wait_ge(s["res_loaded"], b.n * 16 + 16)
                wait_since(pool, k.h_done, b.n)
                pool.tensor_tensor(hb[:], k.h_all[:, bass.ds(b.n * 2, 2), :],
                                   k.rows[:, ATT_BO].unsqueeze(1).broadcast_to([P, 2, D]), ALU.add)
                pool.tensor_tensor(hb_txt[:], txt_res[:], k.rows[0:LT, ATT_BO], ALU.add).then_inc(s["hb_ready"], 1)
                if ends(b):
                    guard_feed(pool)
                    k.feed_first["moments"](pool)
            next_b = turn.batch(0)
            if next_b and not starts(next_b) and not turn.batch(3):
                moments(pool, next_b)
            if turn.is_step(1):
                set_ones()
            if b := turn.batch(3):
                for h in range(NH):
                    if h == NH // 2 and next_b and not starts(next_b):
                        moments(pool, next_b)
                    pool.wait_ge(s["exp_done"], b.n * NH + (h + 1))
                    apart(pool, k.passed_pool)
                    v = prob[:, h % HSLOTS, 0:2 * W_KT1].rearrange("p (t q) -> p t q", t=2)[:, :, 0:P]
                    pool.affine_select(out=v, in_=v, compare_op=ALU.is_ge, fill=0.0, base=0, pattern=[[0, 2], [1, P]],
                                       channel_multiplier=-1).then_inc(s["seen"], 1)
        run_steps(pool, step, 6, BATCH, 4)

    first = Batch(0, 0, 0)
    k.attend_first = {"stats": lambda dve: stats(dve, first), "moments": lambda pool: moments(pool, first),
                      "normalise": lambda act: normalise(act, first),
                      "round_xt": lambda act: round_xt(act, first), "rest_xt": lambda dve: rest_xt(dve, first)}
    return {"sync": sync, "scalar": scalar, "vector": vector, "tensor": tensor, "gpsimd": gpsimd}


ORDER = "s0 m0 s1 m1 m2 s2 m3 s3 v0 m4 m5 s4 m6 s5 v1 m7 s6 m8 s7 m9 v2 m10 m11 v3".split()


STATS_AT, NORMALISE_AT, TURN_AT = 1, 3, 5


def feed_forward(nc, k, own):
    sb, sem, io = lambda n, s, d=F32: k.sb(n, s, d, own), k.sem, k.io
    T = FF_TOK // P
    st = sb("ff_st", [P, T, 6])
    mv = sb("ff_mv", [P, T, 2])
    ve = sb("ff_ve", [P, T])
    rn = sb("ff_rn", [P, T, 2])
    xn = sb("ff_xn", [P, T, D])
    xt = [[sb(f"ff_xt_{x}{i}", [P, 2, FF_TOK], F32R) for x in ("hi", "lo")] for i in range(2)]
    g = sb("ff_g", [P, 2, FF_TOK])
    g_hi = sb("ff_g_hi", [P, 2, FF_TOK], F32R)
    g_lo = sb("ff_g_lo", [P, 2, FF_TOK], F32R)
    hb = sb("ff_hb", [P, 2, T, D])
    out = sb("ff_out", [P, 2, T, D])
    names = ("txt_in st_ready mv_ready ve_ready rstd_ready rn_ready xn_ready xnT_ps xnT_hi xnT_lo u_ps g_ready g_hi g_lo "
             "y_ps hb_ready out_ready").split()
    s = {n: sem("ff_" + n) for n in names}
    stored = [sem(f"ff_stored{i}") for i in range(2)]
    XT, UB, YB = (0, 1), (4, 5), ((6, 7), (2, 3))

    def stats(dve, b):
        if b.fixed and b.n == 2:
            dve.wait_ge(s["txt_in"], 16)
        wait_since(dve, s["mv_ready"], b.n * T)
        for t in range(T):
            dve.bn_stats(st[:, t], k.h_all[:, bass.ds(b.n * T + t, 1), :].rearrange("p o d -> p (o d)")).then_inc(s["st_ready"], 1)
        dve.wait_ge(s["st_ready"], b.n * T + T)
        wait_since(dve, s["rn_ready"], b.n)
        apart(dve, k.passed_dve)
        for t in range(T):
            dve.bn_aggr(mv[:, t], st[:, t]).then_inc(s["mv_ready"], 1)

    def rest_xt(dve, b):
        for a in range(2):
            dve.wait_ge(s["xnT_hi"], b.n * 2 + (a + 1))
            wait_since(dve, s["u_ps"], (b.n - 1) * 8)
            dve.tensor_tensor(xt[b.parity][1][:, a], k.psum[:, XT[a]], xt[b.parity][0][:, a].bitcast(F32),
                              ALU.subtract).then_inc(s["xnT_lo"], 1)

    def normalise(act, b):
        act.wait_ge(s["rn_ready"], b.n + 1)
        wait_since(act, s["xnT_ps"], b.n)
        for t in range(T):
            last = act.activation(xn[:, t], k.h_all[:, bass.ds(b.n * T + t, 1), :].rearrange("p o d -> p (o d)"),
                                  ACT.Identity, bias=rn[:, t, 1:2], scale=rn[:, t, 0:1])
        last.then_inc(s["xn_ready"], 1)

    def round_xt(act, b):
        for a in range(2):
            act.wait_ge(s["xnT_ps"], b.n + 1)
            wait_since(act, s["u_ps"], (b.n - 1) * 8)
            act.activation(xt[b.parity][0][:, a], k.psum[:, XT[a]], ACT.Copy).then_inc(s["xnT_hi"], 1)

    def turn_xn(pe, b):
        pe.wait_ge(s["xn_ready"], b.n + 1)
        wait_since(pe, s["xnT_lo"], b.n * 2)
        for a in range(2):
            for t in range(T):
                last = pe.transpose(k.psum[:, XT[a], P * t:P * t + P], xn[:, t, P * a:P * a + P], k.ident[:])
        last.then_inc(s["xnT_ps"], 1)

    def moments(pool, b):
        pool.wait_ge(s["mv_ready"], b.n * T + T)
        wait_since(pool, s["xn_ready"], b.n)
        apart(pool, k.passed_pool)
        pool.tensor_scalar(ve[:], mv[:, :, 1], 1.0, EPS, ALU.mult, ALU.add).then_inc(s["ve_ready"], 1)
        pool.tensor_scalar(rn[:, :, 1], mv[:, :, 0], -1.0, 0.0, ALU.mult, ALU.add)
        pool.wait_ge(s["ve_ready"], b.n + 1)
        pool.tensor_tensor(rn[:, :, 0], ve[:], k.half_neg[:, 0:T], ALU.pow).then_inc(s["rstd_ready"], 1)
        pool.wait_ge(s["rstd_ready"], b.n + 1)
        pool.tensor_tensor(rn[:, :, 1], rn[:, :, 1], rn[:, :, 0], ALU.mult).then_inc(s["rn_ready"], 1)
        if b.fixed and b.n == 2:
            pool.wait_ge(s["txt_in"], 16)
        wait_since(pool, s["out_ready"], b.n - 1)
        pool.tensor_tensor(hb[:, b.parity], k.h_all[:, bass.ds(b.n * T, T), :],
                           k.rows[:, FF_B].unsqueeze(1).broadcast_to([P, T, D]), ALU.add).then_inc(s["hb_ready"], 1)

    def sync(sp):
        sp.dma_start(k.h_all[:, IMG_TILES:], k.h_txt_dram.rearrange("(t p) d -> p t d", p=P)).then_inc(s["txt_in"], 16)

        def step(turn):
            if b := turn.batch(1):
                sp.wait_ge(s["out_ready"], b.n + 1)
                u = b.parity
                if b.fixed and b.n == FF_STEPS - 1:
                    for t in range(T):
                        for j in range(4):
                            sp.dma_start(io["out"][4 * t + j, L:S], out[LT * j:LT * j + LT, u, t]).then_inc(stored[u], 16)
                else:
                    apart(sp, k.passed_sp)
                    for j in range(2):
                        dst = io["out"][bass.ds(b.n * 2 + j, 1), 0:L].rearrange("o (t p) d -> p (o t) d", p=P)
                        sp.dma_start(dst, out[:, u, 2 * j:2 * j + 2]).then_inc(stored[u], 16)
        run_steps(sp, step, 5, FF_STEPS, 1, first=1)
        sp.wait_ge(stored[1], 16 * 2 * 4)
        sp.wait_ge(stored[0], 16 * (2 * 4 + 16))

    def scalar(act):
        def step(turn):
            next_b, b = turn.batch(0), turn.batch(1)
            for c in range(8):
                if b:
                    act.wait_ge(s["u_ps"], b.n * 8 + (c + 1))
                    wait_since(act, s["g_lo"], b.n * 8 + (c - 1))
                    act.activation(g[:, c % 2], k.psum[:, UB[c % 2]], ACT.Gelu, bias=k.b_gelu[:, c:c + 1]).then_inc(s["g_ready"], 1)
                if c == NORMALISE_AT and next_b:
                    normalise(act, next_b)
                if c == TURN_AT and next_b:
                    round_xt(act, next_b)
        run_steps(act, step, 5, FF_STEPS, 1, first=1)

    def vector(dve):
        def leave(b):
            dve.wait_ge(s["y_ps"], b.n * 8 + 8)
            dve.wait_ge(s["hb_ready"], b.n + 1)
            if b.parity:
                wait_since(dve, stored[1], b.half * 32)
            else:
                wait_since(dve, stored[0], b.half * 32)
            for c in range(2):
                last = dve.tensor_tensor(out[:, b.parity, 2 * c:2 * c + 2], k.psum[:, YB[b.parity][c]].rearrange("p (t d) -> p t d", t=2),
                                         hb[:, b.parity, 2 * c:2 * c + 2], ALU.add)
            last.then_inc(s["out_ready"], 1)

        def step(turn):
            next_b, b, last_b = turn.batch(0), turn.batch(1), turn.batch(2)
            for c in range(8):
                if b:
                    dve.wait_ge(s["g_ready"], b.n * 8 + (c + 1))
                    wait_since(dve, s["y_ps"], b.n * 8 + (c - 1))
                    dve.tensor_scalar(g_hi[:, c % 2], g[:, c % 2], 1.0, None, ALU.mult).then_inc(s["g_hi"], 1)
                    dve.wait_ge(s["g_hi"], b.n * 8 + (c + 1))
                    dve.tensor_tensor(g_lo[:, c % 2], g[:, c % 2], g_hi[:, c % 2].bitcast(F32), ALU.subtract).then_inc(s["g_lo"], 1)
                if c == 0 and last_b:
                    leave(last_b)
                if c == STATS_AT and next_b:
                    stats(dve, next_b)
                if c == TURN_AT and next_b:
                    rest_xt(dve, next_b)
        run_steps(dve, step, 5, FF_STEPS, 2, first=1)

    def tensor(pe):
        def down(b, c):
            pe.wait_ge(s["g_lo"], b.n * 8 + (c + 1))
            if c == 0:
                wait_since(pe, s["out_ready"], b.n - 1)
                if b.fixed and b.n == 1:
                    pe.wait_ge(k.h_done, BATCH)
            for t in range(T):
                first = c == 0 and t % 2 == 0
                last = split_product(pe, k.psum[:, YB[b.parity][t // 2], D * (t % 2):D * (t % 2) + D],
                                     [v[:, c % 2, P * t:P * t + P] for v in (g_hi, g_lo)], [v[:, c] for v in k.w_dn],
                                     start=first, stop=c == 7, check=True)
            last.then_inc(s["y_ps"], 1)

        def up(b, c):
            x = xt[b.parity]
            wait_since(pe, s["g_ready"], b.n * 8 + (c - 1))
            for a in range(2):
                last = split_product(pe, k.psum[:, UB[c % 2]], [w[:, a, c] for w in k.w_up], [v[:, a] for v in x],
                                     start=a == 0, stop=a == 1)
            last.then_inc(s["u_ps"], 1)

        def step(turn):
            next_b, b, last_b = turn.batch(0), turn.batch(1), turn.batch(2)
            if b:
                pe.wait_ge(s["xnT_lo"], b.n * 2 + 2)
            for c in range(8):
                if b:
                    up(b, c)
                    if c:
                        down(b, c - 1)
                if c == 0 and last_b:
                    down(last_b, 7)
                if c == TURN_AT and next_b:
                    turn_xn(pe, next_b)
        run_steps(pe, step, 5, FF_STEPS, 2, first=1)

    def gpsimd(pool):
        def step(turn):
            if b := turn.batch(0):
                moments(pool, b)
        run_steps(pool, step, 5, FF_STEPS, 1, first=1)

    first = Batch(0, 0, 0)
    k.feed_first = {"stats": lambda dve: stats(dve, first), "rest_xt": lambda dve: rest_xt(dve, first),
                    "normalise": lambda act: normalise(act, first), "round_xt": lambda act: round_xt(act, first),
                    "turn_xn": lambda pe: turn_xn(pe, first), "moments": lambda pool: moments(pool, first)}
    return {"sync": sync, "scalar": scalar, "vector": vector, "tensor": tensor, "gpsimd": gpsimd}


def stage_weight(weights, s, unit_out, unit_in):
    pair = ((unit_out >> (s + 1)) << s) | (unit_out & ((1 << s) - 1))
    return weights[s][pair, (unit_out >> s) & 1, (unit_in >> s) & 1]


def block_coefficients(weights, transposed):
    unit = np.arange(8)[None, :] * P + np.arange(P)[:, None]
    out = np.empty((P, STAGES - IN_BLOCK, 8, 2), weights.dtype)
    for s in range(IN_BLOCK, STAGES):
        other = unit ^ (1 << s)
        out[:, s - IN_BLOCK, :, 0] = stage_weight(weights, s, unit, unit)
        out[:, s - IN_BLOCK, :, 1] = stage_weight(weights, s, other, unit) if transposed else stage_weight(weights, s, unit, other)
    return out


def path_table(weights, inputs_free):
    out = np.empty((P, PATHS), weights.dtype)
    p, f = np.arange(P)[:, None, None], np.arange(8)[None, :, None] * P
    for s in range(IN_BLOCK):
        at, n = stage_columns(s, inputs_free)
        free = np.arange(n)[None, None, :]
        low = (1 << s) - 1
        output, inp = (p, free << s) if inputs_free else (free, p)
        before = f + ((inp & ~low) | (output & low))
        after = (before & ~(1 << s)) | (output & (1 << s))
        out[:, at:at + 8 * n] = stage_weight(weights, s, after, before).reshape(P, 8 * n)
    return out


def kernel(x, txt, L0_tok_Wq_w, L0_tok_Wq_b, L0_tok_Wk_w, L0_tok_Wk_b, L0_tok_Wv_w, L0_tok_Wv_b, L0_tok_w_bias,
           L0_tok_out_w, L0_tok_out_b, L0_tok_ln_g, L0_tok_ln_b, L0_tok_local_mask, L0_attn_Wq, L0_attn_bq, L0_attn_Wk,
           L0_attn_bk, L0_attn_Wv, L0_attn_bv, L0_attn_Wo, L0_attn_bo, L0_ffn_W_exp, L0_ffn_b_exp, L0_ffn_up_weights,
           L0_ffn_up_bias, L0_ffn_down_weights, L0_ffn_W_con, L0_ffn_b_con, L0_ffn_down_bias):
    import concourse.bacc as bacc
    from concourse.bass_utils import run_bass_kernel_spmd

    a = np.asarray
    x = a(x)
    arrays = {
        "x": x.reshape(BATCH, C, L, 2, 2).transpose(0, 4, 1, 3, 2).reshape(BATCH, P, 2 * L),
        "xt": x.transpose(0, 2, 3, 1).reshape(BATCH, L, D),
        "txt": a(txt).reshape(BATCH * LT, D),
        "w_tok": np.stack([a(w).T for w in (L0_tok_Wq_w, L0_tok_Wk_w, L0_tok_Wv_w)]),
        "b_tok_rows": np.stack([np.tile(a(b), 4) for b in (L0_tok_Wq_b, L0_tok_Wk_b, L0_tok_Wv_b)]),
        "b_tok_q": np.tile(a(L0_tok_Wq_b), 2).reshape(P, 1),
        "ew": a(L0_tok_w_bias).T,
        "mask": np.ascontiguousarray(a(L0_tok_local_mask).T).view(np.uint32),
        "w_out": a(L0_tok_out_w),
        "rows": np.stack([a(v) for v in (L0_tok_out_b, L0_tok_ln_g, L0_tok_ln_b, L0_attn_bv, L0_attn_bo, L0_ffn_b_con,
                                         L0_ffn_down_bias)]),
        "w_att": np.stack([a(v) for v in (L0_attn_Wq, L0_attn_Wk, L0_attn_Wv, L0_attn_Wo)]),
        "b_qk": np.stack([a(v).reshape(2, P) for v in (L0_attn_bq, L0_attn_bk)]).transpose(2, 0, 1),
        "w_exp": np.concatenate([a(L0_ffn_W_exp).T, a(L0_ffn_b_exp)[:, None]], axis=1),
        "w_con": a(L0_ffn_W_con),
        "coef_up": block_coefficients(a(L0_ffn_up_weights), False),
        "coef_dn": block_coefficients(a(L0_ffn_down_weights), True),
        "table_up": path_table(a(L0_ffn_up_weights), False),
        "table_dn": path_table(a(L0_ffn_down_weights), True),
        "up_bias": a(L0_ffn_up_bias).reshape(8, P).T,
    }
    nc = bacc.Bacc("TRN2", target_bir_lowering=False, num_devices=1)
    io, feeds = {}, {}
    for name, v in arrays.items():
        v = np.ascontiguousarray(v)
        feeds[f"in_{name}"] = v
        io[name] = nc.dram_tensor(f"in_{name}", v.shape, mybir.dt.from_np(v.dtype), kind="ExternalInput").ap()
    io["out"] = nc.dram_tensor("out_h", (BATCH, S, D), F32, kind="ExternalOutput").ap()
    build(nc, io)
    return run_bass_kernel_spmd(nc, [feeds], core_ids=[0]).results[0]["out_h"]
```
